# Optimizing a Trainium2 kernel written in Bass

```python
import numpy as np
import jax
import jax.numpy as jnp

def _softmax(x, axis=-1):
    return jax.nn.softmax(x, axis=axis)
def _gelu(x):
    return jax.nn.gelu(x, approximate=True)
def _silu(x):
    return jax.nn.silu(x)
def _sigmoid(x):
    return jax.nn.sigmoid(x)
def _layernorm(x, axis=-1, eps=1e-5):
    m = jnp.mean(x, axis=axis, keepdims=True)
    v = jnp.var(x, axis=axis, keepdims=True)
    return (x - m) / jnp.sqrt(v + eps)
def _scatter_add(tgt, idx, src, axis=0):
    return tgt.at[idx].add(src)
def _segment_sum(src, seg, n):
    return jax.ops.segment_sum(src, seg, n)

kernel_name = 'mk_conv_attn_hybrid_d2_conv_nhwc384_0b9d5f'

def setup_inputs(seed: int = 0):
    np.random.seed(seed)
    _w = jnp.asarray
    def _rec_inputs():
        import jax
        import jax.numpy as jnp
        _gk = jax.random.key(seed)
        x = -0.0005963 + 1.001 * jax.random.normal(jax.random.fold_in(_gk, 1), (8, 32, 32, 384), jnp.float32)
        return x
    x = _rec_inputs()
    def _L0_conv_setup():
        import jax, jax.numpy as jnp
        import numpy as np
        B, H, W, C = (8, 32, 32, 384)
        NH, HD = (6, 64)
        SCALE = HD ** (-0.5)

        def _get_rel_pos(rel_pos, q_size, k_size):
            coords = jnp.arange(q_size)[:, None] - jnp.arange(k_size)[None, :] + (k_size - 1)
            return rel_pos[coords]
        key = jax.random.key(seed)
        ks = jax.random.split(key, 7)
        return {'x': jax.random.normal(ks[0], (B, H, W, C), jnp.float32), 'qkv_w': jax.random.normal(ks[1], (C, 3 * C), jnp.float32) * 0.02, 'qkv_b': jax.random.normal(ks[2], (3 * C,), jnp.float32) * 0.02, 'proj_w': jax.random.normal(ks[3], (C, C), jnp.float32) * 0.02, 'proj_b': jax.random.normal(ks[4], (C,), jnp.float32) * 0.02, 'rel_pos_h': jax.random.normal(ks[5], (2 * H - 1, HD), jnp.float32) * 0.02, 'rel_pos_w': jax.random.normal(ks[6], (2 * W - 1, HD), jnp.float32) * 0.02}
    _L0_conv_all = _L0_conv_setup()
    _L0_conv_in = {k: v for k, v in _L0_conv_all.items() if k in ('qkv_w', 'qkv_b', 'proj_w', 'proj_b', 'rel_pos_h', 'rel_pos_w', )}
    del _L0_conv_all

    def _L1_attn_setup():
        import jax, jax.numpy as jnp
        import numpy as np
        B, S, E, H = (8, 2048, 384, 6)
        D = E // H
        key = jax.random.key(seed)
        ks = jax.random.split(key, 5)
        s = 1.0 / np.sqrt(E)
        return {'x': jax.random.normal(ks[0], (B, S, E), dtype=jnp.float32), 'Wq': jax.random.normal(ks[1], (E, E), dtype=jnp.float32) * s, 'Wk': jax.random.normal(ks[2], (E, E), dtype=jnp.float32) * s, 'Wv': jax.random.normal(ks[3], (E, E), dtype=jnp.float32) * s, 'Wo': jax.random.normal(ks[4], (E, E), dtype=jnp.float32) * s, 'bo': jnp.zeros((E,), dtype=jnp.float32)}
    _L1_attn_all = _L1_attn_setup()
    _L1_attn_in = {k: v for k, v in _L1_attn_all.items() if k in ('Wq', 'Wk', 'Wv', 'Wo', 'bo', )}
    del _L1_attn_all

    def _L1_ffn_setup():
        import jax, jax.numpy as jnp
        import numpy as np
        D_MODEL = 384
        D_FF = 1536
        key = jax.random.key(seed)
        k_x, k1, k2, k3, k4 = jax.random.split(key, 5)
        std = 0.02
        return {'x': jax.random.normal(k_x, (16, 2048, D_MODEL), dtype=jnp.float32), 'c_fc_1': std * jax.random.normal(k1, (1536, 32), dtype=jnp.float32), 'c_fc_2': std * jax.random.normal(k2, (1, 12), dtype=jnp.float32), 'c_proj_1': std * jax.random.normal(k3, (32, 1536), dtype=jnp.float32), 'c_proj_2': std * jax.random.normal(k4, (12, 1), dtype=jnp.float32)}
    _L1_ffn_all = _L1_ffn_setup()
    _L1_ffn_in = {k: v for k, v in _L1_ffn_all.items() if k in ('c_fc_1', 'c_fc_2', 'c_proj_1', 'c_proj_2', )}
    del _L1_ffn_all

    return {
        "x": x,
        "L0_conv_qkv_w": _L0_conv_in["qkv_w"],
        "L0_conv_qkv_b": _L0_conv_in["qkv_b"],
        "L0_conv_proj_w": _L0_conv_in["proj_w"],
        "L0_conv_proj_b": _L0_conv_in["proj_b"],
        "L0_conv_rel_pos_h": _L0_conv_in["rel_pos_h"],
        "L0_conv_rel_pos_w": _L0_conv_in["rel_pos_w"],
        "L1_attn_Wq": _L1_attn_in["Wq"],
        "L1_attn_Wk": _L1_attn_in["Wk"],
        "L1_attn_Wv": _L1_attn_in["Wv"],
        "L1_attn_Wo": _L1_attn_in["Wo"],
        "L1_attn_bo": _L1_attn_in["bo"],
        "L1_ffn_c_fc_1": _L1_ffn_in["c_fc_1"],
        "L1_ffn_c_fc_2": _L1_ffn_in["c_fc_2"],
        "L1_ffn_c_proj_1": _L1_ffn_in["c_proj_1"],
        "L1_ffn_c_proj_2": _L1_ffn_in["c_proj_2"],
    }

def reference(x, L0_conv_qkv_w, L0_conv_qkv_b, L0_conv_proj_w, L0_conv_proj_b, L0_conv_rel_pos_h, L0_conv_rel_pos_w, L1_attn_Wq, L1_attn_Wk, L1_attn_Wv, L1_attn_Wo, L1_attn_bo, L1_ffn_c_fc_1, L1_ffn_c_fc_2, L1_ffn_c_proj_1, L1_ffn_c_proj_2):
    import jax
    import jax.numpy as jnp
    def _L0_conv_ref(x, qkv_w, qkv_b, proj_w, proj_b, rel_pos_h, rel_pos_w):
        import jax, jax.numpy as jnp
        import numpy as np
        B, H, W, C = (8, 32, 32, 384)
        NH, HD = (6, 64)
        SCALE = HD ** (-0.5)

        def _get_rel_pos(rel_pos, q_size, k_size):
            coords = jnp.arange(q_size)[:, None] - jnp.arange(k_size)[None, :] + (k_size - 1)
            return rel_pos[coords]
        b, h, w, c = x.shape
        hw = h * w
        qkv = x.reshape(b, hw, c) @ qkv_w + qkv_b
        qkv = qkv.reshape(b, hw, 3, NH, HD).transpose(2, 0, 3, 1, 4)
        qkv = qkv.reshape(3, b * NH, hw, HD)
        q, k, v = (qkv[0], qkv[1], qkv[2])
        attn = jnp.einsum('bqd,bkd->bqk', q * SCALE, k)
        Rh = _get_rel_pos(rel_pos_h, h, h)
        Rw = _get_rel_pos(rel_pos_w, w, w)
        r_q = q.reshape(b * NH, h, w, HD)
        rel_h = jnp.einsum('bhwc,hkc->bhwk', r_q, Rh)
        rel_w = jnp.einsum('bhwc,wkc->bhwk', r_q, Rw)
        attn = attn.reshape(b * NH, h, w, h, w) + rel_h[:, :, :, :, None] + rel_w[:, :, :, None, :]
        attn = attn.reshape(b * NH, hw, hw)
        attn = jax.nn.softmax(attn, axis=-1)
        out = jnp.einsum('bqk,bkd->bqd', attn, v)
        out = out.reshape(b, NH, h, w, HD).transpose(0, 2, 3, 1, 4).reshape(b, h, w, c)
        return out @ proj_w + proj_b

    def _L1_attn_ref(x, Wq, Wk, Wv, Wo, bo):
        import jax, jax.numpy as jnp
        import numpy as np
        B, S, E, H = (8, 2048, 384, 6)
        D = E // H
        b, s, e = x.shape
        q = (x @ Wq).reshape(b, s, H, D).transpose(0, 2, 1, 3)
        k = (x @ Wk).reshape(b, s, H, D).transpose(0, 2, 1, 3)
        v = (x @ Wv).reshape(b, s, H, D).transpose(0, 2, 1, 3)
        scores = jnp.einsum('bhqd,bhkd->bhqk', q, k) / jnp.sqrt(jnp.asarray(D, x.dtype))
        causal = jnp.tril(jnp.ones((s, s), dtype=bool))
        scores = jnp.where(causal, scores, -jnp.inf)
        attn = jax.nn.softmax(scores, axis=-1)
        out = jnp.einsum('bhqk,bhkd->bhqd', attn, v)
        out = out.transpose(0, 2, 1, 3).reshape(b, s, e)
        return out @ Wo + bo

    def _L1_ffn_ref(x, c_fc_1, c_fc_2, c_proj_1, c_proj_2):
        import jax, jax.numpy as jnp
        import numpy as np
        D_MODEL = 384
        D_FF = 1536
        w_fc = jnp.kron(c_fc_1, c_fc_2)
        w_proj = jnp.kron(c_proj_1, c_proj_2)
        h = x @ w_fc.T
        h = jax.nn.gelu(h, approximate=False)
        out = h @ w_proj.T
        return out

    def _gn(v, G=32, eps=1e-5):
        B_, H_, W_, C_ = v.shape
        g = v.reshape(B_, H_, W_, G, C_ // G)
        m = jnp.mean(g, axis=(1, 2, 4), keepdims=True)
        s = jnp.var(g, axis=(1, 2, 4), keepdims=True)
        return ((g - m) / jnp.sqrt(s + eps)).reshape(v.shape)

    def _ln_c(v, eps=1e-6):
        m = jnp.mean(v, axis=-1, keepdims=True)
        s = jnp.var(v, axis=-1, keepdims=True)
        return (v - m) / jnp.sqrt(s + eps)

    def _ln_t(v, eps=1e-5):
        m = jnp.mean(v, axis=-1, keepdims=True)
        s = jnp.var(v, axis=-1, keepdims=True)
        return (v - m) / jnp.sqrt(s + eps)

    def _to_tokens(v):
        B_, H_, W_, C_ = v.shape
        return v.reshape(B_, H_ * W_, C_)
    def _from_tokens(t, like):
        return t.reshape(like.shape)

    x = x + _L0_conv_ref(_gn(x), L0_conv_qkv_w, L0_conv_qkv_b, L0_conv_proj_w, L0_conv_proj_b, L0_conv_rel_pos_h, L0_conv_rel_pos_w)
    t = _to_tokens(x)
    t = t + _L1_attn_ref(_ln_t(t), L1_attn_Wq, L1_attn_Wk, L1_attn_Wv, L1_attn_Wo, L1_attn_bo)
    t = t + _L1_ffn_ref(_ln_t(t), L1_ffn_c_fc_1, L1_ffn_c_fc_2, L1_ffn_c_proj_1, L1_ffn_c_proj_2)
    x = _from_tokens(t, x)
    return x


_drawn_inputs = setup_inputs


def setup_inputs(seed=0):
    import zlib

    import numpy as np

    out = dict(_drawn_inputs(seed))
    spreads = {'L1_attn_bo': (0.0, 0.399)}
    factors = {'L0_conv_qkv_w': 8.0,
     'L0_conv_qkv_b': 4.724,
     'L0_conv_proj_w': 4.56,
     'L0_conv_rel_pos_h': 8.0,
     'L0_conv_rel_pos_w': 8.0,
     'L1_ffn_c_fc_1': 8.0,
     'L1_ffn_c_fc_2': 8.0,
     'L1_ffn_c_proj_1': 8.0,
     'L1_ffn_c_proj_2': 8.0,
     'L0_conv_proj_b': 8.0}
    for name, (base, spread) in spreads.items():
        noise = np.random.default_rng([zlib.crc32(name.encode()), seed]).standard_normal(out[name].shape)
        drawn = base * np.exp(spread * noise) if base else spread * noise
        out[name] = jnp.asarray(drawn.astype(out[name].dtype))
    for name, factor in factors.items():
        out[name] = (out[name] * factor).astype(out[name].dtype)
    return out
```

```python
from contextlib import ExitStack

import concourse.bass as bass
from concourse import mybir

F32 = mybir.dt.float32
F16 = mybir.dt.float16
BF16 = mybir.dt.bfloat16
ALU = mybir.AluOpType
ACT = mybir.ActivationFunctionType
AX = mybir.AxisListType

P = 128
IMG = 32
T = IMG * IMG
NT = T // P
C = 384
NC_ = C // P
NH = 6
HD = 64
NPAIR = NH // 2
BANK = 512
NREL = 2 * IMG - 1
GC = 12
FF = 1536
NF = FF // P
FA, FB = 32, 12
SCALE = HD ** -0.5
MSCALE = 64.0
MASKED = -1.0e30
STORES = 32
VW = 2 * HD + 1


def slot(h):
    return (h % 2) * NPAIR + h // 2


def own(h):
    return slice(0, HD) if h % 2 == 0 else slice(HD, P)


def other(h):
    return slice(HD, P) if h % 2 == 0 else slice(0, HD)


def crows(h):
    return slice(0, HD + 1) if h % 2 == 0 else slice(0, P)


def mrow(h):
    return HD if h % 2 == 0 else 0


class Mem:
    pass


def allocate(nc, ctx, m):
    def sb(name, shape, dt):
        return ctx.enter_context(nc.sbuf_tensor(name, shape, dt))

    m.wqkv_hi = [sb(f"wqkv{n}_hi", [P, NC_, 3 * C], F16) for n in range(2)]
    m.wqkv_lo = [sb(f"wqkv{n}_lo", [P, NC_, 3 * C], F16) for n in range(2)]
    m.wo_hi = [sb(f"wo{n}_hi", [P, NC_, C], F16) for n in range(2)]
    m.wo_lo = [sb(f"wo{n}_lo", [P, NC_, C], F16) for n in range(2)]
    m.bqk = sb("bqk", [P, 2 * NPAIR], F32)
    m.bv = sb("bv", [P, C], F32)
    m.bo = [sb(f"bo{n}", [P, C], F32) for n in range(2)]
    m.rel_hi = sb("rel_hi", [P, 2, NREL], F16)
    m.rel_lo = sb("rel_lo", [P, 2, NREL], F16)
    m.c1 = sb("c1", [3 * FA, FF], F16)
    m.cp = sb("cp", [P, NF, FA], F32)
    m.cf2 = sb("cf2", [P, FB], F32)
    m.cp2 = sb("cp2", [P, FB], F32)
    m.spread = sb("spread", [P, C], F32)
    m.group = sb("group", [P, NC_, C], F32)
    m.ident = sb("ident", [P, P], F32)
    m.ident16 = sb("ident16", [P, P], F16)
    m.identb = sb("identb", [P, P], BF16)
    m.mask_kq = sb("mask_kq", [P, P], BF16)
    m.mask_qk = sb("mask_qk", [P, P], BF16)
    m.minus_half = sb("minus_half", [P, NT], F32)
    m.xin = sb("xin", [P, NT, C], F32)
    m.x = sb("x", [P, NT, C], F32)
    m.hT = sb("hT", [P, NC_, T], F16)
    m.lT = sb("lT", [P, NC_, T], F16)
    m.o = sb("o", [P, NT, C], F32)
    m.qa = sb("qa", [P, NH, T], F16)
    m.qb = sb("qb", [P, NH, T], F16)
    m.qc = sb("qc", [P, NH, T], F16)
    m.ka0 = sb("ka0", [P, NH, T], F16)
    m.kc = sb("kc", [P, NH, T], F16)
    m.v = sb("v", [P, NT, NH, VW], F16)
    m.p32 = sb("p32", [P, 3, 2, BANK], F32)
    m.ph = sb("ph", [P, 3, 2, BANK], F16)
    m.pl = sb("pl", [P, 3, 2, BANK], F16)
    m.stats = sb("stats", [P, NT, 6], F32)
    m.mv = sb("mv", [P, NT, 2], F32)
    m.small = sb("small", [P, 6, NT], F32)
    m.mxp = sb("mxp", [P, 2, 2, NT], F32)
    m.nm = sb("nm", [P, 2, NT], F16)
    m.rs = sb("rs", [P, 2, 4], F32)
    m.ps = ctx.enter_context(nc.psum_tensor("ps", [P, 8, BANK], F32))


class Stage:

    def __init__(self, nc, ctx, name, sems):
        self.nc, self.ctx, self.name = nc, ctx, name
        self.sems = [ctx.enter_context(nc.semaphore(f"{name}_{s}")) for s in sems]

    def __enter__(self):
        self.inner = ExitStack()
        return (self.inner.enter_context(self.nc.Block()), *self.sems)

    def __exit__(self, *a):
        return self.inner.__exit__(*a)


def constants(nc, ctx, m, d, stored):
    stage = [m.o[:, 0:3, :], m.o[:, 3:6, :],
             m.p32[:, 0:2, :, :].rearrange("p a b c -> p (a b c)")[:, 0:3 * C].rearrange("p (a b) -> p a b", a=3),
             m.x[:, 0:3, :], m.x[:, 3:6, :]]
    NS = len(stage)
    pieces = []
    w0 = d.qkv_w.rearrange("(k p) n -> p k n", p=P)
    for k in range(NC_):
        pieces.append((w0[:, k, :].rearrange("p (a b) -> p a b", a=3), m.wqkv_hi[0][:, k, :].rearrange("p (a b) -> p a b", a=3),
                       m.wqkv_lo[0][:, k, :].rearrange("p (a b) -> p a b", a=3)))
    for i, w in enumerate((d.wq, d.wk, d.wv)):
        pieces.append((w.rearrange("(k p) n -> p k n", p=P), m.wqkv_hi[1][:, :, i * C:(i + 1) * C], m.wqkv_lo[1][:, :, i * C:(i + 1) * C]))
    for n, w in enumerate((d.proj_w, d.wo)):
        pieces.append((w.rearrange("(k p) n -> p k n", p=P), m.wo_hi[n][:, :, :], m.wo_lo[n][:, :, :]))

    rel2 = m.ph[:, 0, :, :].rearrange("p a b -> p (a b)").bitcast(F32)[0:NREL, 0:4 * HD].rearrange("p (a b) -> p a b", a=4)
    anti = m.ph[:, 1, :, :].rearrange("p a b -> p (a b)").bitcast(F32)[0:NREL, 0:NREL]
    c1in = m.pl[:, 0, :, :].rearrange("p a b -> p (a b)").bitcast(F32)[:, 0:NF * FA].rearrange("p (a b) -> p a b", a=NF)
    cpin = m.hT[:, :, :].rearrange("p a b -> p (a b)").bitcast(F32)[0:FA, 0:FF]
    relf = m.pl[:, 1, :, :].rearrange("p a b -> p (a b)").bitcast(F32)[:, 0:2 * NREL].rearrange("p (a b) -> p a b", a=2)
    c1f = m.lT[:, :, :].rearrange("p a b -> p (a b)").bitcast(F32)[0:FA, 0:FF]

    loads = [ctx.enter_context(nc.semaphore(f"const_load{i}")) for i in range(NS)]
    st = Stage(nc, ctx, "const", ["tables_in", "biases_in", "hi_done", "lo_done", "filled", "shaped", "rel_mm", "rel_out", "rel_hi", "c1_mm",
                                  "c1_out", "c1_hi", "cp_mm", "cp_out"])
    with st as (block, tables_in, biases_in, hi_done, lo_done, filled, shaped, rel_mm, rel_out, rel_hi, c1_mm, c1_out, c1_hi, cp_mm, cp_out):
        @block.sync
        def _(sp):
            sp.sem_inc(stored, STORES)
            for i, r in enumerate((d.rel_h, d.rel_h, d.rel_w, d.rel_w)):
                sp.dma_start(rel2[:, i, :], r).then_inc(tables_in, 16)
            sp.dma_start(c1in, d.c_fc_1.rearrange("(i p) a -> p i a", p=P)).then_inc(tables_in, 16)
            sp.dma_start(cpin, d.c_proj_1).then_inc(tables_in, 16)
            for i, (src, _, _) in enumerate(pieces):
                if i >= NS:
                    sp.wait_ge(lo_done, i - NS + 1)
                sp.dma_start(stage[i % NS], src).then_inc(loads[i % NS], 16)

        @block.scalar
        def _(act):
            act.dma_start(m.bqk[:, :], d.qkv_b[0:2 * C].rearrange("(m p) -> p m", p=P), allow_slow_non_contiguous=True).then_inc(biases_in, 16)
            for dst, src in ((m.bv, d.qkv_b[2 * C:3 * C]), (m.bo[0], d.proj_b), (m.bo[1], d.bo),
                             (m.cf2, d.c_fc_2.rearrange("a b -> (a b)")), (m.cp2, d.c_proj_2.rearrange("a b -> (a b)"))):
                act.dma_start(dst[:, :], src.partition_broadcast(P)).then_inc(biases_in, 16)
            act.dma_start(m.xin[:, :, :], d.x_tiles[0]).then_inc(biases_in, 16)
            for i, (_, hi, _) in enumerate(pieces):
                act.wait_ge(loads[i % NS], 16 * (i // NS + 1))
                nc.scalar.activation(hi, stage[i % NS], ACT.Copy).then_inc(hi_done, 1)
            act.wait_ge(cp_mm, NF)
            nc.scalar.activation(m.cp[:, :, :], m.ps[:, 4, 0:NF * FA].rearrange("p (a b) -> p a b", a=NF), ACT.Copy).then_inc(cp_out, 1)
            act.wait_ge(c1_mm, NF)
            nc.scalar.activation(c1f, m.ps[0:FA, 1:4, :].rearrange("p a b -> p (a b)"), ACT.Copy).then_inc(c1_out, 1)
            act.wait_ge(biases_in, 16 * 7)

        @block.vector
        def _(dve):
            for i, (_, hi, lo) in enumerate(pieces):
                dve.wait_ge(hi_done, i + 1)
                nc.vector.tensor_tensor(lo, stage[i % NS], hi, ALU.subtract).then_inc(lo_done, 1)
            dve.wait_ge(rel_mm, 2)
            nc.vector.tensor_scalar(relf, m.ps[:, 0, 0:2 * NREL].rearrange("p (a b) -> p a b", a=2), 1.0 / SCALE, None, ALU.mult).then_inc(rel_out, 1)
            dve.wait_ge(rel_out, 1)
            nc.vector.tensor_copy(m.rel_hi[:, :, :], relf).then_inc(rel_hi, 1)
            dve.wait_ge(rel_hi, 1)
            nc.vector.tensor_tensor(m.rel_lo[:, :, :], relf, m.rel_hi[:, :, :], ALU.subtract)
            dve.wait_ge(c1_out, 1)
            nc.vector.tensor_copy(m.c1[0:FA, :], c1f).then_inc(c1_hi, 1)
            nc.vector.tensor_copy(m.c1[FA:2 * FA, :], c1f)
            dve.wait_ge(c1_hi, 1)
            nc.vector.tensor_tensor(m.c1[2 * FA:3 * FA, :], c1f, m.c1[0:FA, :], ALU.subtract)
            dve.wait_ge(biases_in, 16 * 7)
            dve.wait_ge(shaped, 1)
            nc.vector.tensor_tensor(m.spread[:, :].rearrange("p (a b) -> p a b", b=FB), m.spread[:, :].rearrange("p (a b) -> p a b", b=FB),
                                    m.cp2[:, :].unsqueeze(1).broadcast_to([P, FA, FB]), ALU.mult)

        @block.gpsimd
        def _(pool):
            count = [0]

            def fill(ap, value):
                nc.gpsimd.memset(ap, value).then_inc(filled, 1)
                count[0] += 1
                pool.wait_ge(filled, count[0])

            def carve(ap, op, fill_value, base, pattern, mult):
                nc.gpsimd.affine_select(out=ap, in_=ap, compare_op=op, fill=fill_value, base=base, pattern=pattern,
                                        channel_multiplier=mult).then_inc(filled, 1)
                count[0] += 1
                pool.wait_ge(filled, count[0])

            for t in (m.ident[:, :], m.ident16[:, :], m.identb[:, :], anti, m.mask_kq[:, :], m.mask_qk[:, :], m.spread[:, :],
                      m.ka0[:, :, :], m.qc[:, :, :], m.kc[:, :, :]):
                fill(t, 0.0)
            fill(m.group[:, :, :], 1.0 / GC)
            fill(m.minus_half[:, :], -0.5)
            fill(m.v[:, :, :, HD:HD + 1], 1.0)
            for h in range(NH):
                fill(m.kc[mrow(h):mrow(h) + 1, slot(h), :], MSCALE)
            for t in (m.ident[:, :], m.ident16[:, :], m.identb[:, :]):
                carve(t, ALU.not_equal, 1.0, 0, [[-1, P]], 1)
            carve(anti, ALU.not_equal, 1.0, -(NREL - 1), [[1, NREL]], 1)
            carve(m.mask_kq[:, :], ALU.is_ge, MASKED, 0, [[1, P]], -1)
            carve(m.mask_qk[:, :], ALU.is_ge, MASKED, 0, [[-1, P]], 1)
            for k in range(NC_):
                gk = m.group[:, k, :].rearrange("p (g r) -> p g r", r=GC)
                carve(gk, ALU.is_ge, 0.0, k * P, [[-GC, C // GC], [0, GC]], 1)
            for k in range(NC_):
                gk = m.group[:, k, :].rearrange("p (g r) -> p g r", r=GC)
                carve(gk, ALU.is_ge, 0.0, GC - 1 - k * P, [[GC, C // GC], [0, GC]], -1)
            for base_h in (HD, 0):
                s = slice(0, NPAIR) if base_h == HD else slice(NPAIR, NH)
                kh = m.ka0[base_h:base_h + IMG, s, :].rearrange("p s (a b) -> p s a b", a=IMG)
                kw = m.ka0[base_h + IMG:base_h + 2 * IMG, s, :].rearrange("p s (a b) -> p s a b", a=IMG)
                carve(kh, ALU.not_equal, 1.0, 0, [[0, NPAIR], [-1, IMG], [0, IMG]], 1)
                carve(kw, ALU.not_equal, 1.0, 0, [[0, NPAIR], [0, IMG], [-1, IMG]], 1)
            for j in range(4):
                sv = m.spread[j * FA:(j + 1) * FA, :].rearrange("p (a b) -> p a b", b=FB)
                carve(sv, ALU.not_equal, 1.0, 0, [[-1, FA], [0, FB]], 1)
            nc.gpsimd.memset(m.small[:, :, :], 0.0).then_inc(shaped, 1)

        @block.tensor
        def _(pe):
            pe.wait_ge(shaped, 1)
            pe.wait_ge(tables_in, 16 * 6)
            for i in range(2):
                nc.tensor.matmul(m.ps[:, 0, i * NREL:(i + 1) * NREL], rel2[:, 2 * i:2 * i + 2, :].rearrange("p a b -> p (a b)"), anti,
                                 start=True, stop=True).then_inc(rel_mm, 1)
            for i in range(NF):
                nc.tensor.transpose(m.ps[:, 4, i * FA:(i + 1) * FA], cpin[:, i * P:(i + 1) * P], m.ident[0:FA, 0:FA]).then_inc(cp_mm, 1)
            for i in range(NF):
                nc.tensor.transpose(m.ps[0:FA, 1 + i // 4, (i % 4) * P:(i % 4 + 1) * P], c1in[:, i, :], m.ident[:, :]).then_inc(c1_mm, 1)


def transpose_tiles(nc, pe, m, src, c, done, ready=None, free=None):
    for t in range(NT):
        if ready is not None:
            pe.wait_ge(ready, t + 1)
        nc.tensor.transpose(m.ps[:, 2 * c + t // 4, (t % 4) * P:(t % 4 + 1) * P], src[:, t, c * P:(c + 1) * P], m.ident[:, :]).then_inc(done, 1)


def group_norm(nc, ctx, m):
    st = Stage(nc, ctx, "gn", ["transposed", "stats", "agg", "mean_mm", "mean_out", "dev", "dev2", "var_mm", "var_eps", "rstd", "shift",
                               "normed", "hi", "lo"])
    mean_g, dev, tvar, veps, rstd, shift = (m.small[:, i, 0:NC_] for i in range(6))
    acc = m.ps[:, 6, 0:NC_]
    acc2 = m.ps[:, 7, 0:NC_]
    with st as (block, transposed, stats, agg, mean_mm, mean_out, devd, dev2, var_mm, var_eps, rstd_done, shift_done, normed, hi, lo):
        @block.tensor
        def _(pe):
            for c in range(NC_):
                transpose_tiles(nc, pe, m, m.xin, c, transposed)
            pe.wait_ge(agg, NC_)
            for i in range(NC_):
                for k in range(NC_):
                    mm = nc.tensor.matmul(acc[:, i:i + 1], m.group[:, k, i * P:(i + 1) * P], m.mv[:, k, 0:1], start=(k == 0), stop=(k == NC_ - 1))
            mm.then_inc(mean_mm, 1)
            pe.wait_ge(dev2, 1)
            for i in range(NC_):
                for k in range(NC_):
                    mm = nc.tensor.matmul(acc2[:, i:i + 1], m.group[:, k, i * P:(i + 1) * P], tvar[:, k:k + 1], start=(k == 0), stop=(k == NC_ - 1))
            mm.then_inc(var_mm, 1)

        @block.vector
        def _(dve):
            for c in range(NC_):
                for j in range(2):
                    dve.wait_ge(transposed, c * NT + 4 * (j + 1))
                    nc.vector.bn_stats(m.stats[:, 2 * c + j, :], m.ps[:, 2 * c + j, :]).then_inc(stats, 1)
            for c in range(NC_):
                dve.wait_ge(stats, 2 * (c + 1))
                nc.vector.bn_aggr(m.mv[:, c, :], m.stats[:, 2 * c:2 * c + 2, :]).then_inc(agg, 1)
            dve.wait_ge(mean_mm, 1)
            nc.vector.tensor_copy(mean_g, acc).then_inc(mean_out, 1)
            dve.wait_ge(mean_out, 1)
            dve.wait_ge(agg, NC_)
            nc.vector.tensor_tensor(dev, m.mv[:, 0:NC_, 0], mean_g, ALU.subtract).then_inc(devd, 1)
            dve.wait_ge(devd, 1)
            nc.vector.tensor_tensor(tvar, dev, dev, ALU.mult).then_inc(devd, 1)
            dve.wait_ge(devd, 2)
            nc.vector.tensor_tensor(tvar, tvar, m.mv[:, 0:NC_, 1], ALU.add).then_inc(dev2, 1)
            dve.wait_ge(var_mm, 1)
            nc.vector.tensor_scalar(veps, acc2, 1e-5, None, ALU.add).then_inc(var_eps, 1)
            dve.wait_ge(rstd_done, 1)
            nc.vector.scalar_tensor_tensor(shift, mean_g, -1.0, rstd, ALU.mult, ALU.mult).then_inc(shift_done, 1)
            xn = m.o[:, :, :].rearrange("p a b -> p (a b)").rearrange("p (a b) -> p a b", a=NC_)
            for c in range(NC_):
                dve.wait_ge(hi, c + 1)
                nc.vector.tensor_tensor(m.lT[:, c, :], xn[:, c, :], m.hT[:, c, :], ALU.subtract).then_inc(lo, 1)

        @block.gpsimd
        def _(pool):
            pool.wait_ge(var_eps, 1)
            nc.gpsimd.tensor_tensor(rstd, veps, m.minus_half[:, 0:NC_], ALU.pow).then_inc(rstd_done, 1)

        @block.scalar
        def _(act):
            xn = m.o[:, :, :].rearrange("p a b -> p (a b)").rearrange("p (a b) -> p a b", a=NC_)
            act.wait_ge(shift_done, 1)
            act.wait_ge(rstd_done, 1)
            for c in range(NC_):
                nc.scalar.activation(xn[:, c, :], m.ps[:, 2 * c:2 * c + 2, :].rearrange("p a b -> p (a b)"), ACT.Identity,
                                     scale=rstd[:, c:c + 1], bias=shift[:, c:c + 1]).then_inc(normed, 1)
                act.wait_ge(normed, c + 1)
                nc.scalar.activation(m.hT[:, c, :], xn[:, c, :], ACT.Copy).then_inc(hi, 1)


def layer_norm_rows(nc, dve, m, t, ln_stats, ln_mv):
    nc.vector.bn_stats(m.stats[:, t, :], m.x[:, t, :]).then_inc(ln_stats, 1)
    dve.wait_ge(ln_stats, t + 1)
    nc.vector.bn_aggr(m.mv[:, t, :], m.stats[:, t, :]).then_inc(ln_mv, 1)


def layer_norm_transposed(nc, ctx, m):
    st = Stage(nc, ctx, "ln", ["stats", "mv", "eps", "rstd", "normed", "transposed", "hi", "lo"])
    veps, rstd = m.small[:, 0, :], m.small[:, 1, :]
    with st as (block, stats, mv, eps, rstd_done, normed, transposed, hi, lo):
        @block.vector
        def _(dve):
            for t in range(NT):
                layer_norm_rows(nc, dve, m, t, stats, mv)
            dve.wait_ge(mv, NT)
            nc.vector.tensor_scalar(veps, m.mv[:, :, 1], 1e-5, None, ALU.add).then_inc(eps, 1)
            dve.wait_ge(rstd_done, 1)
            for t in range(NT):
                nc.vector.tensor_scalar(m.o[:, t, :], m.x[:, t, :], m.mv[:, t, 0:1], rstd[:, t:t + 1], ALU.subtract, ALU.mult).then_inc(normed, 1)
            for c in range(NC_):
                dve.wait_ge(hi, c + 1)
                nc.vector.tensor_tensor(m.lT[:, c, :], m.ps[:, 2 * c:2 * c + 2, :].rearrange("p a b -> p (a b)"), m.hT[:, c, :],
                                        ALU.subtract).then_inc(lo, 1)

        @block.gpsimd
        def _(pool):
            pool.wait_ge(eps, 1)
            nc.gpsimd.tensor_tensor(rstd, veps, m.minus_half[:, :], ALU.pow).then_inc(rstd_done, 1)

        @block.tensor
        def _(pe):
            for c in range(NC_):
                transpose_tiles(nc, pe, m, m.o, c, transposed, ready=normed if c == 0 else None)

        @block.scalar
        def _(act):
            for c in range(NC_):
                act.wait_ge(transposed, NT * (c + 1))
                nc.scalar.activation(m.hT[:, c, :], m.ps[:, 2 * c:2 * c + 2, :].rearrange("p a b -> p (a b)"), ACT.Copy).then_inc(hi, 1)


def projections(nc, ctx, m, layer):
    st = Stage(nc, ctx, f"qkv{layer}", ["mm", "hi", "lo", "kcopy", "v_mm", "v32", "v_hi", "v_lo"])
    wh, wl = m.wqkv_hi[layer], m.wqkv_lo[layer]
    NM = 2 * NPAIR
    ka = m.ka0 if layer == 0 else m.qb
    v32 = m.o

    def out2(i):
        return m.ps[:, 2 * (i % 4):2 * (i % 4) + 2, :].rearrange("p a b -> p (a b)")

    with st as (block, mm_done, hi, lo, kcopy, v_mm, v32_done, v_hi, v_lo):
        @block.tensor
        def _(pe):
            for i in range(NM):
                if i >= 4:
                    pe.wait_ge(lo, 2 * (i - 3))
                steps = [(w, x, k) for k in range(NC_) for w, x in ((wh, m.hT), (wh, m.lT), (wl, m.hT))]
                for n, (w, x, k) in enumerate(steps):
                    for j in range(2):
                        mm = nc.tensor.matmul(m.ps[:, 2 * (i % 4) + j, :], w[:, k, i * P:(i + 1) * P], x[:, k, j * BANK:(j + 1) * BANK],
                                              start=(n == 0), stop=(n == len(steps) - 1))
                mm.then_inc(mm_done, 1)
            for t in range(NT):
                bank = (4 + t) % 8 if t < 4 else t - 4
                if t < 4:
                    if t % 2 == 0:
                        pe.wait_ge(lo, 2 * (3 + t // 2))
                elif t % 2 == 0:
                    pe.wait_ge(lo, 2 * (5 + (t - 4) // 2))
                steps = [(x, w, k) for k in range(NC_) for x, w in ((m.hT, wh), (m.hT, wl), (m.lT, wh))]
                for n, (x, w, k) in enumerate(steps):
                    mm = nc.tensor.matmul(m.ps[:, bank, 0:C], x[:, k, t * P:(t + 1) * P], w[:, k, 2 * C:3 * C],
                                          start=(n == 0), stop=(n == len(steps) - 1))
                mm.then_inc(v_mm, 1)

        @block.scalar
        def _(act):
            for i in range(NM):
                act.wait_ge(mm_done, i + 1)
                for e in range(2):
                    h = 2 * (i % NPAIR) + e
                    dst = m.qa if i < NPAIR else ka
                    if layer == 0:
                        nc.scalar.activation(dst[own(h), slot(h), :], out2(i)[own(h), :], ACT.Identity, bias=m.bqk[own(h), i:i + 1]).then_inc(hi, 1)
                    else:
                        nc.scalar.activation(dst[own(h), slot(h), :], out2(i)[own(h), :], ACT.Copy).then_inc(hi, 1)
            for t in range(NT):
                act.wait_ge(v32_done, t + 1)
                nc.scalar.activation(m.v[:, t, :, 0:HD], v32[:, t, :].rearrange("p (h d) -> p h d", d=HD), ACT.Copy).then_inc(v_hi, 1)

        @block.vector
        def _(dve):
            for i in range(NM):
                for e in range(2):
                    h = 2 * (i % NPAIR) + e
                    is_q = i < NPAIR
                    src = m.qa if is_q else ka
                    if layer == 0:
                        dst = m.qb[own(h), slot(h), :] if is_q else m.kc[own(h), slot(h), :]
                    else:
                        dst = m.qa[other(h), slot(h), :] if is_q else m.kc[own(h), slot(h), :]
                    dve.wait_ge(hi, 2 * i + e + 1)
                    if layer == 0:
                        nc.vector.scalar_tensor_tensor(dst, out2(i)[own(h), :], m.bqk[own(h), i:i + 1], src[own(h), slot(h), :],
                                                       ALU.add, ALU.subtract).then_inc(lo, 1)
                    else:
                        nc.vector.tensor_tensor(dst, out2(i)[own(h), :], src[own(h), slot(h), :], ALU.subtract).then_inc(lo, 1)
                    if is_q:
                        nc.vector.tensor_copy(m.qc[own(h), slot(h), :], src[own(h), slot(h), :])
                    elif layer == 1:
                        nc.vector.tensor_copy(ka[other(h), slot(h), :], src[own(h), slot(h), :])
            for t in range(NT):
                bank = (4 + t) % 8 if t < 4 else t - 4
                dve.wait_ge(v_mm, t + 1)
                if layer == 0:
                    nc.vector.tensor_tensor(v32[:, t, :], m.ps[:, bank, 0:C], m.bv[:, :], ALU.add).then_inc(v32_done, 1)
                else:
                    nc.vector.tensor_copy(v32[:, t, :], m.ps[:, bank, 0:C]).then_inc(v32_done, 1)

        @block.gpsimd
        def _(pool):
            for t in range(NT):
                pool.wait_ge(v_hi, t + 1)
                nc.gpsimd.tensor_tensor(m.v[:, t, :, HD + 1:VW], v32[:, t, :].rearrange("p (h d) -> p h d", d=HD), m.v[:, t, :, 0:HD],
                                        ALU.subtract).then_inc(v_lo, 1)


def relative_positions(nc, ctx, m):
    st = Stage(nc, ctx, "rel", ["mm", "hi", "lo"])
    HALF = IMG // 2

    def base(parity, axis):
        return (HD if parity == 0 else 0) + IMG * axis

    def parts(chunk):
        for pair in range(NPAIR):
            for parity in range(2):
                for axis in range(2):
                    b = base(parity, axis)
                    src = m.ps[b:b + IMG, 4 * chunk:4 * chunk + 4, 0:4 * NPAIR * IMG].rearrange("p k (i s w) -> p k i s w", i=4, s=NPAIR)[:, :, :, pair, :]

                    def dst(buf, b=b, axis=axis, pair=pair, parity=parity):
                        full = buf[b:b + IMG, parity * NPAIR + pair, :].rearrange("p (h w) -> p h w", h=IMG)
                        if axis == 0:
                            return full[:, chunk * HALF:(chunk + 1) * HALF, :].rearrange("p (k i) w -> p k i w", i=4)
                        return full[:, :, chunk * HALF:(chunk + 1) * HALF].rearrange("p h (k i) -> p k i h", i=4)

                    yield src, dst

    with st as (block, mm_done, hi, lo):
        @block.tensor
        def _(pe):
            for pos in range(IMG):
                for axis in range(2):
                    for parity in range(2):
                        rows = own(parity)
                        b = base(parity, axis)
                        o = m.ps[b:b + IMG, pos // 4, (pos % 4) * NPAIR * IMG:(pos % 4 + 1) * NPAIR * IMG].rearrange("p (s w) -> p s w", s=NPAIR)
                        sl = slice(parity * NPAIR, (parity + 1) * NPAIR)

                        def queries(buf):
                            full = buf[rows, sl, :].rearrange("p s (h w) -> p s h w", h=IMG)
                            return full[:, :, pos, :] if axis == 0 else full[:, :, :, pos]
                        t0 = IMG - 1 - pos
                        steps = ((m.rel_hi, m.qa), (m.rel_hi, m.qb), (m.rel_lo, m.qa))
                        for n, (r, q) in enumerate(steps):
                            mm = nc.tensor.matmul(o, r[rows, axis, t0:t0 + IMG], queries(q), start=(n == 0), stop=(n == len(steps) - 1))
                if pos % HALF == HALF - 1:
                    mm.then_inc(mm_done, 1)

        @block.scalar
        def _(act):
            n = 0
            for chunk in range(2):
                act.wait_ge(mm_done, chunk + 1)
                for src, dst in parts(chunk):
                    n += 1
                    if n > 4:
                        act.wait_ge(lo, n - 4)
                    nc.scalar.activation(dst(m.qa), src, ACT.Copy).then_inc(hi, 1)

        @block.vector
        def _(dve):
            n = 0
            for chunk in range(2):
                for src, dst in parts(chunk):
                    n += 1
                    dve.wait_ge(hi, n)
                    nc.vector.tensor_tensor(dst(m.qb), src, dst(m.qa), ALU.subtract).then_inc(lo, 1)


def attention(nc, ctx, m, layer, prefetch=None):
    ka = m.ka0 if layer == 0 else m.qb
    causal = layer == 1
    HALFT = BANK // P
    if causal:
        groups = [(hf, kt, max(hf * BANK, kt * P)) for hf in range(2) for kt in range(0, 4 * (hf + 1), 2)]
        tiles = [(qt, kh, min(BANK, (qt + 1) * P - kh * BANK)) for qt in range(NT) for kh in range(2) if (qt + 1) * P > kh * BANK]
        per_group = [3, 3, 3, 3, 0, 0]
        row_at = 4
        both = slice(4, NT)
    else:
        groups = [(hf, kt, hf * BANK) for hf in range(2) for kt in range(0, NT, 2)]
        tiles = [(qt, kh, BANK) for qt in range(NT) for kh in range(2)]
        per_group = [3, 3, 3, 3, 2, 2, 0, 0]
        row_at = 6
        both = slice(0, NT)
    NG, NTL = len(groups), len(tiles)
    N = NH * NG
    RING = 3
    starts = [sum(per_group[:g]) for g in range(NG)]
    last_of_half = {g for g in range(NG) if g == NG - 1 or groups[g + 1][0] != groups[g][0]}

    def on_pool(i):
        return i % 3 == 2

    def pool_before(i):
        return i // 3

    def wait_pl(eng, i, pl_dve, pl_pool):
        if on_pool(i):
            eng.wait_ge(pl_pool, pool_before(i) + 1)
        else:
            eng.wait_ge(pl_dve, i - pool_before(i) + 1)

    def cols(i):
        hf, _, q0 = groups[i % NG]
        return (hf + 1) * BANK - q0

    def max_tile(h, n):
        return h * NTL + n

    st = Stage(nc, ctx, f"attn{layer}", ["scores", "exp", "hi", "pl_dve", "pl_pool", "pv", "tile", "reduced", "combined", "nm", "row_t", "row",
                                         "half_done", "recip", "out"])
    with st as (block, scores, exp_done, hi_done, pl_dve, pl_pool, pv_done, tile_done, reduced, combined, nm_done, row_t, row, half_done,
                recip, out_done):
        @block.tensor
        def _(pe):
            def maximum_scores(h, n):
                qt, kh, w = tiles[n]
                r = max_tile(h, n)
                if r >= 2:
                    pe.wait_ge(reduced, r - 1)
                if n < 2 and h > 0:
                    pe.wait_ge(row, h)
                bank = 4 + r % 2
                s = slot(h)
                diag = causal and (qt + 1) * P - kh * BANK <= BANK
                if diag:
                    nc.tensor.matmul(m.ps[:, bank, w - P:w], m.identb[:, :], m.mask_qk[:, :], start=True, stop=False, skip_group_check=True)
                mm = nc.tensor.matmul(m.ps[:, bank, 0:w], m.qa[:, s, qt * P:(qt + 1) * P], ka[:, s, kh * BANK:kh * BANK + w],
                                      start=not diag, stop=True, skip_group_check=True)
                mm.then_inc(tile_done, 1)

            def maximum_row(h):
                pe.wait_ge(nm_done, h + 1)
                pe.wait_ge(reduced, (h + 1) * NTL)
                r = mrow(h)
                o = m.ps[:, 4, :].bitcast(F16)
                for qt in range(NT):
                    mm = nc.tensor.transpose(o[r:r + 1, qt * P:(qt + 1) * P], m.nm[:, h % 2, qt:qt + 1], m.ident16[:, :])
                mm.then_inc(row_t, 1)

            def score_tiles(i):
                h, g = i // NG, i % NG
                hf, kt0, q0 = groups[g]
                w = cols(i)
                s = slot(h)
                if g == 0:
                    pe.wait_ge(row, h + 1)
                if i >= 2:
                    pe.wait_ge(exp_done, i - 1)
                q = slice(q0, q0 + w)
                for j in range(2):
                    k = slice((kt0 + j) * P, (kt0 + j + 1) * P)
                    o = m.ps[:, 2 * (i % 2) + j, 0:w]
                    nc.tensor.matmul(o, ka[:, s, k], m.qa[:, s, q], start=True, stop=False)
                    if layer == 0:
                        nc.tensor.matmul(o, ka[:, s, k], m.qb[:, s, q], start=False, stop=False)
                    d0 = (kt0 + j) * P - q0
                    diag = causal and 0 <= d0 < w
                    if diag:
                        nc.tensor.matmul(o[:, d0:d0 + P], m.identb[:, :], m.mask_kq[:, :], start=False, stop=False, skip_group_check=True)
                    mm = nc.tensor.matmul(o, m.kc[crows(h), s, k], m.qc[crows(h), s, q], start=False, stop=True)
                mm.then_inc(scores, 1)

            def weighted_values(i):
                h, g = i // NG, i % NG
                hf, kt0, q0 = groups[g]
                half = 2 * h + hf
                first = g == 0 or groups[g - 1][0] != hf
                if first and half >= 2:
                    pe.wait_ge(out_done, half - 1)
                pe.wait_ge(hi_done, i + 1)
                wait_pl(pe, i, pl_dve, pl_pool)
                work = []
                for j in range(2):
                    kt = kt0 + j
                    for qt in range(q0 // P, HALFT * (hf + 1)):
                        if causal and qt < kt:
                            continue
                        c0 = (qt - hf * HALFT) * (HD + 1)
                        e0 = qt * P - q0
                        hi_p = m.ph[:, i % RING, j, e0:e0 + P]
                        lo_p = m.pl[:, i % RING, j, e0:e0 + P]
                        work += [(c0, HD + 1, hi_p, m.v[:, kt, h, 0:HD + 1]), (c0, HD, hi_p, m.v[:, kt, h, HD + 1:VW]),
                                 (c0, HD + 1, lo_p, m.v[:, kt, h, 0:HD + 1])]
                for n, (c0, w, e, v) in enumerate(work):
                    mm = nc.tensor.matmul(m.ps[:, 6 + half % 2, c0:c0 + w], e, v, start=(first and n == 0),
                                          stop=(g in last_of_half and n == len(work) - 1), skip_group_check=True)
                mm.then_inc(pv_done, 1)

            for n in range(NTL):
                maximum_scores(0, n)
            maximum_row(0)
            for i in range(N + 2):
                h, g = i // NG, i % NG
                if i < N:
                    score_tiles(i)
                    if h + 1 < NH:
                        for n in range(starts[g], starts[g] + per_group[g]):
                            maximum_scores(h + 1, n)
                        if g == row_at:
                            maximum_row(h + 1)
                if i >= 2:
                    weighted_values(i - 2)

        @block.scalar
        def _(act):
            def row_out(h):
                act.wait_ge(row_t, h + 1)
                r = mrow(h)
                nc.scalar.activation(m.qc[r:r + 1, slot(h), :], m.ps[:, 4, :].bitcast(F16)[r:r + 1, :], ACT.Copy).then_inc(row, 1)

            row_out(0)
            for i in range(N):
                h, g = i // NG, i % NG
                w = cols(i)
                act.wait_ge(scores, i + 1)
                if i >= RING:
                    wait_pl(act, i - RING, pl_dve, pl_pool)
                nc.scalar.activation(m.p32[:, i % RING, :, 0:w], m.ps[:, 2 * (i % 2):2 * (i % 2) + 2, 0:w], ACT.Exp, scale=SCALE).then_inc(exp_done, 1)
                act.wait_ge(exp_done, i + 1)
                if i >= RING:
                    act.wait_ge(pv_done, i - RING + 1)
                nc.scalar.activation(m.ph[:, i % RING, :, 0:w], m.p32[:, i % RING, :, 0:w], ACT.Copy).then_inc(hi_done, 1)
                if g == row_at and h + 1 < NH:
                    row_out(h + 1)

        def low_part(eng, engine, i, sem):
            w = cols(i)
            eng.wait_ge(hi_done, i + 1)
            if i >= RING:
                eng.wait_ge(pv_done, i - RING + 1)
            engine.tensor_tensor(m.pl[:, i % RING, :, 0:w], m.p32[:, i % RING, :, 0:w], m.ph[:, i % RING, :, 0:w], ALU.subtract).then_inc(sem, 1)

        @block.vector
        def _(dve):
            done = [0]

            def reduce_tile(h, n):
                qt, kh, w = tiles[n]
                r = max_tile(h, n)
                if n == 0 and h >= 2:
                    dve.wait_ge(nm_done, h - 1)
                dve.wait_ge(tile_done, r + 1)
                nc.vector.reduce_max(m.mxp[:, h % 2, kh, qt:qt + 1], m.ps[:, 4 + r % 2, 0:w], AX.X).then_inc(reduced, 1)

            def combine(h):
                dve.wait_ge(reduced, (h + 1) * NTL)
                if h >= 2:
                    dve.wait_ge(row_t, h - 1)
                nc.vector.tensor_tensor(m.mxp[:, h % 2, 0, both], m.mxp[:, h % 2, 0, both], m.mxp[:, h % 2, 1, both], ALU.max).then_inc(combined, 1)
                dve.wait_ge(combined, h + 1)
                nc.vector.tensor_scalar(m.nm[:, h % 2, :], m.mxp[:, h % 2, 0, :], -1.0 / MSCALE, None, ALU.mult).then_inc(nm_done, 1)

            def normalise(i):
                h, g = i // NG, i % NG
                hf = groups[g][0]
                half = 2 * h + hf
                acc = m.ps[:, 6 + half % 2, 0:HALFT * (HD + 1)].rearrange("p (t c) -> p t c", c=HD + 1)
                dve.wait_ge(pv_done, i + 1)
                nc.vector.reciprocal(m.rs[:, half % 2, :], acc[:, :, HD]).then_inc(recip, 1)
                dve.wait_ge(recip, half + 1)
                nc.vector.tensor_tensor(m.o[:, hf * HALFT:(hf + 1) * HALFT, h * HD:(h + 1) * HD], acc[:, :, 0:HD],
                                        m.rs[:, half % 2, :].unsqueeze(2).broadcast_to([P, HALFT, HD]), ALU.mult).then_inc(out_done, 1)

            for n in range(NTL):
                reduce_tile(0, n)
            combine(0)
            for i in range(N + 2):
                h, g = i // NG, i % NG
                if i < N and h + 1 < NH:
                    for n in range(starts[g], starts[g] + per_group[g]):
                        reduce_tile(h + 1, n)
                    if g == row_at - 1:
                        combine(h + 1)
                if 1 <= i <= N and not on_pool(i - 1):
                    low_part(dve, nc.vector, i - 1, pl_dve)
                if i >= 2 and (i - 2) % NG in last_of_half:
                    normalise(i - 2)

        @block.gpsimd
        def _(pool):
            for i in range(N):
                if on_pool(i):
                    low_part(pool, nc.gpsimd, i, pl_pool)

        if prefetch is not None:
            prefetch(block)


def out_projection(nc, ctx, m, layer, stored=None, stored_before=None):
    st = Stage(nc, ctx, f"proj{layer}", ["biased", "transposed", "hi", "lo", "mm", "added", "x_free"])
    src = m.xin if layer == 0 else m.x
    with st as (block, biased, transposed, hi, lo, mm_done, added, x_free):
        if stored is not None:
            @block.sync
            def _(sp):
                sp.wait_ge(stored, stored_before)
                sp.sem_inc(x_free, 1)

        @block.gpsimd
        def _(pool):
            nc.gpsimd.tensor_tensor(src[:, :, :], src[:, :, :], m.bo[layer][:, :].unsqueeze(1).broadcast_to([P, NT, C]), ALU.add).then_inc(biased, 1)

        @block.tensor
        def _(pe):
            for c in range(NC_):
                transpose_tiles(nc, pe, m, m.o, c, transposed)
            pe.wait_ge(lo, NC_)
            for t in range(NT):
                if t >= 2:
                    pe.wait_ge(added, t - 1)
                steps = [(x, w, k) for k in range(NC_) for x, w in ((m.hT, m.wo_hi[layer]), (m.hT, m.wo_lo[layer]), (m.lT, m.wo_hi[layer]))]
                for n, (x, w, k) in enumerate(steps):
                    mm = nc.tensor.matmul(m.ps[:, 6 + t % 2, 0:C], x[:, k, t * P:(t + 1) * P], w[:, k, :], start=(n == 0), stop=(n == len(steps) - 1))
                mm.then_inc(mm_done, 1)

        @block.scalar
        def _(act):
            for c in range(NC_):
                act.wait_ge(transposed, NT * (c + 1))
                nc.scalar.activation(m.hT[:, c, :], m.ps[:, 2 * c:2 * c + 2, :].rearrange("p a b -> p (a b)"), ACT.Copy).then_inc(hi, 1)

        @block.vector
        def _(dve):
            for c in range(NC_):
                dve.wait_ge(hi, c + 1)
                nc.vector.tensor_tensor(m.lT[:, c, :], m.ps[:, 2 * c:2 * c + 2, :].rearrange("p a b -> p (a b)"), m.hT[:, c, :],
                                        ALU.subtract).then_inc(lo, 1)
            dve.wait_ge(biased, 1)
            if stored is not None:
                dve.wait_ge(x_free, 1)
            for t in range(NT):
                dve.wait_ge(mm_done, t + 1)
                nc.vector.tensor_tensor(m.x[:, t, :], m.ps[:, 6 + t % 2, 0:C], src[:, t, :], ALU.add).then_inc(added, 1)


def feed_forward(nc, ctx, m, out_ap, stored):
    st = Stage(nc, ctx, "ff", ["stats", "mv", "eps", "rstd", "normed", "scaled", "x2", "x2_t", "x2_hi", "x2_hi2", "x2_lo", "up", "act", "down",
                               "down_out", "spread", "added", "down_each"])
    veps, rstd = m.small[:, 0, :], m.small[:, 1, :]
    x2 = m.small[:, 2:6, :]
    x2 = m.ph[:, 0, :, :].rearrange("p a b -> p (a b)").bitcast(F32)[:, 0:NT * FA].rearrange("p (t a) -> p t a", t=NT)
    stack = m.hT[0:3 * FA, 0, :]
    x2f = m.lT[:, :, :].rearrange("p a b -> p (a b)").bitcast(F32)[0:FA, 0:T]
    o2 = m.pl[:, 0:2, :, :].rearrange("p r a b -> p (r a b)").bitcast(F32)[:, 0:T]
    NHID = 3

    def hidden(i):
        return m.p32[:, i % NHID, :, :].rearrange("p a b -> p (a b)")

    with st as (block, stats, mv, eps, rstd_done, normed, scaled, x2_done, x2_t, x2_hi, x2_hi2, x2_lo, up, act_done, down, down_out, spread, added, down_each):
        @block.vector
        def _(dve):
            for t in range(NT):
                layer_norm_rows(nc, dve, m, t, stats, mv)
            dve.wait_ge(mv, NT)
            nc.vector.tensor_scalar(veps, m.mv[:, :, 1], 1e-5, None, ALU.add).then_inc(eps, 1)
            dve.wait_ge(rstd_done, 1)
            for t in range(NT):
                nc.vector.tensor_scalar(m.o[:, t, :], m.x[:, t, :], m.mv[:, t, 0:1], rstd[:, t:t + 1], ALU.subtract, ALU.mult).then_inc(normed, 1)
            for t in range(NT):
                dve.wait_ge(scaled, t + 1)
                nc.vector.reduce_sum(x2[:, t, :], m.o[:, t, :].rearrange("p (a b) -> p a b", b=FB), AX.X).then_inc(x2_done, 1)
            dve.wait_ge(x2_t, 1)
            nc.vector.tensor_copy(x2f, m.ps[0:FA, 0:2, :].rearrange("p a b -> p (a b)")).then_inc(x2_hi, 1)
            dve.wait_ge(x2_hi, 1)
            nc.vector.tensor_copy(stack[0:FA, :], x2f).then_inc(x2_hi2, 1)
            nc.vector.tensor_copy(stack[2 * FA:3 * FA, :], x2f).then_inc(x2_hi2, 1)
            dve.wait_ge(x2_hi2, 2)
            nc.vector.tensor_tensor(stack[FA:2 * FA, :], x2f, stack[0:FA, :], ALU.subtract).then_inc(x2_lo, 1)
            dve.wait_ge(down, 1)
            nc.vector.tensor_copy(o2, m.ps[:, 4:6, :].rearrange("p a b -> p (a b)")).then_inc(down_out, 1)
            for t in range(NT):
                dve.wait_ge(spread, t + 1)
                nc.vector.tensor_tensor(m.x[:, t, :], m.ps[:, 6 + t % 2, 0:C], m.x[:, t, :], ALU.add).then_inc(added, 1)

        @block.gpsimd
        def _(pool):
            pool.wait_ge(eps, 1)
            nc.gpsimd.tensor_tensor(rstd, veps, m.minus_half[:, :], ALU.pow).then_inc(rstd_done, 1)
            for t in range(NT):
                pool.wait_ge(normed, t + 1)
                o3 = m.o[:, t, :].rearrange("p (a b) -> p a b", b=FB)
                nc.gpsimd.tensor_tensor(o3, o3, m.cf2[:, :].unsqueeze(1).broadcast_to([P, FA, FB]), ALU.mult).then_inc(scaled, 1)

        @block.tensor
        def _(pe):
            for t in range(NT):
                pe.wait_ge(x2_done, t + 1)
                mm = nc.tensor.transpose(m.ps[0:FA, t // 4, (t % 4) * P:(t % 4 + 1) * P], x2[:, t, :], m.ident[:, :])
            mm.then_inc(x2_t, 1)
            pe.wait_ge(x2_lo, 1)

            def down_product(i):
                pe.wait_ge(act_done, i + 1)
                q = i % 4
                for j in range(2):
                    mm = nc.tensor.matmul(m.ps[q * FA:(q + 1) * FA, 4 + j, :], m.cp[:, i, :], hidden(i)[:, j * BANK:(j + 1) * BANK],
                                          start=(i < 4), stop=(i >= NF - 4), skip_group_check=True)
                mm.then_inc(down, 1) if i == NF - 1 else mm.then_inc(down_each, 1)

            for i in range(NF + 1):
                if i < NF:
                    if i >= 2:
                        pe.wait_ge(act_done, i - 1)
                    for j in range(2):
                        mm = nc.tensor.matmul(m.ps[:, 2 * (i % 2) + j, :], m.c1[:, i * P:(i + 1) * P], stack[:, j * BANK:(j + 1) * BANK], start=True, stop=True)
                    mm.then_inc(up, 1)
                if i >= 1:
                    down_product(i - 1)
            pe.wait_ge(down_out, 1)
            for t in range(NT):
                if t >= 2:
                    pe.wait_ge(added, t - 1)
                nc.tensor.matmul(m.ps[:, 6 + t % 2, 0:C], o2[:, t * P:(t + 1) * P], m.spread[:, :], start=True, stop=True).then_inc(spread, 1)

        @block.scalar
        def _(act):
            for i in range(NF):
                act.wait_ge(up, i + 1)
                if i >= NHID:
                    act.wait_ge(down_each, i - NHID + 1)
                nc.scalar.activation(hidden(i), m.ps[:, 2 * (i % 2):2 * (i % 2) + 2, :].rearrange("p a b -> p (a b)"), ACT.Gelu).then_inc(act_done, 1)

        @block.sync
        def _(sp):
            for half in range(2):
                sp.wait_ge(added, 4 * (half + 1))
                sp.dma_start(out_ap[:, 4 * half:4 * half + 4, :], m.x[:, 4 * half:4 * half + 4, :]).then_inc(stored, 16)


class Dram:
    pass


def build(nc, x, qkv_w, qkv_b, proj_w, proj_b, rel_h, rel_w, wq, wk, wv, wo, bo, c_fc_1, c_fc_2, c_proj_1, c_proj_2, out):
    d = Dram()
    d.qkv_w, d.qkv_b, d.proj_w, d.proj_b, d.rel_h, d.rel_w = qkv_w, qkv_b, proj_w, proj_b, rel_h, rel_w
    d.wq, d.wk, d.wv, d.wo, d.bo = wq, wk, wv, wo, bo
    d.c_fc_1, d.c_fc_2, d.c_proj_1, d.c_proj_2 = c_fc_1, c_fc_2, c_proj_1, c_proj_2
    images = x.shape[0]
    d.x_tiles = x.rearrange("b h w c -> b (h w) c").rearrange("b (t p) c -> b p t c", p=P)
    out_tiles = out.rearrange("b h w c -> b (h w) c").rearrange("b (t p) c -> b p t c", p=P)
    with ExitStack() as ctx:
        m = Mem()
        allocate(nc, ctx, m)
        stored = ctx.enter_context(nc.semaphore("stored"))
        constants(nc, ctx, m, d, stored)
        loop_ctx = ctx
        first = ctx.enter_context(nc.semaphore("loop_first"))
        with nc.Fori(0, images) as b:
            group_norm(nc, loop_ctx, m)
            projections(nc, loop_ctx, m, 0)
            relative_positions(nc, loop_ctx, m)
            attention(nc, loop_ctx, m, 0)
            out_projection(nc, loop_ctx, m, 0, stored, (b + 1) * STORES)
            layer_norm_transposed(nc, loop_ctx, m)
            projections(nc, loop_ctx, m, 1)

            next_in = loop_ctx.enter_context(nc.semaphore("next_in"))

            def prefetch(block):
                @block.sync
                def _(sp):
                    sp.dma_start(m.xin[:, :, :], d.x_tiles[(b + 1) % images]).then_inc(next_in, 16)
                    sp.wait_ge(next_in, 16)

            attention(nc, loop_ctx, m, 1, prefetch)
            out_projection(nc, loop_ctx, m, 1)
            feed_forward(nc, loop_ctx, m, out_tiles[b], stored)
            last = loop_ctx.enter_context(nc.semaphore("loop_last"))
            nc.gpsimd.sem_clear(range(first.num, last.num + 1))
            nc.all_engine_barrier()
        with nc.Block() as block:
            @block.sync
            def _(sp):
                sp.wait_ge(stored, (images + 1) * STORES)


_INS = ['x', 'L0_conv_qkv_w', 'L0_conv_qkv_b', 'L0_conv_proj_w', 'L0_conv_proj_b', 'L0_conv_rel_pos_h', 'L0_conv_rel_pos_w',
        'L1_attn_Wq', 'L1_attn_Wk', 'L1_attn_Wv', 'L1_attn_Wo', 'L1_attn_bo', 'L1_ffn_c_fc_1', 'L1_ffn_c_fc_2', 'L1_ffn_c_proj_1',
        'L1_ffn_c_proj_2']


def kernel(**inputs):
    import numpy as _np
    import concourse.bacc as _bacc
    from concourse import mybir as _mybir
    from concourse.bass_utils import run_bass_kernel_spmd as _run

    nc = _bacc.Bacc("TRN2", target_bir_lowering=False, num_devices=1)
    arrays, args = {}, []
    for name in _INS:
        a = _np.ascontiguousarray(inputs[name])
        arrays[f"in_{name}"] = a
        args.append(nc.dram_tensor(f"in_{name}", a.shape, _mybir.dt.from_np(a.dtype), kind="ExternalInput").ap())
    args.append(nc.dram_tensor("out", inputs["x"].shape, _mybir.dt.float32, kind="ExternalOutput").ap())
    build(nc, *args)
    return _run(nc, [arrays], core_ids=[0]).results[0]["out"]
```

```python
from contextlib import ExitStack

import concourse.bass as bass
from concourse import mybir

F32 = mybir.dt.float32
F16 = mybir.dt.float16
BF16 = mybir.dt.bfloat16
ALU = mybir.AluOpType
ACT = mybir.ActivationFunctionType
AX = mybir.AxisListType

P = 128
IMG = 32
T = IMG * IMG
NT = T // P
C = 384
NC_ = C // P
NH = 6
HD = 64
NPAIR = NH // 2
BANK = 512
NREL = 2 * IMG - 1
GC = 12
FF = 1536
NF = FF // P
FA, FB = 32, 12
SCALE = HD ** -0.5
MSCALE = 64.0
MASKED = -1.0e30
RING = 4
ROW_LEAD = 3
LAG = 3
STORES = 32
VW = 2 * HD + 1


def slot(h):
    return (h % 2) * NPAIR + h // 2


def own(h):
    return slice(0, HD) if h % 2 == 0 else slice(HD, P)


def other(h):
    return slice(HD, P) if h % 2 == 0 else slice(0, HD)


def crows(h):
    return slice(0, HD + 1) if h % 2 == 0 else slice(0, P)


def mrow(h):
    return HD if h % 2 == 0 else 0


class Mem:
    pass


def allocate(nc, ctx, m):
    def sb(name, shape, dt):
        return ctx.enter_context(nc.sbuf_tensor(name, shape, dt))

    m.wqkv_hi = [sb(f"wqkv{n}_hi", [P, NC_, 3 * C], F16) for n in range(2)]
    m.wqkv_lo = [sb(f"wqkv{n}_lo", [P, NC_, 3 * C], F16) for n in range(2)]
    m.wo_hi = [sb(f"wo{n}_hi", [P, NC_, C], F16) for n in range(2)]
    m.wo_lo = [sb(f"wo{n}_lo", [P, NC_, C], F16) for n in range(2)]
    m.bqk = sb("bqk", [P, 2 * NPAIR], F32)
    m.bv = sb("bv", [P, C], F32)
    m.bo = [sb(f"bo{n}", [P, C], F32) for n in range(2)]
    m.rel_hi = sb("rel_hi", [P, 2, NREL], F16)
    m.rel_lo = sb("rel_lo", [P, 2, NREL], F16)
    m.c1 = sb("c1", [3 * FA, FF], F16)
    m.cp = sb("cp", [P, NF, FA], F32)
    m.cf2 = sb("cf2", [P, FB], F32)
    m.cp2 = sb("cp2", [P, FB], F32)
    m.spread = sb("spread", [P, C], F32)
    m.group = sb("group", [P, NC_, C], F32)
    m.ident = sb("ident", [P, P], F32)
    m.ident16 = sb("ident16", [P, P], F16)
    m.identb = sb("identb", [P, P], BF16)
    m.mask_kq = sb("mask_kq", [P, P], BF16)
    m.mask_qk = sb("mask_qk", [P, P], BF16)
    m.minus_half = sb("minus_half", [P, NT], F32)
    m.xin = sb("xin", [P, NT, C], F32)
    m.x = sb("x", [P, NT, C], F32)
    m.hT = sb("hT", [P, NC_, T], F16)
    m.lT = sb("lT", [P, NC_, T], F16)
    m.o = sb("o", [P, NT, C], F32)
    m.qa = sb("qa", [P, NH, T], F16)
    m.qb = sb("qb", [P, NH, T], F16)
    m.qc = sb("qc", [P, NH, T], F16)
    m.ka0 = sb("ka0", [P, NH, T], F16)
    m.kc = sb("kc", [P, NH, T], F16)
    m.v = sb("v", [P, NT, NH, VW], F16)
    m.p32 = sb("p32", [P, RING, 2, BANK], F32)
    m.ph = sb("ph", [P, RING, 2, BANK], F16)
    m.pl = sb("pl", [P, RING, 2, BANK], F16)
    m.stats = sb("stats", [P, NT, 6], F32)
    m.mv = sb("mv", [P, NT, 2], F32)
    m.gstats = sb("gstats", [P, 2, 6], F32)
    m.gmv = sb("gmv", [P, NC_, 2], F32)
    m.small = sb("small", [P, 6, NT], F32)
    m.ln = sb("ln", [P, 3, NT], F32)
    m.rowt = sb("rowt", [NT, P], F16)
    m.mxp = sb("mxp", [P, 2, 2, NT], F32)
    m.nm = sb("nm", [P, 2, NT], F16)
    m.rs = sb("rs", [P, 2, 4], F32)
    m.ps = ctx.enter_context(nc.psum_tensor("ps", [P, 8, BANK], F32))


class Stage:

    def __init__(self, nc, ctx, name, sems):
        self.nc, self.ctx, self.name = nc, ctx, name
        self.sems = [ctx.enter_context(nc.semaphore(f"{name}_{s}")) for s in sems]

    def __enter__(self):
        self.inner = ExitStack()
        return (self.inner.enter_context(self.nc.Block()), *self.sems)

    def __exit__(self, *a):
        return self.inner.__exit__(*a)


def constants(nc, ctx, m, d, stored):
    stage = [m.o[:, 0:3, :], m.o[:, 3:6, :],
             m.p32[:, 0:2, :, :].rearrange("p a b c -> p (a b c)")[:, 0:3 * C].rearrange("p (a b) -> p a b", a=3),
             m.x[:, 0:3, :], m.x[:, 3:6, :]]
    NS = len(stage)
    pieces = []
    w0 = d.qkv_w.rearrange("(k p) n -> p k n", p=P)
    for k in range(NC_):
        pieces.append((w0[:, k, :].rearrange("p (a b) -> p a b", a=3), m.wqkv_hi[0][:, k, :].rearrange("p (a b) -> p a b", a=3),
                       m.wqkv_lo[0][:, k, :].rearrange("p (a b) -> p a b", a=3)))
    for i, w in enumerate((d.wq, d.wk, d.wv)):
        pieces.append((w.rearrange("(k p) n -> p k n", p=P), m.wqkv_hi[1][:, :, i * C:(i + 1) * C], m.wqkv_lo[1][:, :, i * C:(i + 1) * C]))
    for n, w in enumerate((d.proj_w, d.wo)):
        pieces.append((w.rearrange("(k p) n -> p k n", p=P), m.wo_hi[n][:, :, :], m.wo_lo[n][:, :, :]))

    rel2 = m.ph[:, 0, :, :].rearrange("p a b -> p (a b)").bitcast(F32)[0:NREL, 0:4 * HD].rearrange("p (a b) -> p a b", a=4)
    anti = m.ph[:, 1, :, :].rearrange("p a b -> p (a b)").bitcast(F32)[0:NREL, 0:NREL]
    c1in = m.pl[:, 0, :, :].rearrange("p a b -> p (a b)").bitcast(F32)[:, 0:NF * FA].rearrange("p (a b) -> p a b", a=NF)
    cpin = m.hT[:, :, :].rearrange("p a b -> p (a b)").bitcast(F32)[0:FA, 0:FF]
    relf = m.pl[:, 1, :, :].rearrange("p a b -> p (a b)").bitcast(F32)[:, 0:2 * NREL].rearrange("p (a b) -> p a b", a=2)
    c1f = m.lT[:, :, :].rearrange("p a b -> p (a b)").bitcast(F32)[0:FA, 0:FF]

    loads = [ctx.enter_context(nc.semaphore(f"const_load{i}")) for i in range(NS)]
    st = Stage(nc, ctx, "const", ["tables_in", "biases_in", "hi_done", "lo_done", "filled", "shaped", "rel_mm", "rel_out", "rel_hi", "c1_mm",
                                  "c1_out", "c1_hi", "cp_mm", "cp_out"])
    with st as (block, tables_in, biases_in, hi_done, lo_done, filled, shaped, rel_mm, rel_out, rel_hi, c1_mm, c1_out, c1_hi, cp_mm, cp_out):
        @block.sync
        def _(sp):
            sp.sem_inc(stored, STORES)
            for i, r in enumerate((d.rel_h, d.rel_h, d.rel_w, d.rel_w)):
                sp.dma_start(rel2[:, i, :], r).then_inc(tables_in, 16)
            sp.dma_start(c1in, d.c_fc_1.rearrange("(i p) a -> p i a", p=P)).then_inc(tables_in, 16)
            sp.dma_start(cpin, d.c_proj_1).then_inc(tables_in, 16)
            for i, (src, _, _) in enumerate(pieces):
                if i >= NS:
                    sp.wait_ge(lo_done, i - NS + 1)
                sp.dma_start(stage[i % NS], src).then_inc(loads[i % NS], 16)

        @block.scalar
        def _(act):
            act.dma_start(m.bqk[:, :], d.qkv_b[0:2 * C].rearrange("(m p) -> p m", p=P), allow_slow_non_contiguous=True).then_inc(biases_in, 16)
            for dst, src in ((m.bv, d.qkv_b[2 * C:3 * C]), (m.bo[0], d.proj_b), (m.bo[1], d.bo),
                             (m.cf2, d.c_fc_2.rearrange("a b -> (a b)")), (m.cp2, d.c_proj_2.rearrange("a b -> (a b)"))):
                act.dma_start(dst[:, :], src.partition_broadcast(P)).then_inc(biases_in, 16)
            act.dma_start(m.xin[:, :, :], d.x_tiles[0]).then_inc(biases_in, 16)
            for i, (_, hi, _) in enumerate(pieces):
                act.wait_ge(loads[i % NS], 16 * (i // NS + 1))
                nc.scalar.activation(hi, stage[i % NS], ACT.Copy).then_inc(hi_done, 1)
            act.wait_ge(cp_mm, NF)
            nc.scalar.activation(m.cp[:, :, :], m.ps[:, 4, 0:NF * FA].rearrange("p (a b) -> p a b", a=NF), ACT.Copy).then_inc(cp_out, 1)
            act.wait_ge(c1_mm, NF)
            nc.scalar.activation(c1f, m.ps[0:FA, 1:4, :].rearrange("p a b -> p (a b)"), ACT.Copy).then_inc(c1_out, 1)
            act.wait_ge(biases_in, 16 * 7)

        @block.vector
        def _(dve):
            for i, (_, hi, lo) in enumerate(pieces):
                dve.wait_ge(hi_done, i + 1)
                nc.vector.tensor_tensor(lo, stage[i % NS], hi, ALU.subtract).then_inc(lo_done, 1)
            dve.wait_ge(rel_mm, 2)
            nc.vector.tensor_scalar(relf, m.ps[:, 0, 0:2 * NREL].rearrange("p (a b) -> p a b", a=2), 1.0 / SCALE, None, ALU.mult).then_inc(rel_out, 1)
            dve.wait_ge(rel_out, 1)
            nc.vector.tensor_copy(m.rel_hi[:, :, :], relf).then_inc(rel_hi, 1)
            dve.wait_ge(rel_hi, 1)
            nc.vector.tensor_tensor(m.rel_lo[:, :, :], relf, m.rel_hi[:, :, :], ALU.subtract)
            dve.wait_ge(c1_out, 1)
            nc.vector.tensor_copy(m.c1[0:FA, :], c1f).then_inc(c1_hi, 1)
            nc.vector.tensor_copy(m.c1[FA:2 * FA, :], c1f)
            dve.wait_ge(c1_hi, 1)
            nc.vector.tensor_tensor(m.c1[2 * FA:3 * FA, :], c1f, m.c1[0:FA, :], ALU.subtract)
            dve.wait_ge(biases_in, 16 * 7)
            dve.wait_ge(shaped, 1)
            nc.vector.tensor_tensor(m.spread[:, :].rearrange("p (a b) -> p a b", b=FB), m.spread[:, :].rearrange("p (a b) -> p a b", b=FB),
                                    m.cp2[:, :].unsqueeze(1).broadcast_to([P, FA, FB]), ALU.mult)

        @block.gpsimd
        def _(pool):
            count = [0]

            def fill(ap, value):
                nc.gpsimd.memset(ap, value).then_inc(filled, 1)
                count[0] += 1
                pool.wait_ge(filled, count[0])

            def carve(ap, op, fill_value, base, pattern, mult):
                nc.gpsimd.affine_select(out=ap, in_=ap, compare_op=op, fill=fill_value, base=base, pattern=pattern,
                                        channel_multiplier=mult).then_inc(filled, 1)
                count[0] += 1
                pool.wait_ge(filled, count[0])

            for t in (m.ident[:, :], m.ident16[:, :], m.identb[:, :], anti, m.mask_kq[:, :], m.mask_qk[:, :], m.spread[:, :],
                      m.ka0[:, :, :], m.qc[:, :, :], m.kc[:, :, :]):
                fill(t, 0.0)
            fill(m.group[:, :, :], 1.0 / GC)
            fill(m.minus_half[:, :], -0.5)
            fill(m.v[:, :, :, HD:HD + 1], 1.0)
            for h in range(NH):
                fill(m.kc[mrow(h):mrow(h) + 1, slot(h), :], MSCALE)
            for t in (m.ident[:, :], m.ident16[:, :], m.identb[:, :]):
                carve(t, ALU.not_equal, 1.0, 0, [[-1, P]], 1)
            carve(anti, ALU.not_equal, 1.0, -(NREL - 1), [[1, NREL]], 1)
            carve(m.mask_kq[:, :], ALU.is_ge, MASKED, 0, [[1, P]], -1)
            carve(m.mask_qk[:, :], ALU.is_ge, MASKED, 0, [[-1, P]], 1)
            for k in range(NC_):
                gk = m.group[:, k, :].rearrange("p (g r) -> p g r", r=GC)
                carve(gk, ALU.is_ge, 0.0, k * P, [[-GC, C // GC], [0, GC]], 1)
            for k in range(NC_):
                gk = m.group[:, k, :].rearrange("p (g r) -> p g r", r=GC)
                carve(gk, ALU.is_ge, 0.0, GC - 1 - k * P, [[GC, C // GC], [0, GC]], -1)
            for base_h in (HD, 0):
                s = slice(0, NPAIR) if base_h == HD else slice(NPAIR, NH)
                kh = m.ka0[base_h:base_h + IMG, s, :].rearrange("p s (a b) -> p s a b", a=IMG)
                kw = m.ka0[base_h + IMG:base_h + 2 * IMG, s, :].rearrange("p s (a b) -> p s a b", a=IMG)
                carve(kh, ALU.not_equal, 1.0, 0, [[0, NPAIR], [-1, IMG], [0, IMG]], 1)
                carve(kw, ALU.not_equal, 1.0, 0, [[0, NPAIR], [0, IMG], [-1, IMG]], 1)
            for j in range(4):
                sv = m.spread[j * FA:(j + 1) * FA, :].rearrange("p (a b) -> p a b", b=FB)
                carve(sv, ALU.not_equal, 1.0, 0, [[-1, FA], [0, FB]], 1)
            nc.gpsimd.memset(m.small[:, :, :], 0.0).then_inc(shaped, 1)

        @block.tensor
        def _(pe):
            pe.wait_ge(shaped, 1)
            pe.wait_ge(tables_in, 16 * 6)
            for i in range(2):
                nc.tensor.matmul(m.ps[:, 0, i * NREL:(i + 1) * NREL], rel2[:, 2 * i:2 * i + 2, :].rearrange("p a b -> p (a b)"), anti,
                                 start=True, stop=True).then_inc(rel_mm, 1)
            for i in range(NF):
                nc.tensor.transpose(m.ps[:, 4, i * FA:(i + 1) * FA], cpin[:, i * P:(i + 1) * P], m.ident[0:FA, 0:FA]).then_inc(cp_mm, 1)
            for i in range(NF):
                nc.tensor.transpose(m.ps[0:FA, 1 + i // 4, (i % 4) * P:(i % 4 + 1) * P], c1in[:, i, :], m.ident[:, :]).then_inc(c1_mm, 1)


def semaphores(nc, ctx, prefix, names):
    return {n: ctx.enter_context(nc.semaphore(f"{prefix}_{n}")) for n in names.split()}


def flat(ap):
    return ap.rearrange("p a b -> p (a b)")


class Norm:

    def __init__(self, nc, ctx, m, name):
        self.nc, self.m = nc, m
        self.s = semaphores(nc, ctx, name, "transposed copied stats agg mean_mm mean_out dev dev2 var_mm var_eps rstd shift normed hi lo")
        self.mean_g, self.dev, self.tvar, self.veps, self.rstd, self.shift = (m.small[:, i, 0:NC_] for i in range(6))
        self.xn = m.o[:, :, :].rearrange("p a b -> p (a b)").rearrange("p (a b) -> p a b", a=NC_)

    def transposes(self, pe, n):
        m, c, hf = self.m, n // 2, n % 2
        for t in range(4 * hf, 4 * hf + 4):
            mm = self.nc.tensor.transpose(m.ps[:, n, (t % 4) * P:(t % 4 + 1) * P], m.xin[:, t, c * P:(c + 1) * P], m.ident[:, :])
        mm.then_inc(self.s["transposed"], 1)

    def copy(self, act, n):
        act.wait_ge(self.s["transposed"], n + 1)
        self.nc.scalar.activation(self.xn[:, n // 2, (n % 2) * BANK:(n % 2 + 1) * BANK], self.m.ps[:, n, :], ACT.Copy).then_inc(self.s["copied"], 1)

    def stats(self, dve, c):
        nc, m, s = self.nc, self.m, self.s
        dve.wait_ge(s["copied"], 2 * c + 2)
        for j in range(2):
            nc.vector.bn_stats(m.gstats[:, j, :], self.xn[:, c, j * BANK:(j + 1) * BANK]).then_inc(s["stats"], 1)
        dve.wait_ge(s["stats"], 2 * (c + 1))
        nc.vector.bn_aggr(m.gmv[:, c, :], m.gstats[:, :, :]).then_inc(s["agg"], 1)
        dve.wait_ge(s["agg"], c + 1)

    def average(self, pe, bank, value, ready, count, done):
        pe.wait_ge(ready, count)
        for i in range(NC_):
            for k in range(NC_):
                mm = self.nc.tensor.matmul(self.m.ps[:, bank, i:i + 1], self.m.group[:, k, i * P:(i + 1) * P], value(k),
                                           start=(k == 0), stop=(k == NC_ - 1))
        mm.then_inc(done, 1)

    def means(self, pe, bank):
        self.average(pe, bank, lambda k: self.m.gmv[:, k, 0:1], self.s["agg"], NC_, self.s["mean_mm"])

    def deviations(self, dve, bank):
        nc, s, m = self.nc, self.s, self.m
        dve.wait_ge(s["mean_mm"], 1)
        nc.vector.tensor_copy(self.mean_g, m.ps[:, bank, 0:NC_]).then_inc(s["mean_out"], 1)
        dve.wait_ge(s["mean_out"], 1)
        nc.vector.tensor_tensor(self.dev, m.gmv[:, :, 0], self.mean_g, ALU.subtract).then_inc(s["dev"], 1)
        dve.wait_ge(s["dev"], 1)
        nc.vector.tensor_tensor(self.tvar, self.dev, self.dev, ALU.mult).then_inc(s["dev"], 1)
        dve.wait_ge(s["dev"], 2)
        nc.vector.tensor_tensor(self.tvar, self.tvar, m.gmv[:, :, 1], ALU.add).then_inc(s["dev2"], 1)

    def variances(self, pe, bank):
        self.average(pe, bank, lambda k: self.tvar[:, k:k + 1], self.s["dev2"], 1, self.s["var_mm"])

    def eps(self, dve, bank):
        dve.wait_ge(self.s["var_mm"], 1)
        self.nc.vector.tensor_scalar(self.veps, self.m.ps[:, bank, 0:NC_], 1e-5, None, ALU.add).then_inc(self.s["var_eps"], 1)

    def root(self, pool):
        pool.wait_ge(self.s["var_eps"], 1)
        self.nc.gpsimd.tensor_tensor(self.rstd, self.veps, self.m.minus_half[:, 0:NC_], ALU.pow).then_inc(self.s["rstd"], 1)

    def normalise(self, dve):
        nc, s = self.nc, self.s
        dve.wait_ge(s["rstd"], 1)
        nc.vector.scalar_tensor_tensor(self.shift, self.mean_g, -1.0, self.rstd, ALU.mult, ALU.mult).then_inc(s["shift"], 1)
        dve.wait_ge(s["shift"], 1)
        for c in range(NC_):
            nc.vector.tensor_scalar(self.xn[:, c, :], self.xn[:, c, :], self.rstd[:, c:c + 1], self.shift[:, c:c + 1],
                                    ALU.mult, ALU.add).then_inc(s["normed"], 1)

    def high(self, act, c):
        act.wait_ge(self.s["normed"], c + 1)
        self.nc.scalar.activation(self.m.hT[:, c, :], self.xn[:, c, :], ACT.Copy).then_inc(self.s["hi"], 1)

    def low(self, eng, engine, c):
        eng.wait_ge(self.s["hi"], c + 1)
        engine.tensor_tensor(self.m.lT[:, c, :], self.xn[:, c, :], self.m.hT[:, c, :], ALU.subtract).then_inc(self.s["lo"], 1)


def first_norm(nc, ctx, m, norm):
    with nc.Block() as block:
        @block.tensor
        def _(pe):
            for n in range(2 * NC_):
                norm.transposes(pe, n)
            norm.means(pe, 6)
            norm.variances(pe, 7)

        @block.scalar
        def _(act):
            for n in range(2 * NC_):
                norm.copy(act, n)
            for c in range(NC_):
                norm.high(act, c)

        @block.vector
        def _(dve):
            for c in range(NC_):
                norm.stats(dve, c)
            norm.deviations(dve, 6)
            norm.eps(dve, 7)
            norm.normalise(dve)

        @block.gpsimd
        def _(pool):
            norm.root(pool)
            for c in range(NC_):
                norm.low(pool, nc.gpsimd, c)


class Projections:

    def __init__(self, nc, ctx, m, layer):
        self.nc, self.m, self.layer = nc, m, layer
        self.s = semaphores(nc, ctx, f"qkv{layer}", "mm hi lo rel_mm rel_hi rel_lo v_mm v32 v_hi v_lo")
        self.wh, self.wl = m.wqkv_hi[layer], m.wqkv_lo[layer]
        self.ka = m.ka0 if layer == 0 else m.qb
        self.bank = (0, 2, 4, 6, 4, 6) if layer == 0 else (0, 2, 4, 6, 0, 2)

    def out2(self, i):
        return flat(self.m.ps[:, self.bank[i]:self.bank[i] + 2, :])

    def pair_products(self, pe, i, input_ready=None):
        nc, m, s = self.nc, self.m, self.s
        if i >= 4:
            pe.wait_ge(s["lo"], 2 * (i - 2 + 1) if self.layer == 0 else 2 * (i - 4 + 1))
        steps = [(w, x, k) for k in range(NC_) for w, x in ((self.wh, m.hT), (self.wh, m.lT), (self.wl, m.hT))]
        if input_ready is None:
            order = [(n, j) for n in range(len(steps)) for j in range(2)]
        else:
            order = [(n, j) for j in range(2) for n in range(len(steps))]
        for n, j in order:
            w, x, k = steps[n]
            if input_ready is not None and n % 3 == 0:
                input_ready(pe, j, k)
            mm = nc.tensor.matmul(m.ps[:, self.bank[i] + j, :], w[:, k, i * P:(i + 1) * P], x[:, k, j * BANK:(j + 1) * BANK],
                                  start=(n == 0), stop=(n == len(steps) - 1))
        mm.then_inc(s["mm"], 1)

    def pair_high(self, act, i):
        nc, m, s = self.nc, self.m, self.s
        act.wait_ge(s["mm"], i + 1)
        for e in range(2):
            h = 2 * (i % NPAIR) + e
            dst = m.qa if i < NPAIR else self.ka
            if self.layer == 0:
                nc.scalar.activation(dst[own(h), slot(h), :], self.out2(i)[own(h), :], ACT.Identity, bias=m.bqk[own(h), i:i + 1]).then_inc(s["hi"], 1)
            else:
                nc.scalar.activation(dst[own(h), slot(h), :], self.out2(i)[own(h), :], ACT.Copy).then_inc(s["hi"], 1)

    def pair_low(self, dve, i):
        nc, m, s, layer = self.nc, self.m, self.s, self.layer
        for e in range(2):
            h = 2 * (i % NPAIR) + e
            is_q = i < NPAIR
            src = m.qa if is_q else self.ka
            if layer == 0:
                dst = m.qb[own(h), slot(h), :] if is_q else m.kc[own(h), slot(h), :]
            else:
                dst = m.qa[other(h), slot(h), :] if is_q else m.kc[own(h), slot(h), :]
            dve.wait_ge(s["hi"], 2 * i + e + 1)
            if layer == 0:
                last = nc.vector.scalar_tensor_tensor(dst, self.out2(i)[own(h), :], m.bqk[own(h), i:i + 1], src[own(h), slot(h), :],
                                                      ALU.add, ALU.subtract)
            else:
                last = nc.vector.tensor_tensor(dst, self.out2(i)[own(h), :], src[own(h), slot(h), :], ALU.subtract)
            if is_q:
                last = nc.vector.tensor_copy(m.qc[own(h), slot(h), :], src[own(h), slot(h), :])
            elif layer == 1:
                last = nc.vector.tensor_copy(self.ka[other(h), slot(h), :], src[own(h), slot(h), :])
            last.then_inc(s["lo"], 1)

    def rel_base(self, parity, axis):
        return (HD if parity == 0 else 0) + IMG * axis

    def rel_products(self, pe, chunk):
        nc, m, s = self.nc, self.m, self.s
        if chunk == 0:
            pe.wait_ge(s["lo"], 2 * NPAIR)
        else:
            pe.wait_ge(s["rel_lo"], 4 * NPAIR)
        half = IMG // 2
        for at in range(half):
            pos = chunk * half + at
            for axis in range(2):
                for parity in range(2):
                    rows = own(parity)
                    b = self.rel_base(parity, axis)
                    o = m.ps[b:b + IMG, at // 4, (at % 4) * NPAIR * IMG:(at % 4 + 1) * NPAIR * IMG].rearrange("p (s w) -> p s w", s=NPAIR)
                    sl = slice(parity * NPAIR, (parity + 1) * NPAIR)

                    def queries(buf):
                        full = buf[rows, sl, :].rearrange("p s (h w) -> p s h w", h=IMG)
                        return full[:, :, pos, :] if axis == 0 else full[:, :, :, pos]
                    t0 = IMG - 1 - pos
                    steps = ((m.rel_hi, m.qa), (m.rel_hi, m.qb), (m.rel_lo, m.qa))
                    for n, (r, q) in enumerate(steps):
                        mm = nc.tensor.matmul(o, r[rows, axis, t0:t0 + IMG], queries(q), start=(n == 0), stop=(n == len(steps) - 1))
        mm.then_inc(s["rel_mm"], 1)

    def rel_views(self, chunk, n, buf):
        m, half = self.m, IMG // 2
        pair, parity, axis = n // 4, n // 2 % 2, n % 2
        b = self.rel_base(parity, axis)
        src = m.ps[b:b + IMG, 0:4, 0:4 * NPAIR * IMG].rearrange("p k (i s w) -> p k i s w", i=4, s=NPAIR)[:, :, :, pair, :]
        full = buf[b:b + IMG, parity * NPAIR + pair, :].rearrange("p (h w) -> p h w", h=IMG)
        if axis == 0:
            return src, full[:, chunk * half:(chunk + 1) * half, :].rearrange("p (k i) w -> p k i w", i=4)
        return src, full[:, :, chunk * half:(chunk + 1) * half].rearrange("p h (k i) -> p k i h", i=4)

    def rel_high(self, act, chunk, n):
        r = chunk * 4 * NPAIR + n
        act.wait_ge(self.s["rel_mm"], chunk + 1)
        if r >= 4:
            act.wait_ge(self.s["rel_lo"], r - 3)
        src, dst = self.rel_views(chunk, n, self.m.qa)
        self.nc.scalar.activation(dst, src, ACT.Copy).then_inc(self.s["rel_hi"], 1)

    def rel_low(self, dve, chunk, n):
        r = chunk * 4 * NPAIR + n
        dve.wait_ge(self.s["rel_hi"], r + 1)
        src, hi = self.rel_views(chunk, n, self.m.qa)
        _, lo = self.rel_views(chunk, n, self.m.qb)
        self.nc.vector.tensor_tensor(lo, src, hi, ALU.subtract).then_inc(self.s["rel_lo"], 1)

    def v_products(self, pe, t):
        nc, m, s = self.nc, self.m, self.s
        if t == 0:
            pe.wait_ge(s["lo"], 4 * NPAIR)
        if t >= 2:
            pe.wait_ge(s["v32"], t - 1)
        steps = [(x, w, k) for k in range(NC_) for x, w in ((m.hT, self.wh), (m.hT, self.wl), (m.lT, self.wh))]
        for n, (x, w, k) in enumerate(steps):
            mm = nc.tensor.matmul(m.ps[:, 6 + t % 2, 0:C], x[:, k, t * P:(t + 1) * P], w[:, k, 2 * C:3 * C],
                                  start=(n == 0), stop=(n == len(steps) - 1))
        mm.then_inc(s["v_mm"], 1)

    def v_sum(self, dve, t):
        nc, m, s = self.nc, self.m, self.s
        dve.wait_ge(s["v_mm"], t + 1)
        if self.layer == 0:
            nc.vector.tensor_tensor(m.o[:, t, :], m.ps[:, 6 + t % 2, 0:C], m.bv[:, :], ALU.add).then_inc(s["v32"], 1)
        else:
            nc.vector.tensor_copy(m.o[:, t, :], m.ps[:, 6 + t % 2, 0:C]).then_inc(s["v32"], 1)

    def v_high(self, act, t):
        act.wait_ge(self.s["v32"], t + 1)
        self.nc.scalar.activation(self.m.v[:, t, :, 0:HD], self.m.o[:, t, :].rearrange("p (h d) -> p h d", d=HD), ACT.Copy).then_inc(self.s["v_hi"], 1)

    def v_low(self, pool, t):
        pool.wait_ge(self.s["v_hi"], t + 1)
        self.nc.gpsimd.tensor_tensor(self.m.v[:, t, :, HD + 1:VW], self.m.o[:, t, :].rearrange("p (h d) -> p h d", d=HD), self.m.v[:, t, :, 0:HD],
                                     ALU.subtract).then_inc(self.s["v_lo"], 1)


class Attention:

    def __init__(self, nc, ctx, m, layer, proj):
        self.nc, self.m, self.layer, self.proj = nc, m, layer, proj
        self.s = semaphores(nc, ctx, f"attn{layer}", "scores exp hi_act hi_pool pl_dve pl_pool pv use free reduced combined nm row recip out ot_hi")
        self.ka = m.ka0 if layer == 0 else m.qb
        self.causal = layer == 1
        if self.causal:
            self.groups = [(hf, kt, max(hf * BANK, kt * P)) for hf in range(2) for kt in range(0, 4 * (hf + 1), 2)]
            self.tiles = [(qt, kh, min(BANK, (qt + 1) * P - kh * BANK)) for qt in range(NT) for kh in range(2) if (qt + 1) * P > kh * BANK]
            self.both = slice(4, NT)
        else:
            self.groups = [(hf, kt, hf * BANK) for hf in range(2) for kt in range(0, NT, 2)]
            self.tiles = [(qt, kh, BANK) for qt in range(NT) for kh in range(2)]
            self.both = slice(0, NT)
        G = self.NG = len(self.groups)
        self.NTL = len(self.tiles)
        self.N = NH * G
        self.last_of_half = {g for g in range(G) if g == G - 1 or self.groups[g + 1][0] != self.groups[g][0]}
        self.prologue = [("max", 0, n) for n in range(self.NTL)]
        steps = [[] for _ in range(self.N)]
        steps[0].append(("row", 0))
        for h in range(1, NH):
            begin, end = max(0, (h - 1) * G - ROW_LEAD), h * G - ROW_LEAD
            if h > 1:
                steps[begin].append(("row", h - 1))
            for n in range(self.NTL):
                steps[begin + n * (end - begin) // self.NTL].append(("max", h, n))
        steps[(NH - 1) * G - ROW_LEAD].append(("row", NH - 1))
        for c in range(NC_ - 1):
            for hf in range(2):
                steps[(2 * c + 2) * G + LAG + 1 + hf].append(("ot", c, hf))
        self.uses_at = steps
        self.tail = [("ot", NC_ - 1, hf) for hf in range(2)]
        self.index = {}
        for u in self.prologue + [u for st in steps for u in st] + self.tail:
            self.index[u] = len(self.index)
        assert steps[0][0] == ("row", 0)

    def even(self, i):
        return i % 2 == 0

    def wait_hi(self, eng, i):
        eng.wait_ge(self.s["hi_act"] if self.even(i) else self.s["hi_pool"], i // 2 + 1)

    def wait_lo(self, eng, i):
        eng.wait_ge(self.s["pl_pool"] if self.even(i) else self.s["pl_dve"], i // 2 + 1)

    def cols(self, i):
        hf, _, q0 = self.groups[i % self.NG]
        return (hf + 1) * BANK - q0

    def bank(self, u):
        return 4 + self.index[u] % 2

    def use(self, pe, u):
        nc, m, s, r = self.nc, self.m, self.s, self.index[u]
        if r >= 2:
            pe.wait_ge(s["free"], r - 1)
        bank = self.bank(u)
        if u[0] == "max":
            _, h, n = u
            qt, kh, w = self.tiles[n]
            sl = slot(h)
            diag = self.causal and (qt + 1) * P - kh * BANK <= BANK
            if diag:
                nc.tensor.matmul(m.ps[:, bank, w - P:w], m.identb[:, :], m.mask_qk[:, :], start=True, stop=False, skip_group_check=True)
            mm = nc.tensor.matmul(m.ps[:, bank, 0:w], m.qa[:, sl, qt * P:(qt + 1) * P], self.ka[:, sl, kh * BANK:kh * BANK + w],
                                  start=not diag, stop=True, skip_group_check=True)
        elif u[0] == "row":
            _, h = u
            pe.wait_ge(s["nm"], h + 1)
            mm = nc.tensor.transpose(m.ps[0:NT, bank, 0:P // 2].bitcast(F16), m.nm[:, h % 2, :], m.ident16[:, :])
        else:
            _, c, hf = u
            pe.wait_ge(s["out"], 4 * (c + 1))
            for t in range(4 * hf, 4 * hf + 4):
                mm = nc.tensor.transpose(m.ps[:, bank, (t % 4) * P:(t % 4 + 1) * P], m.o[:, t, c * P:(c + 1) * P], m.ident[:, :])
        mm.then_inc(s["use"], 1)

    def score_tiles(self, pe, i):
        nc, m, s = self.nc, self.m, self.s
        h, g = i // self.NG, i % self.NG
        hf, kt0, q0 = self.groups[g]
        w = self.cols(i)
        sl = slot(h)
        if i >= 2:
            pe.wait_ge(s["exp"], i - 1)
        q = slice(q0, q0 + w)
        outs = [m.ps[:, 2 * (i % 2) + j, 0:w] for j in range(2)]
        keys = [slice((kt0 + j) * P, (kt0 + j + 1) * P) for j in range(2)]
        for j in range(2):
            nc.tensor.matmul(outs[j], self.ka[:, sl, keys[j]], m.qa[:, sl, q], start=True, stop=False)
            if self.layer == 0:
                nc.tensor.matmul(outs[j], self.ka[:, sl, keys[j]], m.qb[:, sl, q], start=False, stop=False)
            d0 = (kt0 + j) * P - q0
            if self.causal and 0 <= d0 < w:
                nc.tensor.matmul(outs[j][:, d0:d0 + P], m.identb[:, :], m.mask_kq[:, :], start=False, stop=False, skip_group_check=True)
        if g == 0:
            pe.wait_ge(s["row"], 16 * (h + 1))
        for j in range(2):
            mm = nc.tensor.matmul(outs[j], m.kc[crows(h), sl, keys[j]], m.qc[crows(h), sl, q], start=False, stop=True)
        mm.then_inc(s["scores"], 1)

    def weighted_values(self, pe, i):
        nc, m, s = self.nc, self.m, self.s
        h, g = i // self.NG, i % self.NG
        hf, kt0, q0 = self.groups[g]
        half = 2 * h + hf
        first = g == 0 or self.groups[g - 1][0] != hf
        if i == 0:
            pe.wait_ge(self.proj.s["v_lo"], NT)
        if first and half >= 2:
            pe.wait_ge(s["out"], half - 1)
        self.wait_hi(pe, i)
        self.wait_lo(pe, i)
        work = []
        for j in range(2):
            kt = kt0 + j
            for qt in range(q0 // P, 4 * (hf + 1)):
                if self.causal and qt < kt:
                    continue
                c0 = (qt - hf * 4) * (HD + 1)
                e0 = qt * P - q0
                hi_p = m.ph[:, i % RING, j, e0:e0 + P]
                lo_p = m.pl[:, i % RING, j, e0:e0 + P]
                work += [(c0, HD + 1, hi_p, m.v[:, kt, h, 0:HD + 1]), (c0, HD, hi_p, m.v[:, kt, h, HD + 1:VW]),
                         (c0, HD + 1, lo_p, m.v[:, kt, h, 0:HD + 1])]
        for n, (c0, w, e, v) in enumerate(work):
            mm = nc.tensor.matmul(m.ps[:, 6 + half % 2, c0:c0 + w], e, v, start=(first and n == 0),
                                  stop=(g in self.last_of_half and n == len(work) - 1), skip_group_check=True)
        mm.then_inc(s["pv"], 1)

    def tensor(self, pe, between):
        for i in range(self.N + LAG):
            if i < self.N:
                if i == 0:
                    self.use(pe, ("row", 0))
                self.score_tiles(pe, i)
                for u in self.uses_at[i]:
                    if u != ("row", 0):
                        self.use(pe, u)
            else:
                between(i - self.N)
            if i >= LAG:
                self.weighted_values(pe, i - LAG)
        for u in self.tail:
            self.use(pe, u)

    def high_part(self, eng, i, copy, sem):
        m, w = self.m, self.cols(i)
        eng.wait_ge(self.s["exp"], i + 1)
        if i >= RING:
            eng.wait_ge(self.s["pv"], i - RING + 1)
        copy(m.ph[:, i % RING, :, 0:w], m.p32[:, i % RING, :, 0:w]).then_inc(sem, 1)

    def ot_high(self, act, u):
        _, c, hf = u
        act.wait_ge(self.s["use"], self.index[u] + 1)
        self.nc.scalar.activation(self.m.hT[:, c, hf * BANK:(hf + 1) * BANK], self.m.ps[:, self.bank(u), :], ACT.Copy).then_inc(self.s["ot_hi"], 1)

    def scalar(self, act):
        nc, m, s = self.nc, self.m, self.s
        for i in range(self.N):
            w = self.cols(i)
            act.wait_ge(s["scores"], i + 1)
            if i >= RING:
                self.wait_lo(act, i - RING)
            nc.scalar.activation(m.p32[:, i % RING, :, 0:w], m.ps[:, 2 * (i % 2):2 * (i % 2) + 2, 0:w], ACT.Exp, scale=SCALE).then_inc(s["exp"], 1)
            if self.even(i):
                self.high_part(act, i, lambda out, in_: nc.scalar.activation(out, in_, ACT.Copy), s["hi_act"])
            for u in self.uses_at[i]:
                if u[0] == "ot":
                    self.ot_high(act, u)
        for u in self.tail:
            self.ot_high(act, u)

    def release(self, dve, u):
        nc, m, s, r = self.nc, self.m, self.s, self.index[u]
        bank = self.bank(u)
        if u[0] == "max":
            _, h, n = u
            qt, kh, w = self.tiles[n]
            dve.wait_ge(s["use"], r + 1)
            nc.vector.reduce_max(m.mxp[:, h % 2, kh, qt:qt + 1], m.ps[:, bank, 0:w], AX.X).then_inc(s["free"], 1)
            if n == self.NTL - 1:
                self.combine(dve, h)
        elif u[0] == "row":
            _, h = u
            dve.wait_ge(s["use"], r + 1)
            if h >= 1:
                dve.wait_ge(s["row"], 16 * h)
            nc.vector.tensor_copy(m.rowt[:, :], m.ps[0:NT, bank, 0:P // 2].bitcast(F16)).then_inc(s["free"], 1)
        else:
            _, c, hf = u
            dve.wait_ge(s["ot_hi"], 2 * c + hf + 1)
            half = slice(hf * BANK, (hf + 1) * BANK)
            nc.vector.tensor_tensor(m.lT[:, c, half], m.ps[:, bank, :], m.hT[:, c, half], ALU.subtract).then_inc(s["free"], 1)

    def combine(self, dve, h):
        nc, m, s, both = self.nc, self.m, self.s, self.both
        dve.wait_ge(s["free"], self.index[("max", h, self.NTL - 1)] + 1)
        nc.vector.tensor_tensor(m.mxp[:, h % 2, 0, both], m.mxp[:, h % 2, 0, both], m.mxp[:, h % 2, 1, both], ALU.max).then_inc(s["combined"], 1)
        dve.wait_ge(s["combined"], h + 1)
        nc.vector.tensor_scalar(m.nm[:, h % 2, :], m.mxp[:, h % 2, 0, :], -1.0 / MSCALE, None, ALU.mult).then_inc(s["nm"], 1)

    def low_part(self, eng, engine, i, sem):
        m, w = self.m, self.cols(i)
        self.wait_hi(eng, i)
        if i >= RING:
            eng.wait_ge(self.s["pv"], i - RING + 1)
        engine.tensor_tensor(m.pl[:, i % RING, :, 0:w], m.p32[:, i % RING, :, 0:w], m.ph[:, i % RING, :, 0:w], ALU.subtract).then_inc(sem, 1)

    def normalise(self, dve, i):
        nc, m, s = self.nc, self.m, self.s
        h, g = i // self.NG, i % self.NG
        hf = self.groups[g][0]
        half = 2 * h + hf
        acc = m.ps[:, 6 + half % 2, 0:4 * (HD + 1)].rearrange("p (t c) -> p t c", c=HD + 1)
        dve.wait_ge(s["pv"], i + 1)
        if half == 0:
            dve.wait_ge(self.proj.s["v_lo"], NT)
        nc.vector.reciprocal(m.rs[:, half % 2, :], acc[:, :, HD]).then_inc(s["recip"], 1)
        dve.wait_ge(s["recip"], half + 1)
        nc.vector.tensor_tensor(m.o[:, hf * 4:(hf + 1) * 4, h * HD:(h + 1) * HD], acc[:, :, 0:HD],
                                m.rs[:, half % 2, :].unsqueeze(2).broadcast_to([P, 4, HD]), ALU.mult).then_inc(s["out"], 1)

    def vector(self, dve):
        for i in range(self.N + LAG):
            uses = self.uses_at[i] if i < self.N else []
            for u in uses:
                if u[0] != "ot":
                    self.release(dve, u)
            if 1 <= i <= self.N and not self.even(i - 1):
                self.low_part(dve, self.nc.vector, i - 1, self.s["pl_dve"])
            for u in uses:
                if u[0] == "ot":
                    self.release(dve, u)
            if i >= LAG and (i - LAG) % self.NG in self.last_of_half:
                self.normalise(dve, i - LAG)
        for u in self.tail:
            self.release(dve, u)

    def gpsimd(self, pool):
        nc = self.nc
        for i in range(self.N):
            if self.even(i):
                self.low_part(pool, nc.gpsimd, i, self.s["pl_pool"])
            else:
                self.high_part(pool, i, lambda out, in_: nc.gpsimd.tensor_scalar(out, in_, 1.0, 0.0, ALU.mult, ALU.add), self.s["hi_pool"])

    def sync(self, sp):
        m = self.m
        for h in range(NH):
            sp.wait_ge(self.s["free"], self.index[("row", h)] + 1)
            sp.dma_start(m.qc[mrow(h):mrow(h) + 1, slot(h), :].rearrange("p (a b) -> p a b", a=NT), m.rowt[:, :]).then_inc(self.s["row"], 16)

    def outputs_ready(self, eng, c, hf):
        eng.wait_ge(self.s["free"], self.index[("ot", c, hf)] + 1)


class OutProjection:
    BANKS = (0, 1, 2, 3, 6, 7, 0, 1)

    def __init__(self, nc, ctx, m, layer, attn):
        self.nc, self.m, self.layer, self.attn = nc, m, layer, attn
        self.s = semaphores(nc, ctx, f"proj{layer}", "biased mm added x_free stats mv eps rstd shift normed")
        self.src = m.xin if layer == 0 else m.x

    def bias(self, pool):
        m, src = self.m, self.src
        self.nc.gpsimd.tensor_tensor(src[:, :, :], src[:, :, :], m.bo[self.layer][:, :].unsqueeze(1).broadcast_to([P, NT, C]),
                                     ALU.add).then_inc(self.s["biased"], 1)

    def products(self, pe, t, channels):
        nc, m, a = self.nc, self.m, self.attn
        steps = [(x, w, k) for k in channels for x, w in ((m.hT, m.wo_hi[self.layer]), (m.hT, m.wo_lo[self.layer]), (m.lT, m.wo_hi[self.layer]))]
        if channels[0] == 0:
            a.outputs_ready(pe, 1, t // 4)
            if t < 4:
                pe.wait_ge(a.s["exp"], a.N if t >= 2 else a.N - 1)
            elif t < 6:
                pe.wait_ge(a.s["out"], 2 * NH)
            else:
                pe.wait_ge(self.s["added"], t - 5)
        if channels[-1] == NC_ - 1:
            a.outputs_ready(pe, NC_ - 1, t // 4)
        for n, (x, w, k) in enumerate(steps):
            mm = nc.tensor.matmul(m.ps[:, self.BANKS[t], 0:C], x[:, k, t * P:(t + 1) * P], w[:, k, :],
                                  start=(channels[0] == 0 and n == 0), stop=(channels[-1] == NC_ - 1 and n == len(steps) - 1))
        if channels[-1] == NC_ - 1:
            mm.then_inc(self.s["mm"], 1)

    def between(self, pe):
        def work(step):
            for t in {0: (0, 1), 1: (2, 3)}.get(step, ()):
                self.products(pe, t, range(NC_ - 1))
        return work

    def rest(self, pe):
        for t in range(NT):
            self.products(pe, t, [NC_ - 1] if t < 4 else range(NC_))

    def add(self, dve, t):
        nc, m, s = self.nc, self.m, self.s
        if t == 0:
            dve.wait_ge(s["biased"], 1)
            if self.layer == 0:
                dve.wait_ge(s["x_free"], 1)
        dve.wait_ge(s["mm"], t + 1)
        nc.vector.tensor_tensor(m.x[:, t, :], m.ps[:, self.BANKS[t], 0:C], self.src[:, t, :], ALU.add).then_inc(s["added"], 1)
        dve.wait_ge(s["added"], t + 1)
        nc.vector.bn_stats(m.stats[:, t, :], m.x[:, t, :]).then_inc(s["stats"], 1)
        dve.wait_ge(s["stats"], t + 1)
        nc.vector.bn_aggr(m.mv[:, t, :], m.stats[:, t, :]).then_inc(s["mv"], 1)

    def eps(self, dve, hf):
        dve.wait_ge(self.s["mv"], 4 * (hf + 1))
        t = slice(4 * hf, 4 * hf + 4)
        self.nc.vector.tensor_scalar(self.m.ln[:, 0, t], self.m.mv[:, t, 1], 1e-5, None, ALU.add).then_inc(self.s["eps"], 1)

    def root(self, pool, hf):
        t = slice(4 * hf, 4 * hf + 4)
        pool.wait_ge(self.s["eps"], hf + 1)
        self.nc.gpsimd.tensor_tensor(self.m.ln[:, 1, t], self.m.ln[:, 0, t], self.m.minus_half[:, t], ALU.pow).then_inc(self.s["rstd"], 1)

    def shift(self, dve, hf):
        t = slice(4 * hf, 4 * hf + 4)
        dve.wait_ge(self.s["rstd"], hf + 1)
        self.nc.vector.scalar_tensor_tensor(self.m.ln[:, 2, t], self.m.mv[:, t, 0], -1.0, self.m.ln[:, 1, t], ALU.mult, ALU.mult).then_inc(self.s["shift"], 1)

    def norm(self, act, t, dst):
        act.wait_ge(self.s["shift"], t // 4 + 1)
        self.nc.scalar.activation(dst[:, t, :], self.m.x[:, t, :], ACT.Identity, scale=self.m.ln[:, 1, t:t + 1],
                                  bias=self.m.ln[:, 2, t:t + 1]).then_inc(self.s["normed"], 1)

    def vector(self, dve):
        for t in range(NT):
            self.add(dve, t)
            if t == 3:
                self.eps(dve, 0)
            if t == 5:
                self.shift(dve, 0)
        self.eps(dve, 1)
        self.shift(dve, 1)

    def gpsimd(self, pool):
        for hf in range(2):
            self.root(pool, hf)


class LayerNorm:
    BANKS = ((4, 5, 2), (3, 6, 7))

    def __init__(self, nc, ctx, m, proj):
        self.nc, self.m, self.proj = nc, m, proj
        self.s = semaphores(nc, ctx, "ln", "transposed hi lo")

    def tensor(self, pe):
        m = self.m
        for hf in range(2):
            for c in range(NC_):
                if hf == 0 and c == 2:
                    pe.wait_ge(self.proj.s["added"], 3)
                for t in range(4 * hf, 4 * hf + 4):
                    pe.wait_ge(self.proj.s["normed"], t + 1)
                    mm = self.nc.tensor.transpose(m.ps[:, self.BANKS[hf][c], (t % 4) * P:(t % 4 + 1) * P], m.o[:, t, c * P:(c + 1) * P], m.ident[:, :])
                mm.then_inc(self.s["transposed"], 1)

    def high(self, act, hf, c):
        act.wait_ge(self.s["transposed"], 3 * hf + c + 1)
        self.nc.scalar.activation(self.m.hT[:, c, hf * BANK:(hf + 1) * BANK], self.m.ps[:, self.BANKS[hf][c], :], ACT.Copy).then_inc(self.s["hi"], 1)

    def scalar(self, act):
        for t in range(4):
            self.proj.norm(act, t, self.m.o)
        for c in range(NC_):
            self.high(act, 0, c)
        for t in range(4, NT):
            self.proj.norm(act, t, self.m.o)
        for c in range(NC_):
            self.high(act, 1, c)

    def low(self, dve, hf, c):
        half = slice(hf * BANK, (hf + 1) * BANK)
        dve.wait_ge(self.s["hi"], 3 * hf + c + 1)
        self.nc.vector.tensor_tensor(self.m.lT[:, c, half], self.m.ps[:, self.BANKS[hf][c], :], self.m.hT[:, c, half], ALU.subtract).then_inc(self.s["lo"], 1)

    def vector(self, dve):
        for hf in range(2):
            for c in range(NC_):
                self.low(dve, hf, c)

    def ready(self, pe, j, k):
        pe.wait_ge(self.s["lo"], 3 * j + k + 1)


class FeedForward:
    NHID = RING
    PAIRS = NF // 2

    def __init__(self, nc, ctx, m, proj):
        self.nc, self.m, self.proj = nc, m, proj
        self.s = semaphores(nc, ctx, "ff", "scaled x2 x2_t x2_hi x2_lo up act down each o2 spread added")
        self.y = flat(m.qa[:, :, :]).bitcast(F32).rearrange("p (t c) -> p t c", t=NT)
        self.x2 = m.ph[:, 0, 0, :].bitcast(F32).rearrange("p (t a) -> p t a", t=NT)
        self.stack = m.qb[0:3 * FA, 0, :]
        self.o2 = flat(m.pl[:, 0:2, :, :].rearrange("p r a b -> p r (a b)")).bitcast(F32)

    def scale(self, pool, t):
        pool.wait_ge(self.proj.s["normed"], t + 1)
        y3 = self.y[:, t, :].rearrange("p (a b) -> p a b", b=FB)
        self.nc.gpsimd.tensor_tensor(y3, y3, self.m.cf2[:, :].unsqueeze(1).broadcast_to([P, FA, FB]), ALU.mult).then_inc(self.s["scaled"], 1)

    def reduce(self, dve, t):
        dve.wait_ge(self.s["scaled"], t + 1)
        self.nc.vector.reduce_sum(self.x2[:, t, :], self.y[:, t, :].rearrange("p (a b) -> p a b", b=FB), AX.X).then_inc(self.s["x2"], 1)

    def x2_transposes(self, pe, hf):
        for t in range(4 * hf, 4 * hf + 4):
            pe.wait_ge(self.s["x2"], t + 1)
            mm = self.nc.tensor.transpose(self.m.ps[0:FA, 6 + hf, (t % 4) * P:(t % 4 + 1) * P], self.x2[:, t, :], self.m.ident[:, :])
        mm.then_inc(self.s["x2_t"], 1)

    def x2_high(self, act, hf):
        half = slice(hf * BANK, (hf + 1) * BANK)
        act.wait_ge(self.s["x2_t"], hf + 1)
        for r in (0, 2):
            self.nc.scalar.activation(self.stack[r * FA:(r + 1) * FA, half], self.m.ps[0:FA, 6 + hf, :], ACT.Copy).then_inc(self.s["x2_hi"], 1)

    def x2_low(self, dve, hf):
        half = slice(hf * BANK, (hf + 1) * BANK)
        dve.wait_ge(self.s["x2_hi"], 2 * (hf + 1))
        self.nc.vector.tensor_tensor(self.stack[FA:2 * FA, half], self.m.ps[0:FA, 6 + hf, :], self.stack[0:FA, half], ALU.subtract).then_inc(self.s["x2_lo"], 1)

    def up(self, pe, i):
        m, s = self.m, self.s
        hf, f = i // self.PAIRS, 2 * (i % self.PAIRS)
        if f == 0:
            pe.wait_ge(s["x2_lo"], hf + 1)
        if i >= 2:
            pe.wait_ge(s["act"], i - 1)
        for j in range(2):
            mm = self.nc.tensor.matmul(m.ps[:, 2 * (i % 2) + j, :], m.c1[:, (f + j) * P:(f + j + 1) * P], self.stack[:, hf * BANK:(hf + 1) * BANK],
                                       start=True, stop=True)
        mm.then_inc(s["up"], 1)

    def gelu(self, act, i):
        act.wait_ge(self.s["up"], i + 1)
        if i >= self.NHID:
            act.wait_ge(self.s["each"], i - self.NHID + 1)
        self.nc.scalar.activation(self.m.p32[:, i % self.NHID, :, :], self.m.ps[:, 2 * (i % 2):2 * (i % 2) + 2, :], ACT.Gelu).then_inc(self.s["act"], 1)

    def down(self, pe, i):
        m, s = self.m, self.s
        hf, f = i // self.PAIRS, 2 * (i % self.PAIRS)
        pe.wait_ge(s["act"], i + 1)
        for j in range(2):
            q = (f + j) % 4
            mm = self.nc.tensor.matmul(m.ps[q * FA:(q + 1) * FA, 4 + hf, :], m.cp[:, f + j, :], m.p32[:, i % self.NHID, j, :],
                                       start=(f + j < 4), stop=(f + j >= NF - 4), skip_group_check=True)
        mm.then_inc(s["each"], 1)

    def o2_out(self, dve, hf):
        dve.wait_ge(self.s["each"], self.PAIRS * (hf + 1))
        self.nc.vector.tensor_copy(self.o2[:, hf * BANK:(hf + 1) * BANK], self.m.ps[:, 4 + hf, :]).then_inc(self.s["o2"], 1)

    def spread(self, pe, t):
        if t % 4 == 0:
            pe.wait_ge(self.s["o2"], t // 4 + 1)
        if t >= 2:
            pe.wait_ge(self.s["added"], t - 1)
        self.nc.tensor.matmul(self.m.ps[:, 6 + t % 2, 0:C], self.o2[:, t * P:(t + 1) * P], self.m.spread[:, :], start=True, stop=True).then_inc(self.s["spread"], 1)

    def add(self, dve, t):
        dve.wait_ge(self.s["spread"], t + 1)
        self.nc.vector.tensor_tensor(self.m.x[:, t, :], self.m.ps[:, 6 + t % 2, 0:C], self.m.x[:, t, :], ALU.add).then_inc(self.s["added"], 1)

    def store(self, sp, out_ap, stored):
        for hf in range(2):
            t = slice(4 * hf, 4 * hf + 4)
            sp.wait_ge(self.s["added"], 4 * (hf + 1))
            sp.dma_start(out_ap[:, t, :], self.m.x[:, t, :]).then_inc(stored, 16)


class Dram:
    pass


def build(nc, x, qkv_w, qkv_b, proj_w, proj_b, rel_h, rel_w, wq, wk, wv, wo, bo, c_fc_1, c_fc_2, c_proj_1, c_proj_2, out):
    d = Dram()
    d.qkv_w, d.qkv_b, d.proj_w, d.proj_b, d.rel_h, d.rel_w = qkv_w, qkv_b, proj_w, proj_b, rel_h, rel_w
    d.wq, d.wk, d.wv, d.wo, d.bo = wq, wk, wv, wo, bo
    d.c_fc_1, d.c_fc_2, d.c_proj_1, d.c_proj_2 = c_fc_1, c_fc_2, c_proj_1, c_proj_2
    images = x.shape[0]
    d.x_tiles = x.rearrange("b h w c -> b (h w) c").rearrange("b (t p) c -> b p t c", p=P)
    out_tiles = out.rearrange("b h w c -> b (h w) c").rearrange("b (t p) c -> b p t c", p=P)
    with ExitStack() as ctx:
        m = Mem()
        allocate(nc, ctx, m)
        stored = ctx.enter_context(nc.semaphore("stored"))
        constants(nc, ctx, m, d, stored)
        first_norm(nc, ctx, m, Norm(nc, ctx, m, "gn_first"))
        first = ctx.enter_context(nc.semaphore("loop_first"))
        qkv0 = Projections(nc, ctx, m, 0)
        attn0 = Attention(nc, ctx, m, 0, qkv0)
        proj0 = OutProjection(nc, ctx, m, 0, attn0)
        ln = LayerNorm(nc, ctx, m, proj0)
        qkv1 = Projections(nc, ctx, m, 1)
        attn1 = Attention(nc, ctx, m, 1, qkv1)
        proj1 = OutProjection(nc, ctx, m, 1, attn1)
        ff = FeedForward(nc, ctx, m, proj1)
        norm = Norm(nc, ctx, m, "gn_next")
        next_in = ctx.enter_context(nc.semaphore("next_in"))
        RELS = 4 * NPAIR
        PAIRS = 2 * NPAIR
        with nc.Fori(0, images) as b:
            with nc.Block() as block:
                @block.tensor
                def _(pe):
                    for i in range(4):
                        qkv0.pair_products(pe, i)
                    qkv0.rel_products(pe, 0)
                    for i in range(4, PAIRS):
                        qkv0.pair_products(pe, i)
                    qkv0.rel_products(pe, 1)
                    n0 = 0
                    for t in range(NT):
                        qkv0.v_products(pe, t)
                        if t == 6:
                            pe.wait_ge(qkv0.s["rel_lo"], RELS + 4)
                        want = max(0, t - 5) * attn0.NTL // 2
                        while n0 < want:
                            attn0.use(pe, attn0.prologue[n0])
                            n0 += 1
                    pe.wait_ge(qkv0.s["rel_lo"], 2 * RELS)
                    attn0.tensor(pe, proj0.between(pe))
                    proj0.rest(pe)
                    ln.tensor(pe)
                    for i in range(PAIRS):
                        qkv1.pair_products(pe, i, ln.ready if i == 0 else None)
                    for t in range(NT):
                        qkv1.v_products(pe, t)
                        for n in range(t * attn1.NTL // NT, (t + 1) * attn1.NTL // NT):
                            attn1.use(pe, attn1.prologue[n])
                    attn1.tensor(pe, proj1.between(pe))
                    proj1.rest(pe)
                    pe.wait_ge(next_in, 16)
                    pe.wait_ge(proj1.s["added"], NT)
                    for n in range(2 * NC_):
                        norm.transposes(pe, n)
                    for hf in range(2):
                        ff.x2_transposes(pe, hf)
                    pe.wait_ge(norm.s["copied"], 2 * NC_)
                    for i in range(2 * ff.PAIRS + 1):
                        if i < 2 * ff.PAIRS:
                            ff.up(pe, i)
                        if i >= 1:
                            ff.down(pe, i - 1)
                        if i == ff.PAIRS:
                            norm.means(pe, 7)
                        if i == ff.PAIRS + 2:
                            norm.variances(pe, 7)
                    pe.wait_ge(norm.s["var_eps"], 1)
                    for t in range(NT):
                        ff.spread(pe, t)

                @block.scalar
                def _(act):
                    for i in range(4):
                        qkv0.pair_high(act, i)
                    for n in range(RELS):
                        qkv0.rel_high(act, 0, n)
                    for i in range(4, PAIRS):
                        qkv0.pair_high(act, i)
                    for n in range(RELS):
                        qkv0.rel_high(act, 1, n)
                        if n % 2 == 1 and n >= 3:
                            qkv0.v_high(act, n // 2 - 1)
                    for t in range(RELS // 2 - 1, NT):
                        qkv0.v_high(act, t)
                    attn0.scalar(act)
                    ln.scalar(act)
                    for i in range(PAIRS):
                        qkv1.pair_high(act, i)
                    for t in range(NT):
                        qkv1.v_high(act, t)
                    attn1.scalar(act)
                    for t in range(NT):
                        proj1.norm(act, t, ff.y)
                    for n in range(2 * NC_):
                        norm.copy(act, n)
                    for hf in range(2):
                        ff.x2_high(act, hf)
                    for i in range(2 * ff.PAIRS):
                        ff.gelu(act, i)
                    for c in range(NC_):
                        norm.high(act, c)

                @block.vector
                def _(dve):
                    for i in range(4):
                        qkv0.pair_low(dve, i)
                    for n in range(RELS):
                        qkv0.rel_low(dve, 0, n)
                    for i in range(4, PAIRS):
                        qkv0.pair_low(dve, i)
                    for n in range(RELS):
                        qkv0.rel_low(dve, 1, n)
                        if n % 2 == 1:
                            qkv0.v_sum(dve, n // 2)
                    n0 = 0
                    for t in range(NT):
                        if t >= RELS // 2:
                            qkv0.v_sum(dve, t)
                        want = max(0, t - 5) * attn0.NTL // 2
                        while n0 < want:
                            attn0.release(dve, attn0.prologue[n0])
                            n0 += 1
                    attn0.vector(dve)
                    proj0.vector(dve)
                    ln.vector(dve)
                    for i in range(PAIRS):
                        qkv1.pair_low(dve, i)
                    for t in range(NT):
                        qkv1.v_sum(dve, t)
                        for n in range(t * attn1.NTL // NT, (t + 1) * attn1.NTL // NT):
                            attn1.release(dve, attn1.prologue[n])
                    attn1.vector(dve)
                    proj1.vector(dve)
                    for t in range(NT):
                        ff.reduce(dve, t)
                    for hf in range(2):
                        ff.x2_low(dve, hf)
                    for c in range(NC_):
                        norm.stats(dve, c)
                    norm.deviations(dve, 7)
                    ff.o2_out(dve, 0)
                    norm.eps(dve, 7)
                    norm.normalise(dve)
                    for t in range(NT):
                        if t == 4:
                            ff.o2_out(dve, 1)
                        ff.add(dve, t)

                @block.gpsimd
                def _(pool):
                    proj0.bias(pool)
                    for t in range(NT):
                        qkv0.v_low(pool, t)
                    attn0.gpsimd(pool)
                    proj0.gpsimd(pool)
                    pool.wait_ge(proj0.s["normed"], NT)
                    proj1.bias(pool)
                    for t in range(NT):
                        qkv1.v_low(pool, t)
                    attn1.gpsimd(pool)
                    proj1.gpsimd(pool)
                    for t in range(NT):
                        ff.scale(pool, t)
                    norm.root(pool)
                    for c in range(NC_):
                        norm.low(pool, nc.gpsimd, c)

                @block.sync
                def _(sp):
                    sp.wait_ge(stored, (b + 1) * STORES)
                    sp.sem_inc(proj0.s["x_free"], 1)
                    attn0.sync(sp)
                    sp.wait_ge(proj0.s["added"], NT)
                    sp.dma_start(m.xin[:, :, :], d.x_tiles[(b + 1) % images]).then_inc(next_in, 16)
                    attn1.sync(sp)
                    ff.store(sp, out_tiles[b], stored)
            nc.gpsimd.sem_clear(range(first.num, next_in.num + 1))
            nc.all_engine_barrier()
        with nc.Block() as block:
            @block.sync
            def _(sp):
                sp.wait_ge(stored, (images + 1) * STORES)


_INS = ['x', 'L0_conv_qkv_w', 'L0_conv_qkv_b', 'L0_conv_proj_w', 'L0_conv_proj_b', 'L0_conv_rel_pos_h', 'L0_conv_rel_pos_w',
        'L1_attn_Wq', 'L1_attn_Wk', 'L1_attn_Wv', 'L1_attn_Wo', 'L1_attn_bo', 'L1_ffn_c_fc_1', 'L1_ffn_c_fc_2', 'L1_ffn_c_proj_1',
        'L1_ffn_c_proj_2']


def kernel(**inputs):
    import numpy as _np
    import concourse.bacc as _bacc
    from concourse import mybir as _mybir
    from concourse.bass_utils import run_bass_kernel_spmd as _run

    nc = _bacc.Bacc("TRN2", target_bir_lowering=False, num_devices=1)
    arrays, args = {}, []
    for name in _INS:
        a = _np.ascontiguousarray(inputs[name])
        arrays[f"in_{name}"] = a
        args.append(nc.dram_tensor(f"in_{name}", a.shape, _mybir.dt.from_np(a.dtype), kind="ExternalInput").ap())
    args.append(nc.dram_tensor("out", inputs["x"].shape, _mybir.dt.float32, kind="ExternalOutput").ap())
    build(nc, *args)
    return _run(nc, [arrays], core_ids=[0]).results[0]["out"]
```

```python
from contextlib import ExitStack

import concourse.bass as bass
from concourse import mybir

F32 = mybir.dt.float32
F16 = mybir.dt.float16
BF16 = mybir.dt.bfloat16
ALU = mybir.AluOpType
ACT = mybir.ActivationFunctionType
AX = mybir.AxisListType

P = 128
IMG = 32
T = IMG * IMG
NT = T // P
C = 384
NC_ = C // P
NH = 6
HD = 64
NPAIR = NH // 2
BANK = 512
NREL = 2 * IMG - 1
GC = 12
FF = 1536
NF = FF // P
FA, FB = 32, 12
SCALE = HD ** -0.5
MSCALE = 64.0
MASKED = -1.0e30
BETWEEN = {0: (0, 1), 1: (2,), 3: (3,)}
ROW_AFTER = 5
RING = 4
ROW_LEAD = 3
NORM_STEPS = (9, 23, 27)
LAG = 3
STORES = 32
VW = 2 * HD + 1


def slot(h):
    return (h % 2) * NPAIR + h // 2


def own(h):
    return slice(0, HD) if h % 2 == 0 else slice(HD, P)


def other(h):
    return slice(HD, P) if h % 2 == 0 else slice(0, HD)


def crows(h):
    return slice(0, HD + 1) if h % 2 == 0 else slice(0, P)


def mrow(h):
    return HD if h % 2 == 0 else 0


class Mem:

    def xin_hi(self, c, t0, t1):
        return self.xin[:, t0:t1, c * P:(c + 1) * P].bitcast(F16)[:, :, 0:P]

    def xin_lo(self, c, t0, t1):
        return self.xin[:, t0:t1, c * P:(c + 1) * P].bitcast(F16)[:, :, P:2 * P]


def allocate(nc, ctx, m):
    def sb(name, shape, dt):
        return ctx.enter_context(nc.sbuf_tensor(name, shape, dt))

    m.wqkv_hi = [sb(f"wqkv{n}_hi", [P, NC_, 3 * C], F16) for n in range(2)]
    m.wqkv_lo = [sb(f"wqkv{n}_lo", [P, NC_, 3 * C], F16) for n in range(2)]
    m.wo_hi = [sb(f"wo{n}_hi", [P, NC_, C], F16) for n in range(2)]
    m.wo_lo = [sb(f"wo{n}_lo", [P, NC_, C], F16) for n in range(2)]
    m.bqk = sb("bqk", [P, 2 * NPAIR], F32)
    m.bv = sb("bv", [P, C], F32)
    m.bv16 = sb("bv16", [IMG + 1, C], F16)
    m.ones16 = sb("ones16", [IMG + 1, P], F16)
    m.bo = [sb(f"bo{n}", [P, C], F32) for n in range(2)]
    m.rel_hi = sb("rel_hi", [P, 2, NREL], F16)
    m.rel_lo = sb("rel_lo", [P, 2, NREL], F16)
    m.c1 = sb("c1", [3 * FA, FF], F16)
    m.cp = sb("cp", [P, NF, FA], F32)
    m.cf2 = sb("cf2", [P, FB], F32)
    m.f2sum = sb("f2sum", [P, 1], F32)
    m.cp2 = sb("cp2", [P, FB], F32)
    m.spread = sb("spread", [P, C], F32)
    m.group = sb("group", [P, NC_, C], F32)
    m.ident = sb("ident", [P, P], F32)
    m.ident16 = sb("ident16", [P, P], F16)
    m.identb = sb("identb", [P, P], BF16)
    m.mask_kq = sb("mask_kq", [P, P], BF16)
    m.mask_qk = sb("mask_qk", [P, P], BF16)
    m.minus_half = sb("minus_half", [P, NT], F32)
    m.xin = sb("xin", [P, NT, C], F32)
    m.x = sb("x", [P, NT, C], F32)
    m.hT = sb("hT", [P, NC_, T], F16)
    m.lT = sb("lT", [P, NC_, T], F16)
    m.o = sb("o", [P, NT, C], F32)
    m.qa = sb("qa", [P, NH, T], F16)
    m.qb = sb("qb", [P, NH, T], F16)
    m.qc = sb("qc", [P, NH, T], F16)
    m.ka0 = sb("ka0", [P, NH, T], F16)
    m.kc = sb("kc", [P, NH, T], F16)
    m.v = sb("v", [P, NT, NH, VW], F16)
    m.p32 = sb("p32", [P, RING, 2, BANK], F32)
    m.ph = sb("ph", [P, RING, 2, BANK], F16)
    m.pl = sb("pl", [P, RING, 2, BANK], F16)
    m.stats = sb("stats", [P, NT, 6], F32)
    m.mv = sb("mv", [P, NT, 2], F32)
    m.gstats = sb("gstats", [P, 2, 6], F32)
    m.gmv = sb("gmv", [P, NC_, 2], F32)
    m.small = sb("small", [P, 6, NT], F32)
    m.ln = sb("ln", [P, 3, NT], F32)
    m.rowt = sb("rowt", [NT, P], F16)
    m.mxp = sb("mxp", [P, 2, 2, NT], F32)
    m.nm = sb("nm", [P, 2, NT], F16)
    m.rs = sb("rs", [P, 2, 4], F32)
    m.ps = ctx.enter_context(nc.psum_tensor("ps", [P, 8, BANK], F32))


class Stage:

    def __init__(self, nc, ctx, name, sems):
        self.nc, self.ctx, self.name = nc, ctx, name
        self.sems = [ctx.enter_context(nc.semaphore(f"{name}_{s}")) for s in sems]

    def __enter__(self):
        self.inner = ExitStack()
        return (self.inner.enter_context(self.nc.Block()), *self.sems)

    def __exit__(self, *a):
        return self.inner.__exit__(*a)


def constants(nc, ctx, m, d, stored):
    stage = [m.o[:, 0:3, :], m.o[:, 3:6, :],
             m.p32[:, 0:2, :, :].rearrange("p a b c -> p (a b c)")[:, 0:3 * C].rearrange("p (a b) -> p a b", a=3),
             m.x[:, 0:3, :], m.x[:, 3:6, :]]
    NS = len(stage)
    pieces = []
    w0 = d.qkv_w.rearrange("(k p) n -> p k n", p=P)
    for k in range(NC_):
        pieces.append((w0[:, k, :].rearrange("p (a b) -> p a b", a=3), m.wqkv_hi[0][:, k, :].rearrange("p (a b) -> p a b", a=3),
                       m.wqkv_lo[0][:, k, :].rearrange("p (a b) -> p a b", a=3)))
    for i, w in enumerate((d.wq, d.wk, d.wv)):
        pieces.append((w.rearrange("(k p) n -> p k n", p=P), m.wqkv_hi[1][:, :, i * C:(i + 1) * C], m.wqkv_lo[1][:, :, i * C:(i + 1) * C]))
    for n, w in enumerate((d.proj_w, d.wo)):
        pieces.append((w.rearrange("(k p) n -> p k n", p=P), m.wo_hi[n][:, :, :], m.wo_lo[n][:, :, :]))

    rel2 = m.ph[:, 0, :, :].rearrange("p a b -> p (a b)").bitcast(F32)[0:NREL, 0:4 * HD].rearrange("p (a b) -> p a b", a=4)
    anti = m.ph[:, 1, :, :].rearrange("p a b -> p (a b)").bitcast(F32)[0:NREL, 0:NREL]
    c1in = m.pl[:, 0, :, :].rearrange("p a b -> p (a b)").bitcast(F32)[:, 0:NF * FA].rearrange("p (a b) -> p a b", a=NF)
    cpin = m.hT[:, :, :].rearrange("p a b -> p (a b)").bitcast(F32)[0:FA, 0:FF]
    relf = m.pl[:, 1, :, :].rearrange("p a b -> p (a b)").bitcast(F32)[:, 0:2 * NREL].rearrange("p (a b) -> p a b", a=2)
    c1f = m.lT[:, :, :].rearrange("p a b -> p (a b)").bitcast(F32)[0:FA, 0:FF]

    loads = [ctx.enter_context(nc.semaphore(f"const_load{i}")) for i in range(NS)]
    st = Stage(nc, ctx, "const", ["tables_in", "biases_in", "bias_hi", "hi_done", "lo_done", "filled", "shaped", "rel_mm", "rel_out", "rel_hi", "c1_mm",
                                  "c1_out", "c1_hi", "cp_mm", "cp_out"])
    with st as (block, tables_in, biases_in, bias_hi, hi_done, lo_done, filled, shaped, rel_mm, rel_out, rel_hi, c1_mm, c1_out, c1_hi, cp_mm, cp_out):
        @block.sync
        def _(sp):
            sp.sem_inc(stored, STORES)
            for i, r in enumerate((d.rel_h, d.rel_h, d.rel_w, d.rel_w)):
                sp.dma_start(rel2[:, i, :], r).then_inc(tables_in, 16)
            sp.dma_start(c1in, d.c_fc_1.rearrange("(i p) a -> p i a", p=P)).then_inc(tables_in, 16)
            sp.dma_start(cpin, d.c_proj_1).then_inc(tables_in, 16)
            for i, (src, _, _) in enumerate(pieces):
                if i >= NS:
                    sp.wait_ge(lo_done, i - NS + 1)
                sp.dma_start(stage[i % NS], src).then_inc(loads[i % NS], 16)

        @block.scalar
        def _(act):
            act.dma_start(m.bqk[:, :], d.qkv_b[0:2 * C].rearrange("(m p) -> p m", p=P), allow_slow_non_contiguous=True).then_inc(biases_in, 16)
            for dst, src in ((m.bv, d.qkv_b[2 * C:3 * C]), (m.bo[0], d.proj_b), (m.bo[1], d.bo),
                             (m.cf2, d.c_fc_2.rearrange("a b -> (a b)")), (m.cp2, d.c_proj_2.rearrange("a b -> (a b)"))):
                act.dma_start(dst[:, :], src.partition_broadcast(P)).then_inc(biases_in, 16)
            act.dma_start(m.xin[:, :, :], d.x_tiles[0]).then_inc(biases_in, 16)
            for i, (_, hi, _) in enumerate(pieces):
                act.wait_ge(loads[i % NS], 16 * (i // NS + 1))
                nc.scalar.activation(hi, stage[i % NS], ACT.Copy).then_inc(hi_done, 1)
            act.wait_ge(cp_mm, NF)
            nc.scalar.activation(m.cp[:, :, :], m.ps[:, 4, 0:NF * FA].rearrange("p (a b) -> p a b", a=NF), ACT.Copy).then_inc(cp_out, 1)
            act.wait_ge(c1_mm, NF)
            nc.scalar.activation(c1f, m.ps[0:FA, 1:4, :].rearrange("p a b -> p (a b)"), ACT.Copy).then_inc(c1_out, 1)
            act.wait_ge(biases_in, 16 * 7)

        @block.vector
        def _(dve):
            for i, (_, hi, lo) in enumerate(pieces):
                dve.wait_ge(hi_done, i + 1)
                nc.vector.tensor_tensor(lo, stage[i % NS], hi, ALU.subtract).then_inc(lo_done, 1)
            dve.wait_ge(rel_mm, 2)
            nc.vector.tensor_scalar(relf, m.ps[:, 0, 0:2 * NREL].rearrange("p (a b) -> p a b", a=2), 1.0 / SCALE, None, ALU.mult).then_inc(rel_out, 1)
            dve.wait_ge(rel_out, 1)
            nc.vector.tensor_copy(m.rel_hi[:, :, :], relf).then_inc(rel_hi, 1)
            dve.wait_ge(rel_hi, 1)
            nc.vector.tensor_tensor(m.rel_lo[:, :, :], relf, m.rel_hi[:, :, :], ALU.subtract)
            dve.wait_ge(c1_out, 1)
            nc.vector.tensor_copy(m.c1[0:FA, :], c1f).then_inc(c1_hi, 1)
            nc.vector.tensor_copy(m.c1[FA:2 * FA, :], c1f)
            dve.wait_ge(c1_hi, 1)
            nc.vector.tensor_tensor(m.c1[2 * FA:3 * FA, :], c1f, m.c1[0:FA, :], ALU.subtract)
            dve.wait_ge(biases_in, 16 * 7)
            nc.vector.reduce_sum(m.f2sum[:, :], m.cf2[:, :], AX.X)
            dve.wait_ge(shaped, 1)
            nc.vector.tensor_copy(m.bv16[0:1, :], m.bv[0:1, :])
            nc.vector.tensor_copy(m.bv16[IMG:IMG + 1, :], m.bv[IMG:IMG + 1, :]).then_inc(bias_hi, 1)
            dve.wait_ge(bias_hi, 1)
            nc.vector.tensor_tensor(m.bv16[IMG:IMG + 1, :], m.bv[IMG:IMG + 1, :], m.bv16[IMG:IMG + 1, :], ALU.subtract)
            nc.vector.tensor_tensor(m.spread[:, :].rearrange("p (a b) -> p a b", b=FB), m.spread[:, :].rearrange("p (a b) -> p a b", b=FB),
                                    m.cp2[:, :].unsqueeze(1).broadcast_to([P, FA, FB]), ALU.mult)

        @block.gpsimd
        def _(pool):
            count = [0]

            def fill(ap, value):
                nc.gpsimd.memset(ap, value).then_inc(filled, 1)
                count[0] += 1
                pool.wait_ge(filled, count[0])

            def carve(ap, op, fill_value, base, pattern, mult):
                nc.gpsimd.affine_select(out=ap, in_=ap, compare_op=op, fill=fill_value, base=base, pattern=pattern,
                                        channel_multiplier=mult).then_inc(filled, 1)
                count[0] += 1
                pool.wait_ge(filled, count[0])

            for t in (m.ident[:, :], m.ident16[:, :], m.identb[:, :], anti, m.mask_kq[:, :], m.mask_qk[:, :], m.spread[:, :],
                      m.ka0[:, :, :], m.qc[:, :, :], m.kc[:, :, :], m.bv16[:, :]):
                fill(t, 0.0)
            fill(m.group[:, :, :], 1.0 / GC)
            fill(m.minus_half[:, :], -0.5)
            fill(m.ones16[:, :], 1.0)
            fill(m.v[:, :, :, HD:HD + 1], 1.0)
            for h in range(NH):
                fill(m.kc[mrow(h):mrow(h) + 1, slot(h), :], MSCALE)
            for t in (m.ident[:, :], m.ident16[:, :], m.identb[:, :]):
                carve(t, ALU.not_equal, 1.0, 0, [[-1, P]], 1)
            carve(anti, ALU.not_equal, 1.0, -(NREL - 1), [[1, NREL]], 1)
            carve(m.mask_kq[:, :], ALU.is_ge, MASKED, 0, [[1, P]], -1)
            carve(m.mask_qk[:, :], ALU.is_ge, MASKED, 0, [[-1, P]], 1)
            for k in range(NC_):
                gk = m.group[:, k, :].rearrange("p (g r) -> p g r", r=GC)
                carve(gk, ALU.is_ge, 0.0, k * P, [[-GC, C // GC], [0, GC]], 1)
            for k in range(NC_):
                gk = m.group[:, k, :].rearrange("p (g r) -> p g r", r=GC)
                carve(gk, ALU.is_ge, 0.0, GC - 1 - k * P, [[GC, C // GC], [0, GC]], -1)
            for base_h in (HD, 0):
                s = slice(0, NPAIR) if base_h == HD else slice(NPAIR, NH)
                kh = m.ka0[base_h:base_h + IMG, s, :].rearrange("p s (a b) -> p s a b", a=IMG)
                kw = m.ka0[base_h + IMG:base_h + 2 * IMG, s, :].rearrange("p s (a b) -> p s a b", a=IMG)
                carve(kh, ALU.not_equal, 1.0, 0, [[0, NPAIR], [-1, IMG], [0, IMG]], 1)
                carve(kw, ALU.not_equal, 1.0, 0, [[0, NPAIR], [0, IMG], [-1, IMG]], 1)
            for j in range(4):
                sv = m.spread[j * FA:(j + 1) * FA, :].rearrange("p (a b) -> p a b", b=FB)
                carve(sv, ALU.not_equal, 1.0, 0, [[-1, FA], [0, FB]], 1)
            nc.gpsimd.memset(m.small[:, :, :], 0.0).then_inc(shaped, 1)

        @block.tensor
        def _(pe):
            pe.wait_ge(shaped, 1)
            pe.wait_ge(tables_in, 16 * 6)
            for i in range(2):
                nc.tensor.matmul(m.ps[:, 0, i * NREL:(i + 1) * NREL], rel2[:, 2 * i:2 * i + 2, :].rearrange("p a b -> p (a b)"), anti,
                                 start=True, stop=True).then_inc(rel_mm, 1)
            for i in range(NF):
                nc.tensor.transpose(m.ps[:, 4, i * FA:(i + 1) * FA], cpin[:, i * P:(i + 1) * P], m.ident[0:FA, 0:FA]).then_inc(cp_mm, 1)
            for i in range(NF):
                nc.tensor.transpose(m.ps[0:FA, 1 + i // 4, (i % 4) * P:(i % 4 + 1) * P], c1in[:, i, :], m.ident[:, :]).then_inc(c1_mm, 1)


def semaphores(nc, ctx, prefix, names):
    return {n: ctx.enter_context(nc.semaphore(f"{prefix}_{n}")) for n in names.split()}


def flat(ap):
    return ap.rearrange("p a b -> p (a b)")


def tiles(ap):
    return ap.rearrange("p (t q) -> p t q", q=P)


class Norm:

    def __init__(self, nc, ctx, m, name):
        self.nc, self.m = nc, m
        self.s = semaphores(nc, ctx, name, "transposed copied stats agg mean_mm mean_out dev dev2 var_mm var_eps rstd shift normed hi lo")
        self.mean_g, self.dev, self.tvar, self.veps, self.rstd, self.shift = (m.small[:, i, 0:NC_] for i in range(6))
        self.temp = [buf[:, NC_ - 1, :].bitcast(F32) for buf in (m.hT, m.lT)]

    def unit(self, n):
        c, hf = n // 2, n % 2
        return self.m.xin[:, 4 * hf:4 * hf + 4, c * P:(c + 1) * P]

    def transposes(self, pe, n, bank):
        c, hf = n // 2, n % 2
        for t in range(4 * hf, 4 * hf + 4):
            mm = self.nc.tensor.transpose(self.m.ps[:, bank, (t % 4) * P:(t % 4 + 1) * P], self.m.xin[:, t, c * P:(c + 1) * P], self.m.ident[:, :])
        return mm

    def copy(self, act, n, bank):
        self.nc.scalar.activation(self.unit(n), tiles(self.m.ps[:, bank, :]), ACT.Copy).then_inc(self.s["copied"], 1)

    def stats(self, dve, n, bank):
        return self.nc.vector.bn_stats(self.m.gstats[:, n % 2, :], self.m.ps[:, bank, :])

    def aggregate(self, dve, c):
        self.nc.vector.bn_aggr(self.m.gmv[:, c, :], self.m.gstats[:, :, :]).then_inc(self.s["agg"], 1)
        dve.wait_ge(self.s["agg"], c + 1)

    def average(self, pe, bank, value):
        for i in range(NC_):
            for k in range(NC_):
                mm = self.nc.tensor.matmul(self.m.ps[:, bank, i:i + 1], self.m.group[:, k, i * P:(i + 1) * P], value(k),
                                           start=(k == 0), stop=(k == NC_ - 1))
        return mm

    def means(self, pe, bank):
        pe.wait_ge(self.s["agg"], NC_)
        return self.average(pe, bank, lambda k: self.m.gmv[:, k, 0:1])

    def mean_out(self, dve, bank):
        return self.nc.vector.tensor_copy(self.mean_g, self.m.ps[:, bank, 0:NC_])

    def deviations(self, dve):
        nc, s, m = self.nc, self.s, self.m
        nc.vector.tensor_tensor(self.dev, m.gmv[:, :, 0], self.mean_g, ALU.subtract).then_inc(s["dev"], 1)
        dve.wait_ge(s["dev"], 1)
        nc.vector.tensor_tensor(self.tvar, self.dev, self.dev, ALU.mult).then_inc(s["dev"], 1)
        dve.wait_ge(s["dev"], 2)
        nc.vector.tensor_tensor(self.tvar, self.tvar, m.gmv[:, :, 1], ALU.add).then_inc(s["dev2"], 1)

    def variances(self, pe, bank):
        pe.wait_ge(self.s["dev2"], 1)
        return self.average(pe, bank, lambda k: self.tvar[:, k:k + 1])

    def eps(self, dve, bank):
        return self.nc.vector.tensor_scalar(self.veps, self.m.ps[:, bank, 0:NC_], 1e-5, None, ALU.add)

    def root(self, pool):
        self.nc.gpsimd.tensor_tensor(self.rstd, self.veps, self.m.minus_half[:, 0:NC_], ALU.pow).then_inc(self.s["rstd"], 1)

    def shifts(self, dve):
        dve.wait_ge(self.s["rstd"], 1)
        self.nc.vector.scalar_tensor_tensor(self.shift, self.mean_g, -1.0, self.rstd, ALU.mult, ALU.mult).then_inc(self.s["shift"], 1)

    def normalise(self, act, n):
        c, s = n // 2, self.s
        if n == 0:
            act.wait_ge(s["shift"], 1)
        if n >= 2:
            act.wait_ge(s["lo"], n - 1)
        self.nc.scalar.activation(tiles(self.temp[n % 2]), self.unit(n), ACT.Identity, scale=self.rstd[:, c:c + 1],
                                  bias=self.shift[:, c:c + 1]).then_inc(s["normed"], 1)

    def high(self, act, n):
        c, hf = n // 2, n % 2
        act.wait_ge(self.s["normed"], n + 1)
        self.nc.scalar.activation(self.m.xin_hi(c, 4 * hf, 4 * hf + 4), tiles(self.temp[n % 2]), ACT.Copy).then_inc(self.s["hi"], 1)

    def low(self, pool, n):
        c, hf = n // 2, n % 2
        half = slice(4 * hf, 4 * hf + 4)
        pool.wait_ge(self.s["hi"], n + 1)
        self.nc.gpsimd.tensor_tensor(self.m.xin_lo(c, 4 * hf, 4 * hf + 4), tiles(self.temp[n % 2]), self.m.xin_hi(c, 4 * hf, 4 * hf + 4),
                                     ALU.subtract).then_inc(self.s["lo"], 1)


def first_image(nc, ctx, m, norm, qkv):
    s = norm.s
    with nc.Block() as block:
        @block.tensor
        def _(pe):
            for n in range(2 * NC_):
                norm.transposes(pe, n, n).then_inc(s["transposed"], 1)
            norm.means(pe, 6).then_inc(s["mean_mm"], 1)
            norm.variances(pe, 7).then_inc(s["var_mm"], 1)
            pe.wait_ge(s["lo"], 2 * NC_)
            for i in range(2 * NPAIR):
                qkv.pair_products(pe, i)

        @block.scalar
        def _(act):
            for n in range(2 * NC_):
                act.wait_ge(s["transposed"], n + 1)
                norm.copy(act, n, n)
            for n in range(2 * NC_):
                norm.normalise(act, n)
                norm.high(act, n)
            for i in range(2 * NPAIR):
                qkv.pair_high(act, i)

        @block.vector
        def _(dve):
            for n in range(2 * NC_):
                dve.wait_ge(s["copied"], n + 1)
                norm.stats(dve, n, n).then_inc(s["stats"], 1)
                if n % 2 == 1:
                    dve.wait_ge(s["stats"], n + 1)
                    norm.aggregate(dve, n // 2)
            dve.wait_ge(s["mean_mm"], 1)
            norm.mean_out(dve, 6).then_inc(s["mean_out"], 1)
            dve.wait_ge(s["mean_out"], 1)
            norm.deviations(dve)
            dve.wait_ge(s["var_mm"], 1)
            norm.eps(dve, 7).then_inc(s["var_eps"], 1)
            norm.shifts(dve)
            for i in range(2 * NPAIR):
                qkv.pair_low(dve, i)

        @block.gpsimd
        def _(pool):
            pool.wait_ge(s["var_eps"], 1)
            norm.root(pool)
            for n in range(2 * NC_):
                norm.low(pool, n)


class Projections:

    def __init__(self, nc, ctx, m, layer, name):
        self.nc, self.m, self.layer = nc, m, layer
        self.s = semaphores(nc, ctx, name, "mm hi lo rel_mm rel_hi rel_lo v_mm v32 v_lo" if layer == 0
                            else "mm hi lo v_mm v32 v_lo")
        self.wh, self.wl = m.wqkv_hi[layer], m.wqkv_lo[layer]
        self.ka = m.ka0 if layer == 0 else m.qb
        self.order = (0, 1, 2, 3, 4, 5) if layer == 0 else (0, 3, 1, 4, 2, 5)
        self.bank = (6, 4, 2, 4, 2, 4) if layer == 0 else (0, 2, 4, 6, 0, 2)
        self.before = (0, 0, 0, 4, 6, 8) if layer == 0 else (0, 0, 0, 0, 2, 4)

    def high(self, k, t0, t1):
        return self.m.xin_hi(k, t0, t1) if self.layer == 0 else self.m.hT[:, k, t0 * P:t1 * P]

    def low(self, k, t0, t1):
        return self.m.xin_lo(k, t0, t1) if self.layer == 0 else self.m.lT[:, k, t0 * P:t1 * P]

    def out2(self, i):
        return flat(self.m.ps[:, self.bank[i]:self.bank[i] + 2, :])

    def pair_products(self, pe, i, input_ready=None, part=(0, 2 * 3 * NC_)):
        nc, m, s = self.nc, self.m, self.s
        if self.before[i] and part[0] == 0:
            pe.wait_ge(s["lo"], self.before[i])
        steps = [(w, x, k) for k in range(NC_) for w, x in ((self.wh, self.high), (self.wh, self.low), (self.wl, self.high))]
        if input_ready is None:
            order = [(n, j) for n in range(len(steps)) for j in range(2)]
        else:
            order = [(n, j) for j in range(2) for n in range(len(steps))]
        for n, j in order[part[0]:part[1]]:
            w, x, k = steps[n]
            if input_ready is not None and n % 3 == 0:
                input_ready(pe, j, k)
            mm = nc.tensor.matmul(m.ps[:, self.bank[i] + j, :], w[:, k, self.order[i] * P:(self.order[i] + 1) * P], x(k, 4 * j, 4 * j + 4),
                                  start=(n == 0), stop=(n == len(steps) - 1))
        if part[1] == len(order):
            mm.then_inc(s["mm"], 1)

    def fill(self, pe, begin, end):
        each = 2 * 3 * NC_
        for i in range(begin // each, (end - 1) // each + 1):
            self.pair_products(pe, i, part=(max(begin - i * each, 0), min(end - i * each, each)))

    def pair_high(self, act, i, heads=(0, 1)):
        nc, m, s = self.nc, self.m, self.s
        act.wait_ge(s["mm"], i + 1)
        f = self.order[i]
        for e in heads:
            h = 2 * (f % NPAIR) + e
            dst = m.qa if f < NPAIR else self.ka
            if self.layer == 0:
                nc.scalar.activation(dst[own(h), slot(h), :], self.out2(i)[own(h), :], ACT.Identity, bias=m.bqk[own(h), f:f + 1]).then_inc(s["hi"], 1)
            else:
                nc.scalar.activation(dst[own(h), slot(h), :], self.out2(i)[own(h), :], ACT.Copy).then_inc(s["hi"], 1)

    def pair_low(self, dve, i, heads=(0, 1)):
        nc, m, s, layer = self.nc, self.m, self.s, self.layer
        f = self.order[i]
        for e in heads:
            h = 2 * (f % NPAIR) + e
            is_q = f < NPAIR
            src = m.qa if is_q else self.ka
            if layer == 0:
                dst = m.qb[own(h), slot(h), :] if is_q else m.kc[own(h), slot(h), :]
            else:
                dst = m.qa[other(h), slot(h), :] if is_q else m.kc[own(h), slot(h), :]
            dve.wait_ge(s["hi"], 2 * i + e + 1)
            if layer == 0:
                last = nc.vector.scalar_tensor_tensor(dst, self.out2(i)[own(h), :], m.bqk[own(h), f:f + 1], src[own(h), slot(h), :],
                                                      ALU.add, ALU.subtract)
            else:
                last = nc.vector.tensor_tensor(dst, self.out2(i)[own(h), :], src[own(h), slot(h), :], ALU.subtract)
            if is_q:
                last = nc.vector.tensor_copy(m.qc[own(h), slot(h), :], src[own(h), slot(h), :])
            elif layer == 1:
                last = nc.vector.tensor_copy(self.ka[other(h), slot(h), :], src[own(h), slot(h), :])
            last.then_inc(s["lo"], 1)

    def rel_base(self, parity, axis):
        return (HD if parity == 0 else 0) + IMG * axis

    def rel_products(self, pe, n):
        nc, m, s = self.nc, self.m, self.s
        if n >= 4:
            pe.wait_ge(s["rel_lo"], 4 * (n - 3))
        for i in range(4):
            pos = 4 * n + i
            for axis in range(2):
                for parity in range(2):
                    rows = own(parity)
                    b = self.rel_base(parity, axis)
                    o = m.ps[b:b + IMG, n % 4, i * NPAIR * IMG:(i + 1) * NPAIR * IMG].rearrange("p (s w) -> p s w", s=NPAIR)
                    sl = slice(parity * NPAIR, (parity + 1) * NPAIR)

                    def queries(buf):
                        full = buf[rows, sl, :].rearrange("p s (h w) -> p s h w", h=IMG)
                        return full[:, :, pos, :] if axis == 0 else full[:, :, :, pos]
                    t0 = IMG - 1 - pos
                    steps = ((m.rel_hi, m.qa), (m.rel_hi, m.qb), (m.rel_lo, m.qa))
                    for k, (r, q) in enumerate(steps):
                        mm = nc.tensor.matmul(o, r[rows, axis, t0:t0 + IMG], queries(q), start=(k == 0), stop=(k == len(steps) - 1))
        mm.then_inc(s["rel_mm"], 1)

    def rel_views(self, r, buf):
        m, n = self.m, r // 4
        parity, axis = r // 2 % 2, r % 2
        b = self.rel_base(parity, axis)
        src = m.ps[b:b + IMG, n % 4, 0:4 * NPAIR * IMG].rearrange("p (i s w) -> p s i w", i=4, s=NPAIR)
        full = buf[b:b + IMG, parity * NPAIR:(parity + 1) * NPAIR, :].rearrange("p s (h w) -> p s h w", h=IMG)
        if axis == 0:
            return src, full[:, :, 4 * n:4 * n + 4, :]
        return src, full[:, :, :, 4 * n:4 * n + 4].rearrange("p s h i -> p s i h")

    def rel_high(self, act, r):
        act.wait_ge(self.s["rel_mm"], r // 4 + 1)
        src, dst = self.rel_views(r, self.m.qa)
        self.nc.scalar.activation(dst, src, ACT.Copy).then_inc(self.s["rel_hi"], 1)

    def rel_low(self, dve, r):
        dve.wait_ge(self.s["rel_hi"], r + 1)
        src, hi = self.rel_views(r, self.m.qa)
        _, lo = self.rel_views(r, self.m.qb)
        self.nc.vector.tensor_tensor(lo, src, hi, ALU.subtract).then_inc(self.s["rel_lo"], 1)

    def v_products(self, pe, t):
        nc, m, s = self.nc, self.m, self.s
        if t == 0 and self.layer == 1:
            pe.wait_ge(s["lo"], 8)
        if t >= 2:
            pe.wait_ge(s["v32"], t - 1)
        steps = [(x, w, k) for k in range(NC_) for x, w in ((self.high, self.wh), (self.high, self.wl), (self.low, self.wh))]
        for n, (x, w, k) in enumerate(steps):
            mm = nc.tensor.matmul(m.ps[:, 6 + t % 2, 0:C], flat_tile(x(k, t, t + 1)), w[:, k, 2 * C:3 * C],
                                  start=(n == 0), stop=(self.layer == 1 and n == len(steps) - 1))
        if self.layer == 0:
            mm = nc.tensor.matmul(m.ps[:, 6 + t % 2, 0:C], m.ones16[:, :], m.bv16[:, :], start=False, stop=True)
        mm.then_inc(s["v_mm"], 1)

    def v_high(self, act, t):
        nc, m, s = self.nc, self.m, self.s
        act.wait_ge(s["v_mm"], t + 1)
        nc.scalar.activation(m.v[:, t, :, 0:HD], m.ps[:, 6 + t % 2, 0:C].rearrange("p (h d) -> p h d", d=HD), ACT.Copy)
        nc.scalar.activation(m.o[:, t, :], m.ps[:, 6 + t % 2, 0:C], ACT.Copy).then_inc(s["v32"], 1)

    def v_low(self, pool, t):
        pool.wait_ge(self.s["v32"], t + 1)
        self.nc.gpsimd.tensor_tensor(self.m.v[:, t, :, HD + 1:VW], self.m.o[:, t, :].rearrange("p (h d) -> p h d", d=HD), self.m.v[:, t, :, 0:HD],
                                     ALU.subtract).then_inc(self.s["v_lo"], 1)


def flat_tile(ap):
    return ap if len(ap.shape) == 2 else ap.rearrange("p t q -> p (t q)")


class Attention:

    def __init__(self, nc, ctx, m, layer, proj, norm=None, next_in=None):
        self.nc, self.m, self.layer, self.proj, self.norm_, self.next_in = nc, m, layer, proj, norm, next_in
        self.s = semaphores(nc, ctx, f"attn{layer}", "scores exp hi_act hi_pool pl_dve pl_pool pv use free reduced combined nm row recip out ot_hi")
        self.ka = m.ka0 if layer == 0 else m.qb
        self.causal = layer == 1
        if self.causal:
            self.groups = [(hf, kt, max(hf * BANK, kt * P)) for hf in range(2) for kt in range(0, 4 * (hf + 1), 2)]
            self.tiles = [(qt, kh, min(BANK, (qt + 1) * P - kh * BANK)) for qt in range(NT) for kh in range(2) if (qt + 1) * P > kh * BANK]
            self.both = slice(4, NT)
        else:
            self.groups = [(hf, kt, hf * BANK) for hf in range(2) for kt in range(0, NT, 2)]
            self.tiles = [(qt, kh, BANK) for qt in range(NT) for kh in range(2)]
            self.both = slice(0, NT)
        G = self.NG = len(self.groups)
        self.NTL = len(self.tiles)
        self.N = NH * G
        self.last_of_half = {g for g in range(G) if g == G - 1 or self.groups[g + 1][0] != self.groups[g][0]}
        self.prologue = [("max", 0, n) for n in range(self.NTL)]
        steps = [[] for _ in range(self.N)]
        if self.causal:
            self.prologue += [("max", 1, n) for n in range(self.NTL)]
            self.prologue.insert(self.NTL + ROW_AFTER, ("row", 0))
            ends = [0, 0] + [h * G - ROW_LEAD for h in range(2, NH)]
        else:
            ends = [0] + [h * G - ROW_LEAD for h in range(1, NH)]
            steps[0].append(("row", 0))
        for h in range(1, NH):
            begin, end = ends[h - 1], ends[h]
            if end > begin:
                for n in range(self.NTL):
                    steps[begin + n * (end - begin) // self.NTL].append(("max", h, n))
            steps[end].append(("row", h))
        for c in range(NC_ - 1):
            for hf in range(2):
                steps[(2 * c + 2) * G + LAG + 1 + hf].append(("ot", c, hf))
        self.norm_at = {}
        if norm is not None:
            for n in range(2 * NC_):
                steps[NORM_STEPS[0] + 2 * n].append(("unit", n))
            steps[NORM_STEPS[1]].append(("mean",))
            steps[NORM_STEPS[1] + 2].append(("variance",))
            self.norm_at = {NORM_STEPS[2] + 2 * n: n for n in range(2 * NC_)}
        for st in steps:
            st.sort(key=lambda u: (u != ("row", 0), u[0] != "max"))
        self.beside_v = (0, 0, 0, 2, 8, 14, 20, 25, len(self.prologue)) if self.causal else (0, 0, 0, 0, 0, 0, 6, len(self.prologue))
        self.uses_at = steps
        self.tail = [("ot", NC_ - 1, hf) for hf in range(2)]
        self.index = {}
        for u in self.prologue + [u for st in steps for u in st] + self.tail:
            self.index[u] = len(self.index)
        ahead = (4, 5, 0, 1, 2, 3) if self.causal else (4, 5, 0, 1)
        self.banks = [ahead[r % len(ahead)] if r < len(self.prologue) else 4 + r % 2 for r in range(len(self.index))]
        self.last_use = [max((q for q in range(r) if self.banks[q] == self.banks[r]), default=None) for r in range(len(self.index))]
        self.scores_after = [max((q for q, bank in enumerate(self.banks) if bank in (2 * i, 2 * i + 1)), default=None) for i in range(2)]

    def even(self, i):
        return i % 2 == 0

    def wait_hi(self, eng, i):
        eng.wait_ge(self.s["hi_act"] if self.even(i) else self.s["hi_pool"], i // 2 + 1)

    def wait_lo(self, eng, i):
        eng.wait_ge(self.s["pl_pool"] if self.even(i) else self.s["pl_dve"], i // 2 + 1)

    def cols(self, i):
        hf, _, q0 = self.groups[i % self.NG]
        return (hf + 1) * BANK - q0

    def prologue_part(self, t):
        return self.prologue[self.beside_v[t]:self.beside_v[t + 1]]

    def early(self, i):
        return [u for u in self.uses_at[i][:2] if u[0] == "max" or u == ("row", 0)]

    def late(self, i):
        return self.uses_at[i][len(self.early(i)):]

    def bank(self, u):
        return self.banks[self.index[u]]

    def use(self, pe, u):
        nc, m, s, r = self.nc, self.m, self.s, self.index[u]
        if self.last_use[r] is not None:
            pe.wait_ge(s["free"], self.last_use[r] + 1)
        bank = self.bank(u)
        if u[0] == "max":
            _, h, n = u
            qt, kh, w = self.tiles[n]
            sl = slot(h)
            diag = self.causal and (qt + 1) * P - kh * BANK <= BANK
            if diag:
                nc.tensor.matmul(m.ps[:, bank, w - P:w], m.identb[:, :], m.mask_qk[:, :], start=True, stop=False, skip_group_check=True)
            mm = nc.tensor.matmul(m.ps[:, bank, 0:w], m.qa[:, sl, qt * P:(qt + 1) * P], self.ka[:, sl, kh * BANK:kh * BANK + w],
                                  start=not diag, stop=True, skip_group_check=True)
        elif u[0] == "row":
            _, h = u
            pe.wait_ge(s["nm"], h + 1)
            mm = nc.tensor.transpose(m.ps[0:NT, bank, 0:P // 2].bitcast(F16), m.nm[:, h % 2, :], m.ident16[:, :])
        elif u[0] == "unit":
            if u[1] == 0:
                pe.wait_ge(self.next_in, 16)
            mm = self.norm_.transposes(pe, u[1], bank)
        elif u[0] == "mean":
            mm = self.norm_.means(pe, bank)
        elif u[0] == "variance":
            mm = self.norm_.variances(pe, bank)
        else:
            _, c, hf = u
            pe.wait_ge(s["out"], 4 * c + 3 + hf)
            for t in range(4 * hf, 4 * hf + 4):
                mm = nc.tensor.transpose(m.ps[:, bank, (t % 4) * P:(t % 4 + 1) * P], m.o[:, t, c * P:(c + 1) * P], m.ident[:, :])
        mm.then_inc(s["use"], 1)

    def score_tiles(self, pe, i):
        nc, m, s = self.nc, self.m, self.s
        h, g = i // self.NG, i % self.NG
        hf, kt0, q0 = self.groups[g]
        w = self.cols(i)
        sl = slot(h)
        if i >= 2:
            pe.wait_ge(s["exp"], i - 1)
        elif self.scores_after[i] is not None:
            pe.wait_ge(s["free"], self.scores_after[i] + 1)
        q = slice(q0, q0 + w)
        outs = [m.ps[:, 2 * (i % 2) + j, 0:w] for j in range(2)]
        keys = [slice((kt0 + j) * P, (kt0 + j + 1) * P) for j in range(2)]
        for j in range(2):
            nc.tensor.matmul(outs[j], self.ka[:, sl, keys[j]], m.qa[:, sl, q], start=True, stop=False)
            if self.layer == 0:
                nc.tensor.matmul(outs[j], self.ka[:, sl, keys[j]], m.qb[:, sl, q], start=False, stop=False)
            d0 = (kt0 + j) * P - q0
            if self.causal and 0 <= d0 < w:
                nc.tensor.matmul(outs[j][:, d0:d0 + P], m.identb[:, :], m.mask_kq[:, :], start=False, stop=False, skip_group_check=True)
        if g == 0:
            pe.wait_ge(s["row"], 16 * (h + 1))
        for j in range(2):
            mm = nc.tensor.matmul(outs[j], m.kc[crows(h), sl, keys[j]], m.qc[crows(h), sl, q], start=False, stop=True)
        mm.then_inc(s["scores"], 1)

    def weighted_values(self, pe, i):
        nc, m, s = self.nc, self.m, self.s
        h, g = i // self.NG, i % self.NG
        hf, kt0, q0 = self.groups[g]
        half = 2 * h + hf
        first = g == 0 or self.groups[g - 1][0] != hf
        if i == 0:
            pe.wait_ge(self.proj.s["v_lo"], NT)
        if first and half >= 2:
            pe.wait_ge(s["out"], half - 1)
        self.wait_hi(pe, i)
        self.wait_lo(pe, i)
        work = []
        for j in range(2):
            kt = kt0 + j
            for qt in range(q0 // P, 4 * (hf + 1)):
                if self.causal and qt < kt:
                    continue
                c0 = (qt - hf * 4) * (HD + 1)
                e0 = qt * P - q0
                hi_p = m.ph[:, i % RING, j, e0:e0 + P]
                lo_p = m.pl[:, i % RING, j, e0:e0 + P]
                work += [(c0, HD + 1, hi_p, m.v[:, kt, h, 0:HD + 1]), (c0, HD, hi_p, m.v[:, kt, h, HD + 1:VW]),
                         (c0, HD + 1, lo_p, m.v[:, kt, h, 0:HD + 1])]
        for n, (c0, w, e, v) in enumerate(work):
            mm = nc.tensor.matmul(m.ps[:, 6 + half % 2, c0:c0 + w], e, v, start=(first and n == 0),
                                  stop=(g in self.last_of_half and n == len(work) - 1), skip_group_check=True)
        mm.then_inc(s["pv"], 1)

    def tensor(self, pe, between, last_values=None):
        for i in range(self.N + LAG):
            if i < self.N:
                if i == 0 and last_values:
                    self.use(pe, ("row", 0))
                    last_values()
                self.score_tiles(pe, i)
                for u in self.early(i):
                    if u != ("row", 0):
                        self.use(pe, u)
            else:
                between(i - self.N)
            if i >= LAG:
                self.weighted_values(pe, i - LAG)
            if i < self.N:
                for u in self.late(i):
                    self.use(pe, u)
            elif i == self.N + LAG - 2:
                self.use(pe, self.tail[0])
        between(LAG)
        self.use(pe, self.tail[1])

    def high_part(self, eng, i, copy, sem):
        m, w = self.m, self.cols(i)
        eng.wait_ge(self.s["exp"], i + 1)
        if i >= RING:
            eng.wait_ge(self.s["pv"], i - RING + 1)
        copy(m.ph[:, i % RING, :, 0:w], m.p32[:, i % RING, :, 0:w]).then_inc(sem, 1)

    def ot_high(self, act, u):
        _, c, hf = u
        act.wait_ge(self.s["use"], self.index[u] + 1)
        self.nc.scalar.activation(self.m.hT[:, c, hf * BANK:(hf + 1) * BANK], self.m.ps[:, self.bank(u), :], ACT.Copy).then_inc(self.s["ot_hi"], 1)

    def scalar(self, act):
        nc, m, s = self.nc, self.m, self.s
        for i in range(self.N):
            w = self.cols(i)
            act.wait_ge(s["scores"], i + 1)
            if i >= RING:
                self.wait_lo(act, i - RING)
            nc.scalar.activation(m.p32[:, i % RING, :, 0:w], m.ps[:, 2 * (i % 2):2 * (i % 2) + 2, 0:w], ACT.Exp, scale=SCALE).then_inc(s["exp"], 1)
            if self.even(i):
                self.high_part(act, i, lambda out, in_: nc.scalar.activation(out, in_, ACT.Copy), s["hi_act"])
            for u in self.uses_at[i]:
                if u[0] == "ot":
                    self.ot_high(act, u)
                elif u[0] == "unit":
                    act.wait_ge(s["use"], self.index[u] + 1)
                    self.norm_.copy(act, u[1], self.bank(u))
            if i in self.norm_at:
                self.norm_.normalise(act, self.norm_at[i])
                self.norm_.high(act, self.norm_at[i])
        if self.norm_at:
            act.wait_ge(self.norm_.s["lo"], 2 * NC_)
        for u in self.tail:
            self.ot_high(act, u)

    def release(self, dve, u):
        nc, m, s, r = self.nc, self.m, self.s, self.index[u]
        bank = self.bank(u)
        if u[0] == "max":
            _, h, n = u
            qt, kh, w = self.tiles[n]
            dve.wait_ge(s["use"], r + 1)
            nc.vector.reduce_max(m.mxp[:, h % 2, kh, qt:qt + 1], m.ps[:, bank, 0:w], AX.X).then_inc(s["free"], 1)
            if n == self.NTL - 1:
                self.combine(dve, h)
        elif u[0] == "row":
            _, h = u
            dve.wait_ge(s["use"], r + 1)
            if h >= 1:
                dve.wait_ge(s["row"], 16 * h)
            nc.vector.tensor_copy(m.rowt[:, :], m.ps[0:NT, bank, 0:P // 2].bitcast(F16)).then_inc(s["free"], 1)
        elif u[0] == "unit":
            n = u[1]
            dve.wait_ge(self.norm_.s["copied"], n + 1)
            self.norm_.stats(dve, n, bank).then_inc(s["free"], 1)
            if n % 2 == 1:
                dve.wait_ge(s["free"], r + 1)
                self.norm_.aggregate(dve, n // 2)
        elif u[0] == "mean":
            dve.wait_ge(s["use"], r + 1)
            self.norm_.mean_out(dve, bank).then_inc(s["free"], 1)
            dve.wait_ge(s["free"], r + 1)
            self.norm_.deviations(dve)
        elif u[0] == "variance":
            dve.wait_ge(s["use"], r + 1)
            self.norm_.eps(dve, bank).then_inc(s["free"], 1)
            self.norm_.shifts(dve)
        else:
            _, c, hf = u
            dve.wait_ge(s["ot_hi"], 2 * c + hf + 1)
            half = slice(hf * BANK, (hf + 1) * BANK)
            nc.vector.tensor_tensor(m.lT[:, c, half], m.ps[:, bank, :], m.hT[:, c, half], ALU.subtract).then_inc(s["free"], 1)

    def combine(self, dve, h):
        nc, m, s, both = self.nc, self.m, self.s, self.both
        dve.wait_ge(s["free"], self.index[("max", h, self.NTL - 1)] + 1)
        nc.vector.tensor_tensor(m.mxp[:, h % 2, 0, both], m.mxp[:, h % 2, 0, both], m.mxp[:, h % 2, 1, both], ALU.max).then_inc(s["combined"], 1)
        dve.wait_ge(s["combined"], h + 1)
        nc.vector.tensor_scalar(m.nm[:, h % 2, :], m.mxp[:, h % 2, 0, :], -1.0 / MSCALE, None, ALU.mult).then_inc(s["nm"], 1)

    def low_part(self, eng, engine, i, sem):
        m, w = self.m, self.cols(i)
        self.wait_hi(eng, i)
        if i >= RING:
            eng.wait_ge(self.s["pv"], i - RING + 1)
        engine.tensor_tensor(m.pl[:, i % RING, :, 0:w], m.p32[:, i % RING, :, 0:w], m.ph[:, i % RING, :, 0:w], ALU.subtract).then_inc(sem, 1)

    def normalise(self, dve, i):
        nc, m, s = self.nc, self.m, self.s
        h, g = i // self.NG, i % self.NG
        hf = self.groups[g][0]
        half = 2 * h + hf
        acc = m.ps[:, 6 + half % 2, 0:4 * (HD + 1)].rearrange("p (t c) -> p t c", c=HD + 1)
        dve.wait_ge(s["pv"], i + 1)
        if half == 0:
            dve.wait_ge(self.proj.s["v_lo"], NT)
        nc.vector.reciprocal(m.rs[:, half % 2, :], acc[:, :, HD]).then_inc(s["recip"], 1)
        dve.wait_ge(s["recip"], half + 1)
        nc.vector.tensor_tensor(m.o[:, hf * 4:(hf + 1) * 4, h * HD:(h + 1) * HD], acc[:, :, 0:HD],
                                m.rs[:, half % 2, :].unsqueeze(2).broadcast_to([P, 4, HD]), ALU.mult).then_inc(s["out"], 1)

    def vector(self, dve, after_row=None):
        for i in range(self.N + LAG + 1):
            early, late = (self.early(i), self.late(i)) if i < self.N else ((), ())
            for u in early:
                self.release(dve, u)
                if u == ("row", 0) and after_row:
                    after_row()
            if i > LAG and (i - 1 - LAG) % self.NG in self.last_of_half:
                self.normalise(dve, i - 1 - LAG)
            if 1 <= i <= self.N and not self.even(i - 1):
                self.low_part(dve, self.nc.vector, i - 1, self.s["pl_dve"])
            for u in late:
                self.release(dve, u)
            if i == self.N + LAG - 2:
                self.release(dve, self.tail[0])
        self.release(dve, self.tail[1])

    def gpsimd(self, pool, beside):
        nc = self.nc
        for i in range(self.N):
            if beside:
                beside(pool, i)
            if self.even(i):
                self.low_part(pool, nc.gpsimd, i, self.s["pl_pool"])
            else:
                self.high_part(pool, i, lambda out, in_: nc.gpsimd.tensor_scalar(out, in_, 1.0, 0.0, ALU.mult, ALU.add), self.s["hi_pool"])
            if ("variance",) in self.uses_at[i]:
                pool.wait_ge(self.s["free"], self.index[("variance",)] + 1)
                self.norm_.root(pool)
            if i in self.norm_at:
                self.norm_.low(pool, self.norm_at[i])

    def row_in(self, sp, h):
        m = self.m
        sp.wait_ge(self.s["free"], self.index[("row", h)] + 1)
        sp.dma_start(m.qc[mrow(h):mrow(h) + 1, slot(h), :].rearrange("p (a b) -> p a b", a=NT), m.rowt[:, :]).then_inc(self.s["row"], 16)

    def outputs_ready(self, eng, c, hf):
        eng.wait_ge(self.s["free"], self.index[("ot", c, hf)] + 1)


class OutProjection:
    BANKS = (0, 1, 2, 3, 6, 7, 0, 1)

    def __init__(self, nc, ctx, m, layer, attn, x_in=None):
        self.nc, self.m, self.layer, self.attn, self.x_in = nc, m, layer, attn, x_in
        self.s = semaphores(nc, ctx, f"proj{layer}", "biased mm added stats mv eps rstd shift normed")

    def bias(self, pool, t):
        m = self.m
        self.nc.gpsimd.tensor_tensor(m.x[:, t, :], m.x[:, t, :], m.bo[self.layer][:, :].unsqueeze(1).broadcast_to([P, t.stop - t.start, C]),
                                     ALU.add).then_inc(self.s["biased"], t.stop - t.start)

    def bias_tiles(self, pool, i):
        if i == 3:
            pool.wait_ge(self.x_in, 16)
        if i % 4 == 3 and i // 4 < NT:
            self.bias(pool, slice(i // 4, i // 4 + 1))

    def products(self, pe, t, channels):
        nc, m, a = self.nc, self.m, self.attn
        steps = [(x, w, k) for k in channels for x, w in ((m.hT, m.wo_hi[self.layer]), (m.hT, m.wo_lo[self.layer]), (m.lT, m.wo_hi[self.layer]))]
        if channels[0] == 0:
            a.outputs_ready(pe, 1, t // 4)
            if t < 4:
                pe.wait_ge(a.s["exp"], a.N if t >= 2 else a.N - 1)
            elif t < 6:
                pe.wait_ge(a.s["out"], 2 * NH)
            else:
                pe.wait_ge(self.s["added"], t - 5)
        if channels[-1] == NC_ - 1:
            a.outputs_ready(pe, NC_ - 1, t // 4)
        for n, (x, w, k) in enumerate(steps):
            mm = nc.tensor.matmul(m.ps[:, self.BANKS[t], 0:C], x[:, k, t * P:(t + 1) * P], w[:, k, :],
                                  start=(channels[0] == 0 and n == 0), stop=(channels[-1] == NC_ - 1 and n == len(steps) - 1))
        if channels[-1] == NC_ - 1:
            mm.then_inc(self.s["mm"], 1)

    def between(self, pe):
        def work(step):
            for t in BETWEEN.get(step, ()):
                self.products(pe, t, range(NC_ - 1))
        return work

    def rest(self, pe):
        for t in range(NT):
            self.products(pe, t, [NC_ - 1] if t < 4 else range(NC_))

    def add(self, dve, t):
        nc, m, s = self.nc, self.m, self.s
        if t == 0:
            dve.wait_ge(s["biased"], NT)
        dve.wait_ge(s["mm"], t + 1)
        nc.vector.tensor_tensor(m.x[:, t, :], m.ps[:, self.BANKS[t], 0:C], m.x[:, t, :], ALU.add).then_inc(s["added"], 1)

    def statistics(self, dve, t):
        dve.wait_ge(self.s["added"], t + 1)
        self.nc.vector.bn_stats(self.m.stats[:, t, :], self.m.x[:, t, :]).then_inc(self.s["stats"], 1)

    def aggregate(self, dve, t):
        dve.wait_ge(self.s["stats"], t + 1)
        self.nc.vector.bn_aggr(self.m.mv[:, t, :], self.m.stats[:, t, :]).then_inc(self.s["mv"], 1)

    def eps(self, dve, hf):
        dve.wait_ge(self.s["mv"], 4 * (hf + 1))
        t = slice(4 * hf, 4 * hf + 4)
        self.nc.vector.tensor_scalar(self.m.ln[:, 0, t], self.m.mv[:, t, 1], 1e-5, None, ALU.add).then_inc(self.s["eps"], 1)

    def root(self, pool, hf):
        t = slice(4 * hf, 4 * hf + 4)
        pool.wait_ge(self.s["eps"], hf + 1)
        self.nc.gpsimd.tensor_tensor(self.m.ln[:, 1, t], self.m.ln[:, 0, t], self.m.minus_half[:, t], ALU.pow).then_inc(self.s["rstd"], 1)

    def shift(self, dve, hf):
        t = slice(4 * hf, 4 * hf + 4)
        dve.wait_ge(self.s["rstd"], hf + 1)
        self.nc.vector.scalar_tensor_tensor(self.m.ln[:, 2, t], self.m.mv[:, t, 0], -1.0, self.m.ln[:, 1, t], ALU.mult, ALU.mult).then_inc(self.s["shift"], 1)

    def norm(self, act, t, dst):
        act.wait_ge(self.s["shift"], t // 4 + 1)
        self.nc.scalar.activation(dst[:, t, :], self.m.x[:, t, :], ACT.Identity, scale=self.m.ln[:, 1, t:t + 1],
                                  bias=self.m.ln[:, 2, t:t + 1]).then_inc(self.s["normed"], 1)

    def vector(self, dve):
        for t in range(NT):
            self.add(dve, t)
            if t >= 1:
                self.aggregate(dve, t - 1)
            if t == 4:
                self.eps(dve, 0)
            self.statistics(dve, t)
            if t == 5:
                self.shift(dve, 0)
        self.aggregate(dve, NT - 1)
        self.eps(dve, 1)
        self.shift(dve, 1)

    def gpsimd(self, pool):
        for hf in range(2):
            self.root(pool, hf)


class LayerNorm:
    BANKS = ((4, 5, 2), (3, 6, 7))

    def __init__(self, nc, ctx, m, proj):
        self.nc, self.m, self.proj = nc, m, proj
        self.s = semaphores(nc, ctx, "ln", "transposed hi lo")

    def tensor(self, pe, hf):
        m = self.m
        for c in range(NC_):
            if hf == 0 and c == 2:
                pe.wait_ge(self.proj.s["added"], 3)
            for t in range(4 * hf, 4 * hf + 4):
                pe.wait_ge(self.proj.s["normed"], t + 1)
                mm = self.nc.tensor.transpose(m.ps[:, self.BANKS[hf][c], (t % 4) * P:(t % 4 + 1) * P], m.o[:, t, c * P:(c + 1) * P], m.ident[:, :])
            mm.then_inc(self.s["transposed"], 1)

    def high(self, act, hf, c):
        act.wait_ge(self.s["transposed"], 3 * hf + c + 1)
        self.nc.scalar.activation(self.m.hT[:, c, hf * BANK:(hf + 1) * BANK], self.m.ps[:, self.BANKS[hf][c], :], ACT.Copy).then_inc(self.s["hi"], 1)

    def scalar(self, act):
        for t in range(4):
            self.proj.norm(act, t, self.m.o)
        for c in range(NC_):
            self.high(act, 0, c)
        for t in range(4, NT):
            self.proj.norm(act, t, self.m.o)
        for c in range(NC_):
            self.high(act, 1, c)

    def low(self, dve, hf, c):
        half = slice(hf * BANK, (hf + 1) * BANK)
        dve.wait_ge(self.s["hi"], 3 * hf + c + 1)
        self.nc.vector.tensor_tensor(self.m.lT[:, c, half], self.m.ps[:, self.BANKS[hf][c], :], self.m.hT[:, c, half], ALU.subtract).then_inc(self.s["lo"], 1)

    def vector(self, dve):
        for hf in range(2):
            for c in range(NC_):
                self.low(dve, hf, c)

    def ready(self, pe, j, k):
        pe.wait_ge(self.s["lo"], 3 * j + k + 1)


class FeedForward:
    NHID = RING
    PAIRS = NF // 2
    BANKS = (6, 6, 6, 6, 0, 1, 0, 1)

    def __init__(self, nc, ctx, m, proj):
        self.nc, self.m, self.proj = nc, m, proj
        self.s = semaphores(nc, ctx, "ff", "scaled summed offset x2 x2_t x2_hi x2_lo up act down each o2 spread added")
        self.scaled = m.o
        self.x2 = m.ph[:, 0, 0, :].bitcast(F32).rearrange("p (t a) -> p t a", t=NT)
        self.stack = flat(m.ph[0:3 * FA, 1, :, :])
        self.o2 = flat(m.pl[:, 0:2, :, :].rearrange("p r a b -> p r (a b)")).bitcast(F32)

    def scale(self, pool, t):
        pool.wait_ge(self.proj.s["added"], t + 1)
        self.nc.gpsimd.tensor_tensor(self.scaled[:, t, :].rearrange("p (a b) -> p a b", b=FB), self.m.x[:, t, :].rearrange("p (a b) -> p a b", b=FB),
                                     self.m.cf2[:, :].unsqueeze(1).broadcast_to([P, FA, FB]), ALU.mult).then_inc(self.s["scaled"], 1)

    def sum(self, dve, t):
        dve.wait_ge(self.s["scaled"], t + 1)
        self.nc.vector.reduce_sum(self.x2[:, t, :], self.scaled[:, t, :].rearrange("p (a b) -> p a b", b=FB), AX.X).then_inc(self.s["summed"], 1)

    def norm(self, dve, hf):
        nc, m, s = self.nc, self.m, self.s
        half = slice(4 * hf, 4 * hf + 4)
        self.proj.shift(dve, hf)
        dve.wait_ge(self.proj.s["shift"], hf + 1)
        nc.vector.tensor_scalar(m.ln[:, 2, half], m.ln[:, 2, half], m.f2sum[:, 0:1], None, ALU.mult).then_inc(s["offset"], 1)
        dve.wait_ge(s["summed"], 4 * (hf + 1))
        dve.wait_ge(s["offset"], hf + 1)
        for t in range(4 * hf, 4 * hf + 4):
            nc.vector.tensor_scalar(self.x2[:, t, :], self.x2[:, t, :], m.ln[:, 1, t:t + 1], m.ln[:, 2, t:t + 1], ALU.mult, ALU.add).then_inc(s["x2"], 1)

    def input(self, dve):
        for t in range(NT):
            self.proj.add(dve, t)
            if t >= 1:
                self.proj.aggregate(dve, t - 1)
            if t == 4:
                self.proj.eps(dve, 0)
            self.proj.statistics(dve, t)
            if t >= 2:
                self.sum(dve, t - 2)
        self.proj.aggregate(dve, NT - 1)
        self.proj.eps(dve, 1)
        self.norm(dve, 0)
        self.sum(dve, NT - 2)
        self.sum(dve, NT - 1)
        self.norm(dve, 1)

    def x2_transposes(self, pe, hf):
        for t in range(4 * hf, 4 * hf + 4):
            pe.wait_ge(self.s["x2"], t + 1)
            mm = self.nc.tensor.transpose(self.m.ps[0:FA, hf, (t % 4) * P:(t % 4 + 1) * P], self.x2[:, t, :], self.m.ident[:, :])
        mm.then_inc(self.s["x2_t"], 1)

    def x2_high(self, act, hf):
        half = slice(hf * BANK, (hf + 1) * BANK)
        act.wait_ge(self.s["x2_t"], hf + 1)
        for r in (0, 2):
            self.nc.scalar.activation(self.stack[r * FA:(r + 1) * FA, half], self.m.ps[0:FA, hf, :], ACT.Copy).then_inc(self.s["x2_hi"], 1)

    def x2_low(self, dve, hf):
        half = slice(hf * BANK, (hf + 1) * BANK)
        dve.wait_ge(self.s["x2_hi"], 2 * (hf + 1))
        self.nc.vector.tensor_tensor(self.stack[FA:2 * FA, half], self.m.ps[0:FA, hf, :], self.stack[0:FA, half], ALU.subtract).then_inc(self.s["x2_lo"], 1)

    def up(self, pe, i):
        m, s = self.m, self.s
        hf, f = i // self.PAIRS, 2 * (i % self.PAIRS)
        if i == 0:
            pe.wait_ge(s["x2_lo"], 2)
        else:
            pe.wait_ge(s["act"], i)
        for j in range(2):
            mm = self.nc.tensor.matmul(m.ps[:, j, :], m.c1[:, (f + j) * P:(f + j + 1) * P], self.stack[:, hf * BANK:(hf + 1) * BANK],
                                       start=True, stop=True)
        mm.then_inc(s["up"], 1)

    def gelu(self, act, i):
        act.wait_ge(self.s["up"], i + 1)
        if i >= self.NHID:
            act.wait_ge(self.s["each"], i - self.NHID + 1)
        self.nc.scalar.activation(self.m.p32[:, i % self.NHID, :, :], self.m.ps[:, 0:2, :], ACT.Gelu).then_inc(self.s["act"], 1)

    def down(self, pe, i):
        m, s = self.m, self.s
        hf, f = i // self.PAIRS, 2 * (i % self.PAIRS)
        pe.wait_ge(s["act"], i + 1)
        for j in range(2):
            q = (f + j) % 4
            mm = self.nc.tensor.matmul(m.ps[q * FA:(q + 1) * FA, 6 + hf, :], m.cp[:, f + j, :], m.p32[:, i % self.NHID, j, :],
                                       start=(f + j < 4), stop=(f + j >= NF - 4), skip_group_check=True)
        mm.then_inc(s["each"], 1)

    def o2_out(self, dve, hf):
        dve.wait_ge(self.s["each"], self.PAIRS * (hf + 1))
        self.nc.vector.tensor_copy(self.o2[:, hf * BANK:(hf + 1) * BANK], self.m.ps[:, 6 + hf, :]).then_inc(self.s["o2"], 1)

    def spread(self, pe, t):
        if t % 4 == 0:
            pe.wait_ge(self.s["o2"], t // 4 + 1)
        if t in (1, 2, 3):
            pe.wait_ge(self.s["added"], t)
        elif t in (4, 5):
            pe.wait_ge(self.s["act"], 2 * self.PAIRS)
        elif t >= 6:
            pe.wait_ge(self.s["added"], t - 1)
        self.nc.tensor.matmul(self.m.ps[:, self.BANKS[t], 0:C], self.o2[:, t * P:(t + 1) * P], self.m.spread[:, :], start=True, stop=True).then_inc(self.s["spread"], 1)

    def add(self, dve, t):
        dve.wait_ge(self.s["spread"], t + 1)
        self.nc.vector.tensor_tensor(self.m.x[:, t, :], self.m.ps[:, self.BANKS[t], 0:C], self.m.x[:, t, :], ALU.add).then_inc(self.s["added"], 1)

    def store(self, sp, out_ap, stored):
        for hf in range(2):
            t = slice(4 * hf, 4 * hf + 4)
            sp.wait_ge(self.s["added"], 4 * (hf + 1))
            sp.dma_start(out_ap[:, t, :], self.m.x[:, t, :]).then_inc(stored, 16)


class Dram:
    pass


def build(nc, x, qkv_w, qkv_b, proj_w, proj_b, rel_h, rel_w, wq, wk, wv, wo, bo, c_fc_1, c_fc_2, c_proj_1, c_proj_2, out):
    d = Dram()
    d.qkv_w, d.qkv_b, d.proj_w, d.proj_b, d.rel_h, d.rel_w = qkv_w, qkv_b, proj_w, proj_b, rel_h, rel_w
    d.wq, d.wk, d.wv, d.wo, d.bo = wq, wk, wv, wo, bo
    d.c_fc_1, d.c_fc_2, d.c_proj_1, d.c_proj_2 = c_fc_1, c_fc_2, c_proj_1, c_proj_2
    images = x.shape[0]
    d.x_tiles = x.rearrange("b h w c -> b (h w) c").rearrange("b (t p) c -> b p t c", p=P)
    out_tiles = out.rearrange("b h w c -> b (h w) c").rearrange("b (t p) c -> b p t c", p=P)
    with ExitStack() as ctx:
        m = Mem()
        allocate(nc, ctx, m)
        stored = ctx.enter_context(nc.semaphore("stored"))
        constants(nc, ctx, m, d, stored)
        first_image(nc, ctx, m, Norm(nc, ctx, m, "gn_first"), Projections(nc, ctx, m, 0, "qkv_first"))
        first = ctx.enter_context(nc.semaphore("loop_first"))
        x_in = ctx.enter_context(nc.semaphore("x_in"))
        next_in = ctx.enter_context(nc.semaphore("next_in"))
        norm = Norm(nc, ctx, m, "gn")
        qkv0 = Projections(nc, ctx, m, 0, "qkv0")
        attn0 = Attention(nc, ctx, m, 0, qkv0, norm, next_in)
        proj0 = OutProjection(nc, ctx, m, 0, attn0, x_in)
        ln = LayerNorm(nc, ctx, m, proj0)
        qkv1 = Projections(nc, ctx, m, 1, "qkv1")
        attn1 = Attention(nc, ctx, m, 1, qkv1)
        proj1 = OutProjection(nc, ctx, m, 1, attn1)
        ff = FeedForward(nc, ctx, m, proj1)
        last = ctx.enter_context(nc.semaphore("loop_last"))
        WITH_V = ((0,), (1,), (2, 3), (4, 5), (6, 7), (), (), ())
        REL_ORDER = list(range(24)) + [24, 25, 28, 29, 26, 27, 30, 31]
        RELS = IMG
        PAIRS = 2 * NPAIR
        EACH = 6 * NC_
        FILL = (0, 6, 6, 6, 6, 6, 6, 6, 6, 6, 0, 0)
        HIGHS = (0, 1, 4, 5, 7, 8, 10, 11)
        SPREADS = (7, 8, 9, 10)
        with nc.Fori(0, images) as b:
            with nc.Block() as block:
                @block.tensor
                def _(pe):
                    for t in range(NT - 1):
                        qkv0.v_products(pe, t)
                        for n in WITH_V[t]:
                            qkv0.rel_products(pe, n)
                        if t == 5:
                            pe.wait_ge(qkv0.s["rel_lo"], RELS - 4)
                        for u in attn0.prologue_part(t):
                            attn0.use(pe, u)
                    def beside_row():
                        qkv0.v_products(pe, NT - 1)
                        pe.wait_ge(qkv0.s["rel_lo"], RELS)
                    attn0.tensor(pe, proj0.between(pe), beside_row)
                    proj0.rest(pe)
                    ln.tensor(pe, 0)
                    qkv1.pair_products(pe, 0, ln.ready, (0, EACH // 2))
                    ln.tensor(pe, 1)
                    qkv1.pair_products(pe, 1, ln.ready, (0, EACH // 2))
                    for i in range(2):
                        qkv1.pair_products(pe, i, ln.ready, (EACH // 2, EACH))
                    for i in range(2, PAIRS):
                        qkv1.pair_products(pe, i)
                    for t in range(NT):
                        qkv1.v_products(pe, t)
                        if t == 3:
                            pe.wait_ge(qkv1.s["lo"], 2 * PAIRS)
                        for u in attn1.prologue_part(t):
                            attn1.use(pe, u)
                    attn1.tensor(pe, proj1.between(pe))
                    proj1.rest(pe)
                    pe.wait_ge(norm.s["lo"], 2 * NC_)
                    pe.wait_ge(proj1.s["added"], 6)
                    qkv0.pair_products(pe, 0)
                    qkv0.pair_products(pe, 1)
                    pe.wait_ge(proj1.s["added"], NT)
                    ff.x2_transposes(pe, 0)
                    ff.x2_transposes(pe, 1)
                    qkv0.pair_products(pe, 2)
                    for i in range(2 * ff.PAIRS + 1):
                        if i < 2 * ff.PAIRS:
                            ff.up(pe, i)
                        if i == 1:
                            pe.wait_ge(qkv0.s["lo"], 2)
                        if i >= 1:
                            ff.down(pe, i - 1)
                        if i < 2 * ff.PAIRS and FILL[i]:
                            qkv0.fill(pe, 3 * EACH + sum(FILL[:i]), 3 * EACH + sum(FILL[:i + 1]))
                        if i in SPREADS:
                            ff.spread(pe, SPREADS.index(i))
                    for t in range(4, NT):
                        ff.spread(pe, t)

                @block.scalar
                def _(act):
                    for t in range(NT):
                        qkv0.v_high(act, t)
                        for n in WITH_V[t]:
                            for r in range(4 * n, 4 * n + 4):
                                qkv0.rel_high(act, r)
                    attn0.scalar(act)
                    ln.scalar(act)
                    for i in range(PAIRS):
                        qkv1.pair_high(act, i)
                    for t in range(NT):
                        qkv1.v_high(act, t)
                    attn1.scalar(act)
                    qkv0.pair_high(act, 0)
                    ff.x2_high(act, 0)
                    ff.x2_high(act, 1)
                    qkv0.pair_high(act, 1)
                    for i in range(2 * ff.PAIRS):
                        ff.gelu(act, i)
                        if i in HIGHS:
                            n = HIGHS.index(i)
                            qkv0.pair_high(act, 2 + n // 2, (n % 2,))

                @block.vector
                def _(dve):
                    for r in REL_ORDER[:-4]:
                        qkv0.rel_low(dve, r)
                    for u in attn0.prologue:
                        attn0.release(dve, u)

                    def after_row():
                        for r in REL_ORDER[-4:]:
                            qkv0.rel_low(dve, r)
                    attn0.vector(dve, after_row)
                    proj0.vector(dve)
                    ln.vector(dve)
                    for i in range(PAIRS):
                        qkv1.pair_low(dve, i)
                    for u in attn1.prologue:
                        attn1.release(dve, u)
                    attn1.vector(dve)
                    ff.input(dve)
                    qkv0.pair_low(dve, 0)
                    ff.x2_low(dve, 0)
                    ff.x2_low(dve, 1)
                    qkv0.pair_low(dve, 1)
                    for i in range(2, 4):
                        qkv0.pair_low(dve, i)
                    ff.o2_out(dve, 0)
                    for t in range(4):
                        ff.add(dve, t)
                        if t in (1, 2):
                            qkv0.pair_low(dve, 4, (t - 1,))
                    qkv0.pair_low(dve, 5, (0,))
                    ff.o2_out(dve, 1)
                    ff.add(dve, 4)
                    ff.add(dve, 5)
                    qkv0.pair_low(dve, 5, (1,))
                    ff.add(dve, 6)
                    ff.add(dve, 7)

                @block.gpsimd
                def _(pool):
                    for t in range(NT):
                        qkv0.v_low(pool, t)
                    attn0.gpsimd(pool, proj0.bias_tiles)
                    proj0.gpsimd(pool)
                    pool.wait_ge(proj0.s["normed"], NT)
                    proj1.bias(pool, slice(0, NT))
                    for t in range(NT):
                        qkv1.v_low(pool, t)
                    attn1.gpsimd(pool, None)
                    for t in range(NT):
                        ff.scale(pool, t)
                        if t == 4:
                            proj1.root(pool, 0)
                    proj1.root(pool, 1)

                @block.sync
                def _(sp):
                    sp.wait_ge(stored, (b + 1) * STORES)
                    sp.dma_start(m.x[:, :, :], d.x_tiles[b]).then_inc(x_in, 16)
                    attn0.row_in(sp, 0)
                    sp.wait_ge(qkv0.s["v_mm"], NT)
                    sp.dma_start(m.xin[:, :, :], d.x_tiles[(b + 1) % images]).then_inc(next_in, 16)
                    for h in range(1, NH):
                        attn0.row_in(sp, h)
                    for h in range(NH):
                        attn1.row_in(sp, h)
                    ff.store(sp, out_tiles[b], stored)
            nc.gpsimd.sem_clear(range(first.num, last.num + 1))
            nc.all_engine_barrier()
        with nc.Block() as block:
            @block.sync
            def _(sp):
                sp.wait_ge(stored, (images + 1) * STORES)


_INS = ['x', 'L0_conv_qkv_w', 'L0_conv_qkv_b', 'L0_conv_proj_w', 'L0_conv_proj_b', 'L0_conv_rel_pos_h', 'L0_conv_rel_pos_w',
        'L1_attn_Wq', 'L1_attn_Wk', 'L1_attn_Wv', 'L1_attn_Wo', 'L1_attn_bo', 'L1_ffn_c_fc_1', 'L1_ffn_c_fc_2', 'L1_ffn_c_proj_1',
        'L1_ffn_c_proj_2']


def kernel(**inputs):
    import numpy as _np
    import concourse.bacc as _bacc
    from concourse import mybir as _mybir
    from concourse.bass_utils import run_bass_kernel_spmd as _run

    nc = _bacc.Bacc("TRN2", target_bir_lowering=False, num_devices=1)
    arrays, args = {}, []
    for name in _INS:
        a = _np.ascontiguousarray(inputs[name])
        arrays[f"in_{name}"] = a
        args.append(nc.dram_tensor(f"in_{name}", a.shape, _mybir.dt.from_np(a.dtype), kind="ExternalInput").ap())
    args.append(nc.dram_tensor("out", inputs["x"].shape, _mybir.dt.float32, kind="ExternalOutput").ap())
    build(nc, *args)
    return _run(nc, [arrays], core_ids=[0]).results[0]["out"]
```
